# Optimizing a Trainium2 kernel written in Bass

```python
import numpy as np
import jax
import jax.numpy as jnp

def _softmax(x, axis=-1):
    return jax.nn.softmax(x, axis=axis)

def _gelu(x):
    return jax.nn.gelu(x, approximate=True)

def _silu(x):
    return jax.nn.silu(x)

def _sigmoid(x):
    return jax.nn.sigmoid(x)

def _layernorm(x, axis=-1, eps=1e-05):
    m = jnp.mean(x, axis=axis, keepdims=True)
    v = jnp.var(x, axis=axis, keepdims=True)
    return (x - m) / jnp.sqrt(v + eps)

def _scatter_add(tgt, idx, src, axis=0):
    return tgt.at[idx].add(src)

def _segment_sum(src, seg, n):
    return jax.ops.segment_sum(src, seg, n)
kernel_name = 'mk_hybrid_d2_jaxref_r8_9fb59e'

def setup_inputs(seed: int=0):
    np.random.seed(seed)
    _w = jnp.asarray

    def _L0_attn_a_setup():
        import jax, jax.numpy as jnp
        import numpy as np
        EMBED_DIM = 128
        B, T = (4, 256)
        key = jax.random.key(seed)
        ks = jax.random.split(key, 7)
        s = 1.0 / np.sqrt(EMBED_DIM)
        return {'x': jax.random.normal(ks[0], (B, T, EMBED_DIM), dtype=jnp.float32), 'Wq': jax.random.uniform(ks[1], (EMBED_DIM, EMBED_DIM), jnp.float32, -s, s), 'bq': jax.random.uniform(ks[2], (EMBED_DIM,), jnp.float32, -s, s), 'Wk': jax.random.uniform(ks[3], (EMBED_DIM, EMBED_DIM), jnp.float32, -s, s), 'bk': jax.random.uniform(ks[4], (EMBED_DIM,), jnp.float32, -s, s), 'Wv': jax.random.uniform(ks[5], (EMBED_DIM, EMBED_DIM), jnp.float32, -s, s), 'bv': jax.random.uniform(ks[6], (EMBED_DIM,), jnp.float32, -s, s)}
    _L0_attn_a_in = _L0_attn_a_setup()

    def _L0_attn_b_setup():
        import jax, jax.numpy as jnp
        import numpy as np
        EMBED_DIM = 128
        NUM_HEADS = 16
        D_K = EMBED_DIM // NUM_HEADS
        MAX_LEN = 128
        BATCH = 4
        SEQ = 128
        key = jax.random.key(seed)
        ks = jax.random.split(key, 6)
        s = 1.0 / np.sqrt(EMBED_DIM)
        return {'x': jax.random.normal(ks[0], (BATCH, SEQ, EMBED_DIM), jnp.float32), 'Wq': jax.random.normal(ks[1], (EMBED_DIM, EMBED_DIM), jnp.float32) * s, 'bq': jnp.zeros((EMBED_DIM,), jnp.float32), 'Wk': jax.random.normal(ks[2], (EMBED_DIM, EMBED_DIM), jnp.float32) * s, 'bk': jnp.zeros((EMBED_DIM,), jnp.float32), 'Wv': jax.random.normal(ks[3], (EMBED_DIM, EMBED_DIM), jnp.float32) * s, 'bv': jnp.zeros((EMBED_DIM,), jnp.float32), 'Wo': jax.random.normal(ks[4], (EMBED_DIM, EMBED_DIM), jnp.float32) * s, 'bo': jnp.zeros((EMBED_DIM,), jnp.float32), 'rel_table': jax.random.normal(ks[5], (2 * MAX_LEN - 1, D_K), jnp.float32)}
    _L0_attn_b_in = _L0_attn_b_setup()

    def _L0_ffn_setup():
        import jax, jax.numpy as jnp
        import numpy as np

        def _bitlinear(x, w_latent):
            scale = jax.lax.stop_gradient(jnp.clip(jnp.mean(jnp.abs(w_latent), axis=1, keepdims=True), 1e-05, None))
            tern = jnp.clip(jnp.round(w_latent / scale), -1.0, 1.0)
            w = w_latent + jax.lax.stop_gradient(tern - w_latent)
            return x @ (w * scale).T
        key = jax.random.key(seed)
        ks = jax.random.split(key, 6)
        dim, hidden, rank = (128, 512, 16)
        B, S = (4, 512)
        x = jax.random.normal(ks[0], (B, S, dim), dtype=jnp.float32)
        w_fc = 0.02 * jax.random.normal(ks[1], (hidden, dim), dtype=jnp.float32)
        w_proj = 0.02 * jax.random.normal(ks[2], (dim, hidden), dtype=jnp.float32)
        u = 0.02 * jax.random.normal(ks[3], (hidden, rank), dtype=jnp.float32)
        v = 0.02 * jax.random.normal(ks[4], (rank, dim), dtype=jnp.float32)
        fast_b = jax.random.normal(ks[5], (rank, rank), dtype=jnp.float32)
        gate = jnp.float32(0.05)
        return {'x': x, 'fast_b': fast_b, 'w_fc': w_fc, 'w_proj': w_proj, 'u': u, 'v': v, 'gate': gate}
    _L0_ffn_in = _L0_ffn_setup()

    def _L1_attn_a_setup():
        import jax, jax.numpy as jnp
        import numpy as np
        EMBED = 128
        HEADS = 16
        key = jax.random.key(seed)
        ks = jax.random.split(key, 6)
        N, S = (1, 512)
        half = EMBED // 2
        x = jax.random.normal(ks[0], (N, S, EMBED), dtype=jnp.float32)
        Wq = jax.random.normal(ks[1], (half, half), dtype=jnp.float32) * 0.02
        Wk = jax.random.normal(ks[2], (half, half), dtype=jnp.float32) * 0.02
        Wv = jax.random.normal(ks[3], (half, half), dtype=jnp.float32) * 0.02
        Wo = jax.random.normal(ks[4], (EMBED, half), dtype=jnp.float32) * 0.02
        bo = jnp.zeros((EMBED,), dtype=jnp.float32)
        return {'x': x, 'Wq': Wq, 'Wk': Wk, 'Wv': Wv, 'Wo': Wo, 'bo': bo}
    _L1_attn_a_in = _L1_attn_a_setup()

    def _L1_attn_b_setup():
        import jax, jax.numpy as jnp
        import numpy as np
        B, S, E, H, W = (4, 256, 128, 16, 128)
        HD = E // H
        key = jax.random.key(seed)
        ks = jax.random.split(key, 5)
        scale = 1.0 / np.sqrt(E)
        x = jax.random.normal(ks[0], (B, S, E), dtype=jnp.float32)
        w_in = jax.random.uniform(ks[1], (3 * E, E), dtype=jnp.float32, minval=-scale, maxval=scale)
        b_in = jnp.zeros((3 * E,), dtype=jnp.float32)
        w_out = jax.random.uniform(ks[2], (E, E), dtype=jnp.float32, minval=-scale, maxval=scale)
        b_out = jnp.zeros((E,), dtype=jnp.float32)
        return {'x': x, 'w_in': w_in, 'b_in': b_in, 'w_out': w_out, 'b_out': b_out}
    _L1_attn_b_in = _L1_attn_b_setup()

    def _L1_ffn_setup():
        import jax, jax.numpy as jnp
        import numpy as np
        B, T, D, H, R, N = (16, 128, 128, 32, 64, 8)
        key = jax.random.key(seed)
        ks = jax.random.split(key, 8)
        s = lambda k, shape, fan: jax.random.normal(k, shape, jnp.float32) / np.sqrt(fan)
        return {'x': jax.random.normal(ks[0], (B, T, D), jnp.float32), 'W_base': s(ks[1], (D, D), D), 'b_base': jnp.zeros((D,), jnp.float32), 'W_enc': s(ks[2], (N, D, H), D), 'b_enc': jnp.zeros((N, H), jnp.float32), 'W_dec': s(ks[3], (N, H, D), H), 'b_dec': jnp.zeros((N, D), jnp.float32), 'W_down': s(ks[4], (N, D, R), D), 'b_down': jnp.zeros((N, R), jnp.float32), 'W_up': s(ks[5], (N, R, D), R), 'b_up': jnp.zeros((N, D), jnp.float32), 'connected_idx': jnp.arange(N, dtype=jnp.int32)}
    _L1_ffn_in = _L1_ffn_setup()
    _d = {'L0_attn_a_x': _L0_attn_a_in['x'], 'L0_attn_a_Wq': _L0_attn_a_in['Wq'], 'L0_attn_a_bq': _L0_attn_a_in['bq'], 'L0_attn_a_Wk': _L0_attn_a_in['Wk'], 'L0_attn_a_bk': _L0_attn_a_in['bk'], 'L0_attn_a_Wv': _L0_attn_a_in['Wv'], 'L0_attn_a_bv': _L0_attn_a_in['bv'], 'L0_attn_b_Wq': _L0_attn_b_in['Wq'], 'L0_attn_b_bq': _L0_attn_b_in['bq'], 'L0_attn_b_Wk': _L0_attn_b_in['Wk'], 'L0_attn_b_bk': _L0_attn_b_in['bk'], 'L0_attn_b_Wv': _L0_attn_b_in['Wv'], 'L0_attn_b_bv': _L0_attn_b_in['bv'], 'L0_attn_b_Wo': _L0_attn_b_in['Wo'], 'L0_attn_b_bo': _L0_attn_b_in['bo'], 'L0_attn_b_rel_table': _L0_attn_b_in['rel_table'], 'L0_ffn_fast_b': _L0_ffn_in['fast_b'], 'L0_ffn_w_fc': _L0_ffn_in['w_fc'], 'L0_ffn_w_proj': _L0_ffn_in['w_proj'], 'L0_ffn_u': _L0_ffn_in['u'], 'L0_ffn_v': _L0_ffn_in['v'], 'L0_ffn_gate': _L0_ffn_in['gate'], 'L1_attn_a_Wq': _L1_attn_a_in['Wq'], 'L1_attn_a_Wk': _L1_attn_a_in['Wk'], 'L1_attn_a_Wv': _L1_attn_a_in['Wv'], 'L1_attn_a_Wo': _L1_attn_a_in['Wo'], 'L1_attn_a_bo': _L1_attn_a_in['bo'], 'L1_attn_b_w_in': _L1_attn_b_in['w_in'], 'L1_attn_b_b_in': _L1_attn_b_in['b_in'], 'L1_attn_b_w_out': _L1_attn_b_in['w_out'], 'L1_attn_b_b_out': _L1_attn_b_in['b_out'], 'L1_ffn_W_base': _L1_ffn_in['W_base'], 'L1_ffn_b_base': _L1_ffn_in['b_base'], 'L1_ffn_W_enc': _L1_ffn_in['W_enc'], 'L1_ffn_b_enc': _L1_ffn_in['b_enc'], 'L1_ffn_W_dec': _L1_ffn_in['W_dec'], 'L1_ffn_b_dec': _L1_ffn_in['b_dec'], 'L1_ffn_W_down': _L1_ffn_in['W_down'], 'L1_ffn_b_down': _L1_ffn_in['b_down'], 'L1_ffn_W_up': _L1_ffn_in['W_up'], 'L1_ffn_b_up': _L1_ffn_in['b_up'], 'L1_ffn_connected_idx': _L1_ffn_in['connected_idx']}
    _x0 = _d['L0_attn_a_x']
    _d['L0_attn_a_x'] = jax.random.normal(jax.random.fold_in(jax.random.key(seed), 1), (8, 512, 128), dtype=_x0.dtype)
    del _x0
    return _d

def reference(L0_attn_a_x, L0_attn_a_Wq, L0_attn_a_bq, L0_attn_a_Wk, L0_attn_a_bk, L0_attn_a_Wv, L0_attn_a_bv, L0_attn_b_Wq, L0_attn_b_bq, L0_attn_b_Wk, L0_attn_b_bk, L0_attn_b_Wv, L0_attn_b_bv, L0_attn_b_Wo, L0_attn_b_bo, L0_attn_b_rel_table, L0_ffn_fast_b, L0_ffn_w_fc, L0_ffn_w_proj, L0_ffn_u, L0_ffn_v, L0_ffn_gate, L1_attn_a_Wq, L1_attn_a_Wk, L1_attn_a_Wv, L1_attn_a_Wo, L1_attn_a_bo, L1_attn_b_w_in, L1_attn_b_b_in, L1_attn_b_w_out, L1_attn_b_b_out, L1_ffn_W_base, L1_ffn_b_base, L1_ffn_W_enc, L1_ffn_b_enc, L1_ffn_W_dec, L1_ffn_b_dec, L1_ffn_W_down, L1_ffn_b_down, L1_ffn_W_up, L1_ffn_b_up, L1_ffn_connected_idx):

    def _L0_attn_a_ref(x, Wq, bq, Wk, bk, Wv, bv):
        import jax, jax.numpy as jnp
        import numpy as np
        EMBED_DIM = 128
        B, T = (4, 256)
        Bsz, Tlen, C = x.shape
        Q = jnp.einsum('btc,dc->btd', x, Wq) + bq
        K = jnp.einsum('btc,dc->btd', x, Wk) + bk
        V = jnp.einsum('btc,dc->btd', x, Wv) + bv
        score = jnp.einsum('bqd,bkd->bqk', Q, K) / jnp.sqrt(jnp.float32(C))
        causal = jnp.tril(jnp.ones((Tlen, Tlen), dtype=bool))
        score = jnp.where(causal, score, -jnp.inf)
        att = jax.nn.softmax(score, axis=-1)
        return jnp.einsum('bqk,bkd->bqd', att, V)

    def _L0_attn_b_ref(x, Wq, bq, Wk, bk, Wv, bv, Wo, bo, rel_table):
        import jax, jax.numpy as jnp
        import numpy as np
        EMBED_DIM = 128
        NUM_HEADS = 16
        D_K = EMBED_DIM // NUM_HEADS
        MAX_LEN = 128
        BATCH = 4
        SEQ = 128
        b, n, e = x.shape
        h, d = (NUM_HEADS, D_K)

        def proj(W, bias):
            y = jnp.einsum('bne,fe->bnf', x, W) + bias
            return y.reshape(b, n, h, d).transpose(0, 2, 1, 3)
        Q = proj(Wq, bq)
        K = proj(Wk, bk)
        V = proj(Wv, bv)
        scores_content = jnp.einsum('bhid,bhjd->bhij', Q, K)
        pos = jnp.arange(n)
        rel_pos = jnp.clip(pos[:, None] - pos[None, :] + MAX_LEN - 1, 0, 2 * MAX_LEN - 2)
        rel_emb = rel_table[rel_pos]
        scores_pos = jnp.einsum('bhid,ijd->bhij', Q, rel_emb)
        scores = (scores_content + scores_pos) / np.sqrt(d).astype(np.float32)
        attn = jax.nn.softmax(scores, axis=-1)
        out = jnp.einsum('bhij,bhjd->bhid', attn, V)
        out = out.transpose(0, 2, 1, 3).reshape(b, n, e)
        return jnp.einsum('bne,fe->bnf', out, Wo) + bo

    def _L0_ffn_ref(x, fast_b, w_fc, w_proj, u, v, gate):
        import jax, jax.numpy as jnp
        import numpy as np

        def _bitlinear(x, w_latent):
            scale = jax.lax.stop_gradient(jnp.clip(jnp.mean(jnp.abs(w_latent), axis=1, keepdims=True), 1e-05, None))
            tern = jnp.clip(jnp.round(w_latent / scale), -1.0, 1.0)
            w = w_latent + jax.lax.stop_gradient(tern - w_latent)
            return x @ (w * scale).T
        h = _bitlinear(x, w_fc) + gate * (x @ v.T @ fast_b.T @ u.T)
        r = jnp.maximum(h, 0.0)
        return _bitlinear(r * r, w_proj)

    def _L1_attn_a_ref(x, Wq, Wk, Wv, Wo, bo):
        import jax, jax.numpy as jnp
        import numpy as np
        EMBED = 128
        HEADS = 16
        N, S, E = x.shape
        H = HEADS
        Dh = E // 2 // H
        scale = float(E // H) ** 0.5
        left = x[..., :E // 2]
        q = (left @ Wq.T).reshape(N, S, H, Dh)
        k = (left @ Wk.T).reshape(N, S, H, Dh)
        v = (left @ Wv.T).reshape(N, S, H, Dh)
        energy = jnp.einsum('nqhd,nkhd->nqkh', q, k)
        att = jax.nn.softmax(energy / scale, axis=2)
        out = jnp.einsum('nqkh,nkhd->nqhd', att, v)
        out = out.reshape(N, S, E // 2)
        return out @ Wo.T + bo

    def _L1_attn_b_ref(x, w_in, b_in, w_out, b_out):
        import jax, jax.numpy as jnp
        import numpy as np
        B, S, E, H, W = (4, 256, 128, 16, 128)
        HD = E // H
        b, s, e = x.shape
        qkv = x @ w_in.T + b_in
        q, k, v = jnp.split(qkv, 3, axis=-1)
        q = q.reshape(b, s, H, HD).transpose(0, 2, 1, 3)
        k = k.reshape(b, s, H, HD).transpose(0, 2, 1, 3)
        v = v.reshape(b, s, H, HD).transpose(0, 2, 1, 3)
        scores = jnp.einsum('bhqd,bhkd->bhqk', q, k) / jnp.sqrt(jnp.asarray(HD, x.dtype))
        i = jnp.arange(s)[:, None]
        j = jnp.arange(s)[None, :]
        allowed = (j <= i) & (j >= i - W)
        scores = jnp.where(allowed[None, None], scores, jnp.asarray(-1000000000.0, x.dtype))
        attn = jax.nn.softmax(scores, axis=-1)
        out = jnp.einsum('bhqk,bhkd->bhqd', attn, v)
        out = out.transpose(0, 2, 1, 3).reshape(b, s, e)
        return out @ w_out.T + b_out

    def _L1_ffn_ref(x, W_base, b_base, W_enc, b_enc, W_dec, b_dec, W_down, b_down, W_up, b_up, connected_idx):
        import jax, jax.numpy as jnp
        import numpy as np
        B, T, D, H, R, N = (16, 128, 128, 32, 64, 8)
        base = jnp.einsum('btd,de->bte', x, W_base) + b_base
        h = jax.nn.relu(jnp.einsum('btd,ndh->nbth', x, W_enc) + b_enc[:, None, None, :])
        recon = jnp.einsum('nbth,nhd->nbtd', h, W_dec) + b_dec[:, None, None, :]
        losses = jnp.mean((recon - x[None]) ** 2, axis=(2, 3))
        top1 = jnp.argmin(losses, axis=0)
        adp = connected_idx[top1]
        Wd, bd = (W_down[adp], b_down[adp])
        Wu, bu = (W_up[adp], b_up[adp])
        mid = jax.nn.relu(jnp.einsum('btd,bdr->btr', x, Wd) + bd[:, None, :])
        adapter_out = jnp.einsum('btr,brd->btd', mid, Wu) + bu[:, None, :]
        return base + adapter_out
    x = L0_attn_a_x
    x = x + _L0_attn_a_ref(_layernorm(x, axis=-1), L0_attn_a_Wq, L0_attn_a_bq, L0_attn_a_Wk, L0_attn_a_bk, L0_attn_a_Wv, L0_attn_a_bv)
    x = x + _L0_ffn_ref(_layernorm(x, axis=-1), L0_ffn_fast_b, L0_ffn_w_fc, L0_ffn_w_proj, L0_ffn_u, L0_ffn_v, L0_ffn_gate)
    x = x + _L0_attn_b_ref(_layernorm(x, axis=-1), L0_attn_b_Wq, L0_attn_b_bq, L0_attn_b_Wk, L0_attn_b_bk, L0_attn_b_Wv, L0_attn_b_bv, L0_attn_b_Wo, L0_attn_b_bo, L0_attn_b_rel_table)
    x = x + _L0_ffn_ref(_layernorm(x, axis=-1), L0_ffn_fast_b, L0_ffn_w_fc, L0_ffn_w_proj, L0_ffn_u, L0_ffn_v, L0_ffn_gate)
    x = x + _L1_attn_a_ref(_layernorm(x, axis=-1), L1_attn_a_Wq, L1_attn_a_Wk, L1_attn_a_Wv, L1_attn_a_Wo, L1_attn_a_bo)
    x = x + _L1_ffn_ref(_layernorm(x, axis=-1), L1_ffn_W_base, L1_ffn_b_base, L1_ffn_W_enc, L1_ffn_b_enc, L1_ffn_W_dec, L1_ffn_b_dec, L1_ffn_W_down, L1_ffn_b_down, L1_ffn_W_up, L1_ffn_b_up, L1_ffn_connected_idx)
    x = x + _L1_attn_b_ref(_layernorm(x, axis=-1), L1_attn_b_w_in, L1_attn_b_b_in, L1_attn_b_w_out, L1_attn_b_b_out)
    x = x + _L1_ffn_ref(_layernorm(x, axis=-1), L1_ffn_W_base, L1_ffn_b_base, L1_ffn_W_enc, L1_ffn_b_enc, L1_ffn_W_dec, L1_ffn_b_dec, L1_ffn_W_down, L1_ffn_b_down, L1_ffn_W_up, L1_ffn_b_up, L1_ffn_connected_idx)
    return x

_drawn_inputs = setup_inputs


def setup_inputs(seed=0):
    import zlib

    import numpy as np

    out = dict(_drawn_inputs(seed))
    spreads = {'L0_attn_b_bq': (0.0, 0.449),
     'L0_attn_b_bk': (0.0, 0.8),
     'L0_attn_b_bv': (0.0, 0.1),
     'L0_attn_b_bo': (0.0, 0.1),
     'L1_attn_a_bo': (0.0, 0.1),
     'L1_attn_b_b_in': (0.0, 0.314),
     'L1_attn_b_b_out': (0.0, 0.1),
     'L1_ffn_b_base': (0.0, 0.1),
     'L1_ffn_b_enc': (0.0, 0.1),
     'L1_ffn_b_dec': (0.0, 0.1),
     'L1_ffn_b_down': (0.0, 0.1),
     'L1_ffn_b_up': (0.0, 0.1)}
    factors = {'L0_attn_a_bq': 8.0,
     'L0_attn_a_bk': 8.0,
     'L0_ffn_fast_b': 8.0,
     'L0_ffn_w_fc': 2.8,
     'L0_ffn_u': 8.0,
     'L0_ffn_v': 8.0,
     'L1_attn_a_Wq': 8.0,
     'L1_attn_a_Wk': 8.0,
     'L1_attn_a_Wv': 8.0,
     'L1_attn_a_Wo': 8.0}
    for name, (base, spread) in spreads.items():
        noise = np.random.default_rng([zlib.crc32(name.encode()), seed]).standard_normal(out[name].shape)
        drawn = base * np.exp(spread * noise) if base else spread * noise
        out[name] = jnp.asarray(drawn.astype(out[name].dtype))
    for name, factor in factors.items():
        out[name] = (out[name] * factor).astype(out[name].dtype)
    return out
```

```python
from contextlib import ExitStack

import concourse.bass as bass
from concourse import mybir

ALU = mybir.AluOpType
ACT = mybir.ActivationFunctionType
AX = mybir.AxisListType
F32 = mybir.dt.float32
BF16 = mybir.dt.bfloat16
I32 = mybir.dt.int32

P = 128
B, T, E = 8, 512, 128
NT = T // P
H = 16
HG, HPG = 4, 4
IB = 64
NIB = T // IB
NU = HG * NIB
UNITS = NT + 3 * NU
MHAS = 3
DHEAD = (8, 4, 8)
POS, FULL, WINDOW = 0, 1, 2
LNS = 8
YS = 7
HID = 512
FT = HID // P
RANK = 16
NA, AH, AR = 8, 32, 64
MAXLEN = 128
NREL = 2 * MAXLEN - 1
TAPS = 4
DELTAS = (192, 128, 64, 0, -64, -128)
RTL = 512
SPLIT_ROWS = 64
SLOTS_Q = (0, 1, 2, 0, 1, 0)
SLOTS_K = (0, 0, 0, 1, 1, 2)
PREP_AT = 4096
NEG = -1e30
EPS = 1e-5
PACK = AR + E + 1

PREP_SECTIONS = (
    ("gate", 1), ("w_fc", FT * P), ("w_proj", HID), ("fast_b", RANK), ("uT", HID), ("v", P), ("relT", NREL),
    ("keep1", P), ("keep0", P),
)
SECTIONS = (
    ("ident", P), ("negident", P), ("wq_a", E), ("wk_a", E), ("wv_a", E), ("bq_a", 1), ("bk_a", 1), ("bv_a", E),
    ("onehot", T), ("spread", P),
    ("wq0", E), ("wk0", E), ("wv0", E), ("wqn0", E), ("bq0", 1), ("bk0", 1), ("bv0", E), ("bqr0", H), ("wo0", HG * E),
    ("wq1", 64), ("wk1", 64), ("wv1", 64), ("wo1", HG * E),
    ("enc", NA * AH), ("b_enc", 2), ("dec", NA * E), ("b_dec", NA), ("pack", NA * PACK), ("w_base", E), ("iota", NA),
    ("wq2", E), ("wk2", E), ("wv2", E), ("bq2", 1), ("bk2", 1), ("bv2", E), ("wo2", HG * E),
)
OFF = {}
WCOLS = 0
for _name, _cols in SECTIONS:
    OFF[_name] = (WCOLS, _cols)
    WCOLS += _cols
PREP_COLS = 0
for _name, _cols in PREP_SECTIONS:
    OFF[_name] = (WCOLS + PREP_COLS, _cols)
    PREP_COLS += _cols

DVE_STEPS = 337
POOL_STEPS = MHAS


def build(nc: bass.Bass, x: bass.AP, packed: bass.AP, cidx: bass.AP, out: bass.AP):
    relpad = nc.dram_tensor("relpad_scratch", (8, RTL), F32, kind="Internal").ap()
    with ExitStack() as ctx:
        def sb(name, shape, dt=F32):
            return ctx.enter_context(nc.sbuf_tensor(name, shape, dt))

        def sem(name):
            return ctx.enter_context(nc.semaphore(name))

        W = sb("W", [P, WCOLS])

        def w(name, rows=P):
            o, n = OFF[name]
            return W[0:rows, o:o + n] if o < WCOLS else PT[0:rows, 1, PREP_AT + o - WCOLS:PREP_AT + o - WCOLS + n]

        ident_b = sb("ident_b", [P, P], BF16)
        ones_b = sb("ones_b", [P, P], BF16)
        ones_f = sb("ones_f", [P, P])
        masks = sb("masks", [P, 2, P], BF16)
        zero_col = sb("zero_col", [P, 1])
        cidx_i = sb("cidx_i", [P, NA], I32)
        cidx_f = sb("cidx_f", [P, NA])
        wrap = sb("wrap", [P, NA])
        Wfc = sb("Wfc", [P, HID])
        Wpr = sb("Wpr", [P, FT, E])
        relwin = sb("relwin", [P, len(DELTAS), TAPS, P])
        relparts = sb("relparts", [8, 3, 2], BF16)
        relrest = sb("relrest", [8, 2, 2])
        relclip_c = sb("relclip_c", [SPLIT_ROWS, 2], BF16)
        relclip = sb("relclip", [SPLIT_ROWS, 2, P], BF16)

        xin = sb("xin", [P, NT, E])
        X = sb("X", [P, NT, E])
        xout = sb("xout", [P, NT, E])
        stats = sb("stats", [P, NT, 6])
        mv = sb("mv", [P, NT, 2])
        fence = sb("fence", [P, 1])
        var = sb("var", [P, NT])
        hvar = sb("hvar", [P, NT])
        rs = [sb(f"rs{i}", [P, NT]) for i in range(2)]
        nt_a = sb("nt_a", [P, NT])
        nt_b = sb("nt_b", [P, NT])
        xn = sb("xn", [P, NT, E])
        xnT = sb("xnT", [E, T])

        QF = sb("QF", [P, T])
        KF = sb("KF", [P, T])
        Q3 = sb("Q3", [P, 3, T], BF16)
        K3 = sb("K3", [P, 3, T], BF16)
        VA = sb("VA", [P, NT, E + 4])
        QO = sb("QO", [SPLIT_ROWS, H, T], BF16)
        KO = sb("KO", [SPLIT_ROWS, H, T], BF16)
        WR = sb("WR", [P, 2, 16, 8])
        QH = sb("QH", [P, 2, HPG, T])
        VO = sb("VO", [P, NT, H, 32])
        PT = sb("PT", [P, 2, NT * HPG * T])
        MX = sb("MX", [P, 2, HPG * IB])
        NM = sb("NM", [P, 2, 2])
        DG = sb("DG", [P, 2, 2, P], BF16)
        OS = sb("OS", [P, T])
        Qrest = REC = xn[:, :, :].rearrange("p t e -> p (t e)")
        Krest = OS
        AT = sb("AT", [P, HG, T])
        arec = sb("arec", [P, NT])
        MID = sb("MID", [P, T])
        SEL = sb("SEL", [P, 2, PACK])
        LP = sb("LP", [P, NA])
        ch = sb("ch", [P, 8, NA])

        def pt(par):
            return PT[:, par, :].rearrange("p (t h i) -> p t h i", t=NT, h=HPG)

        relrow = PT[0:8, 0, 6144:6144 + RTL]
        PTA = PT[:, 0, 0:2 * NT * P].rearrange("p (u t i) -> p u t i", u=2, t=NT)
        RL = PT[:, 0, 0:FT * T].rearrange("p (t i) -> p t i", t=FT)
        R2 = PT[:, 1, 0:FT * T].rearrange("p (t i) -> p t i", t=FT)
        EH = PT[:, 0, 0:2 * T].rearrange("p (t i) -> p t i", t=2)
        DF = PT[:, 1, 0:2 * T].rearrange("p (t i) -> p t i", t=2)
        sq = PT[:, 1, 2 * T:4 * T].rearrange("p (t i) -> p t i", t=2)

        SB = ctx.enter_context(nc.psum_tensor("SB", [P, 3, 1024], F32))
        TB = ctx.enter_context(nc.psum_tensor("TB", [P, 512], F32))
        OB = ctx.enter_context(nc.psum_tensor("OB", [P, 512], F32))

        def bank(n):
            return SB[:, n // 2, 512 * (n % 2):512 * (n % 2) + 512]

        w_loaded = sem("w_loaded")
        prep_pe = sem("prep_pe")
        prep_dve = sem("prep_dve")
        prep_pool = sem("prep_pool")
        rel_loaded = sem("rel_loaded")
        clip_loaded = sem("clip_loaded")
        x_loaded = sem("x_loaded")
        xin_free = sem("xin_free")
        dve_step = sem("dve_step")
        pool_step = sem("pool_step")
        normed = sem("normed")
        turned = sem("turned")
        xnT_ready = sem("xnT_ready")
        proj_a = sem("proj_a")
        qk_a = sem("qk_a")
        v_a = sem("v_a")
        scores_ready = sem("scores_ready")
        colmax_ready = sem("colmax_ready")
        colmax_turned = sem("colmax_turned")
        shift_ready = sem("shift_ready")
        scores_shifted = sem("scores_shifted")
        probs_ready = sem("probs_ready")
        out_a = sem("out_a")
        out_a_used = sem("out_a_used")
        proj = sem("proj")
        q_high = sem("q_high")
        k_high = sem("k_high")
        q_rest = sem("q_rest")
        k_rest = sem("k_rest")
        v_ready = sem("v_ready")
        operands_in = sem("operands_in")
        wq_repeated = sem("wq_repeated")
        q_spread = sem("q_spread")
        q_hot = sem("q_hot")
        pv_ready = sem("pv_ready")
        pv_copied = sem("pv_copied")
        den_ready = sem("den_ready")
        den_used = sem("den_used")
        head_out = sem("head_out")
        hidden = sem("hidden")
        relued = sem("relued")
        squared = sem("squared")
        y_ready = sem("y_ready")
        encoded = sem("encoded")
        enc_relued = sem("enc_relued")
        decoded = sem("decoded")
        diff_ready = sem("diff_ready")
        loss_part = sem("loss_part")
        loss_ready = sem("loss_ready")
        adapter_ready = sem("adapter_ready")
        down_ready = sem("down_ready")
        mid_ready = sem("mid_ready")
        xout_ready = sem("xout_ready")
        stored = sem("stored")

        class Own:

            def __init__(self, eng, semaphore, base):
                self.eng, self.sem, self.base, self.n = eng, semaphore, base, 0

            def done(self, ins):
                self.n += 1
                ins.then_inc(self.sem, 1)

            def settle(self):
                self.eng.wait_ge(self.sem, self.base + self.n)

            def link(self, ins):
                self.done(ins)
                self.settle()

        def operands(a):
            return KO, DHEAD[a]

        def slots_of(a, ib):
            if a != WINDOW:
                return 0, NT
            return (0, 2) if ib >= 2 else (1, 2)

        N_WLOADS = 4
        OPD = 12 * 16
        ZEROED = 32

        def operands_total(a):
            return OPD * (a + 1) + (ZEROED if a >= FULL else 0)

        block = ctx.enter_context(nc.Block())

        @block.sync
        def _(sp):
            cuts = [0, OFF["onehot"][0], OFF["enc"][0], WCOLS]
            sp.dma_start(cidx_i[:, :], cidx).then_inc(w_loaded, 16)
            sp.dma_start(PT[:, 1, PREP_AT:PREP_AT + PREP_COLS], packed[:, WCOLS:]).then_inc(w_loaded, 16)
            for n in range(3):
                sp.dma_start(W[:, cuts[n]:cuts[n + 1]], packed[:, cuts[n]:cuts[n + 1]]).then_inc(w_loaded, 16)
            sp.wait_ge(prep_pool, 1)
            sp.dma_start(relpad, relrow[:, :]).then_inc(stored, 16)
            sp.wait_ge(stored, 16)
            for a in range(16):
                for n, dl in enumerate(DELTAS):
                    for c in range(TAPS):
                        y = 2 * MAXLEN - 1 - dl - (4 * a + c)
                        sp.dma_start(relwin[8 * a:8 * a + 8, n, c, :], relpad[:, y:y + P]).then_inc(rel_loaded, 16)
            sp.wait_ge(prep_pool, 2)
            for s, part in enumerate(SLOTS_K):
                sp.dma_start(relclip_c[8 * s:8 * s + 8, :], relparts[:, part, :]).then_inc(clip_loaded, 16)

            with sp.Fori(0, B) as b:
                sp.wait_ge(xin_free, b + 1)
                sp.dma_start(xin[:, :, :], x[bass.ds(b, 1), :, :].rearrange("o (t p) e -> p (o t) e", p=P)
                             ).then_inc(x_loaded, 16)
                for a in range(MHAS):
                    ko, d = operands(a)
                    rows = d * H

                    def load(dst, slot, src, part):
                        sp.dma_start(dst[d * slot:d * slot + d, :, :], src[0:rows, part, :]).then_inc(operands_in, 16)

                    if a == FULL:
                        sp.wait_ge(k_high, MHAS * b + a + 1)
                        for r0 in (6 * d, 9 * d):
                            sp.dma_start(ko[r0:r0 + 3 * d, :, :], QO[48:48 + 3 * d, :, :]).then_inc(operands_in, 16)
                    for part, sq_, sk_ in ((0, q_high, k_high), (1, q_rest, k_rest), (2, q_rest, k_rest)):
                        need = MHAS * b + a + 1 if part == 0 else 2 * MHAS * b + 2 * a + part
                        sp.wait_ge(sq_, need)
                        for s in range(6):
                            if SLOTS_Q[s] == part:
                                load(QO, s, Q3, part)
                        sp.wait_ge(sk_, need)
                        for s in range(6):
                            if SLOTS_K[s] == part:
                                load(ko, s, K3, part)
                sp.wait_ge(xout_ready, b + 1)
                sp.dma_start(out[bass.ds(b, 1), :, :].rearrange("o (t p) e -> p (o t) e", p=P), xout[:, :, :]
                             ).then_inc(stored, 16)
            sp.wait_ge(stored, 16 * B + 16)

        @block.gpsimd
        def _(pool):
            pool.memset(ones_b[:, :], 1.0)
            pool.memset(ones_f[:, :], 1.0)
            pool.memset(zero_col[:, :], 0.0)
            pool.memset(QO[:, :, :], 0.0)
            pool.memset(KO[:, :, :], 0.0)
            pool.memset(VO[:, :, :, :], 0.0)
            pool.memset(VA[:, :, :], 1.0)
            pool.memset(MID[:, :], 1.0)
            pool.memset(relclip_c[:, :], 0.0).then_inc(pool_step, 1)
            pool.wait_ge(pool_step, 1)
            pool.memset(VO[:, :, :, 8:9], 1.0)
            pool.wait_ge(w_loaded, 16 * (N_WLOADS + 1))
            rel = w("relT", 8)
            pool.tensor_copy(relrow[:, 0:MAXLEN], rel[:, 0:1].broadcast_to([8, MAXLEN]))
            pool.tensor_copy(relrow[:, MAXLEN:MAXLEN + NREL], rel)
            pool.tensor_copy(relrow[:, MAXLEN + NREL:RTL], rel[:, NREL - 1:NREL].broadcast_to([8, RTL - MAXLEN - NREL])
                             ).then_inc(prep_pool, 1)
            ends = rel[:, 0:NREL:NREL - 1]
            pool.tensor_copy(relparts[:, 0, :], ends).then_inc(pool_step, 1)
            pool.wait_ge(pool_step, 2)
            pool.tensor_tensor(relrest[:, 0, :], ends, relparts[:, 0, :], ALU.subtract).then_inc(pool_step, 1)
            pool.wait_ge(pool_step, 3)
            pool.tensor_copy(relparts[:, 1, :], relrest[:, 0, :]).then_inc(pool_step, 1)
            pool.wait_ge(pool_step, 4)
            pool.tensor_tensor(relparts[:, 2, :], relrest[:, 0, :], relparts[:, 1, :], ALU.subtract
                               ).then_inc(prep_pool, 1)
            pool.wait_ge(clip_loaded, 16 * 6)
            pool.tensor_copy(relclip[:, :, :], relclip_c[:, :].unsqueeze(2).broadcast_to([SPLIT_ROWS, 2, P])
                             ).then_inc(prep_pool, 1)

            with pool.Fori(0, B) as b:
                own = Own(pool, pool_step, b * POOL_STEPS + 4)
                for a in range(MHAS):
                    rows = DHEAD[a] * H
                    pool.wait_ge(k_high, MHAS * b + a + 1)
                    own.done(pool.tensor_tensor(Krest[0:rows, :], KF[0:rows, :], K3[0:rows, 0, :], ALU.subtract))
                    pool.tensor_tensor(K3[0:rows, 1, :], KF[0:rows, :], K3[0:rows, 0, :], ALU.subtract
                                       ).then_inc(k_rest, 1)
                    own.settle()
                    pool.wait_ge(k_rest, 2 * MHAS * b + 2 * a + 1)
                    pool.tensor_tensor(K3[0:rows, 2, :], Krest[0:rows, :], K3[0:rows, 1, :], ALU.subtract
                                       ).then_inc(k_rest, 1)
                    if a == POS:
                        for h in range(H):
                            if h >= 2:
                                pool.wait_ge(q_spread, H * b + h - 1)
                            pool.tensor_tensor(WR[:, h % 2, :, :], w("wqn0")[:, 8 * h:8 * h + 8].unsqueeze(1)
                                               .broadcast_to([P, 16, 8]), ones_f[:, :].rearrange(
                                                   "p (a d) -> p a d", a=16), ALU.mult).then_inc(wq_repeated, 1)
                assert own.n == POOL_STEPS, own.n

        @block.tensor
        def _(pe):
            idf = w("ident")
            pe.wait_ge(prep_dve, 1)
            for t in range(FT):
                ins = pe.transpose(bank(0)[:, P * t:P * t + P], RL[:, 0, P * t:P * t + P], idf)
            ins.then_inc(prep_pe, 1)
            pe.wait_ge(prep_dve, 2)
            for t in range(FT):
                ins = pe.transpose(bank(1)[:, P * t:P * t + P], RL[:, 1, P * t:P * t + P], idf)
            ins.then_inc(prep_pe, 1)
            pe.matmul(bank(2)[0:RANK, :], w("fast_b", RANK), w("uT", RANK), start=True, stop=True).then_inc(prep_pe, 1)
            pe.wait_ge(prep_dve, 3)
            pe.matmul(bank(3), w("v", RANK), R2[0:RANK, 0, :], start=True, stop=True).then_inc(prep_pe, 1)
            pe.wait_ge(prep_dve, 4)
            pe.wait_ge(prep_pool, 3)
            pe.wait_ge(rel_loaded, 16 * 16 * len(DELTAS) * TAPS)

            with pe.Fori(0, B) as b:
                def turn_normed(n):
                    pe.wait_ge(normed, LNS * b + n + 1)
                    for t in range(NT):
                        ins = pe.transpose(TB[:, P * t:P * t + P], xn[:, t, :], idf)
                    ins.then_inc(turned, 1)
                    pe.wait_ge(xnT_ready, LNS * b + n + 1)

                def turn_colmax(g, par, cols):
                    pe.wait_ge(colmax_ready, UNITS * b + g + 1)
                    if g > 0:
                        pe.wait_ge(shift_ready, UNITS * b + g)
                    for q in range(cols // P):
                        ins = pe.transpose(TB[:, P * q:P * q + P], MX[:, par, P * q:P * q + P], idf)
                    ins.then_inc(colmax_turned, 1)

                def single_head():
                    pe.matmul(bank(0), w("wq_a"), xnT[:, :], start=True, stop=True).then_inc(proj_a, 1)
                    pe.matmul(bank(1), w("wk_a"), xnT[:, :], start=True, stop=True).then_inc(proj_a, 1)
                    for t in range(NT):
                        ins = pe.matmul(bank(2)[:, P * t:P * t + P], xnT[:, P * t:P * t + P], w("wv_a"),
                                        start=True, stop=True)
                    ins.then_inc(proj_a, 1)
                    pe.wait_ge(qk_a, 2 * b + 2)
                    pe.wait_ge(v_a, b + 1)
                    for k in range(NT + 3):
                        if k < NT:
                            sc = SB[:, k % 3, :]
                            if k == 3:
                                pe.wait_ge(probs_ready, UNITS * b + k - 2)
                            for j in range(k + 1):
                                pe.matmul(sc[:, P * j:P * j + P], KF[:, P * j:P * j + P], QF[:, P * k:P * k + P],
                                          start=(j == 0), stop=False, skip_group_check=True)
                            pe.matmul(sc[:, P * k:P * k + P], ident_b[:, :], masks[:, 1, :], start=False, stop=False,
                                      skip_group_check=True).then_inc(scores_ready, 1)
                        if 1 <= k <= NT:
                            turn_colmax(k - 1, (k - 1) % 2, P)
                        if 2 <= k < NT + 2:
                            u = k - 2
                            pe.wait_ge(shift_ready, UNITS * b + u + 1)
                            pe.matmul(SB[:, u % 3, 0:P * (u + 1)], ones_b[:, :],
                                      DG[:, u % 2, 0:1, :].broadcast_to([P, u + 1, P]), start=False, stop=True,
                                      skip_group_check=True).then_inc(scores_shifted, 1)
                        if k >= 3:
                            u = k - 3
                            pe.wait_ge(probs_ready, UNITS * b + u + 1)
                            if u >= 2:
                                pe.wait_ge(out_a_used, NT * b + u - 1)
                            dst = OB if u % 2 == 0 else bank(5)
                            for j in range(u + 1):
                                ins = pe.matmul(dst[:, 0:E + 2], PTA[:, u % 2, j, :], VA[:, j, 0:E + 2],
                                                start=(j == 0), stop=(j == u))
                            ins.then_inc(out_a, 1)

                def multi_head(a):
                    ko, d = operands(a)
                    rows = d * H
                    ein = E if a != FULL else E // 2
                    first = NT + NU * a
                    for t in range(NT):
                        ins = pe.matmul(bank(2)[:, rows * t:rows * t + rows], xnT[0:ein, P * t:P * t + P],
                                        w(f"wv{a}", ein), start=True, stop=True)
                    ins.then_inc(proj, 1)
                    pe.matmul(bank(0)[0:rows, :], w(f"wq{a}", ein), xnT[0:ein, :], start=True, stop=True).then_inc(proj, 1)
                    pe.matmul(bank(1)[0:rows, :], w(f"wk{a}", ein), xnT[0:ein, :], start=True, stop=True).then_inc(proj, 1)

                    def spread(h):
                        if h > 0:
                            pe.wait_ge(q_hot, H * b + h)
                        if h >= HPG and h % HPG == 3:
                            g = h // HPG - 2
                            if g >= 0:
                                pe.wait_ge(den_used, HG * MHAS * b + g + 1)
                        pe.wait_ge(wq_repeated, H * b + h + 1)
                        pe.matmul(OB[:, :], WR[:, h % 2, :, :].rearrange("p a d -> p (a d)"), xnT[:, :], start=True, stop=True).then_inc(q_spread, 1)

                    if a == POS:
                        for h in range(HPG):
                            spread(h)

                    def scores(k):
                        hg, ib = divmod(k, NIB)
                        lo, hi = slots_of(a, ib)
                        sc = SB[:, k % 3, :].rearrange("p (t h i) -> p t h i", t=NT, h=HPG)
                        if k == 0:
                            pe.wait_ge(operands_in, operands_total(MHAS - 1) * b + operands_total(a))
                            pe.wait_ge(v_ready, MHAS * b + a + 1)
                        if k >= 3:
                            pe.wait_ge(probs_ready, UNITS * b + first + k - 2)
                        if a == POS and ib == 0:
                            pe.wait_ge(q_hot, H * b + HPG * (hg + 1))
                        for s in range(lo, hi):
                            jt = s if a != WINDOW else ib // 2 - 1 + s
                            for h in range(HPG):
                                ins = pe.matmul(sc[:, s, h, :], ko[:, HPG * hg + h, P * jt:P * jt + P],
                                                QO[:, HPG * hg + h, IB * ib:IB * ib + IB],
                                                start=(h == 0 and (s == lo or s % 2 == 0)), stop=False, skip_group_check=True)
                            if a == POS:
                                dl = IB * ib - P * jt
                                if dl in DELTAS:
                                    for c in range(TAPS):
                                        ins = pe.matmul(
                                            sc[:, s, :, c:IB:TAPS], relwin[:, DELTAS.index(dl), c, :],
                                            QH[:, hg % 2, :, IB * ib + c:IB * ib + IB:TAPS],
                                            start=False, stop=False, skip_group_check=True)
                                else:
                                    ins = pe.matmul(sc[:, s, :, :], relclip[:, 0 if dl > 0 else 1, :],
                                                    QO[:, HPG * hg:HPG * hg + HPG, IB * ib:IB * ib + IB],
                                                    start=False, stop=False, skip_group_check=True)
                            if a == WINDOW:
                                m0 = IB * (ib % 2)
                                ins = pe.matmul(sc[:, s, :, :], ident_b[:, :],
                                                masks[:, s:s + 1, m0:m0 + IB].broadcast_to([P, HPG, IB]),
                                                start=False, stop=False, skip_group_check=True)
                        ins.then_inc(scores_ready, 1)

                    def shift(k):
                        lo, hi = slots_of(a, k % NIB)
                        pe.wait_ge(shift_ready, UNITS * b + first + k + 1)
                        row = DG[:, k % 2, :, :].rearrange("p q i -> p (q i)").unsqueeze(1)
                        for s in range(lo, hi, 2):
                            n = min(2, hi - s)
                            ins = pe.matmul(SB[:, k % 3, 256 * s:256 * (s + n)], ones_b[:, :],
                                            row.broadcast_to([P, n, HPG * IB]), start=False, stop=True,
                                            skip_group_check=True)
                        ins.then_inc(scores_shifted, 1)

                    def weigh(hg):
                        pe.wait_ge(probs_ready, UNITS * b + first + NIB * (hg + 1))
                        pr = pt(hg % 2)
                        if a == WINDOW:
                            parts = [(P * t, P, s, t - 1 + s, s == max(0, 1 - t), s == 1)
                                     for t in range(NT) for s in range(max(0, 1 - t), 2)]
                        else:
                            parts = [(0, T, j, j, j == 0, j == NT - 1) for j in range(NT)]
                        for i0, n, s, jt, st, en in parts:
                            for h in range(HPG):
                                ins = pe.matmul(OB[32 * h:32 * h + 32, i0:i0 + n], VO[:, jt, HPG * hg + h, :],
                                                pr[:, s, h, i0:i0 + n], start=st, stop=en)
                        ins.then_inc(pv_ready, 1)

                    def denominators(hg):
                        pe.wait_ge(pv_copied, HG * MHAS * b + HG * a + hg + 1)
                        pe.matmul(OB[:, :], w("spread"), OS[:, :], start=True, stop=True).then_inc(den_ready, 1)

                    for k in range(NU + 5):
                        hg, r = divmod(k, NIB)
                        if k < NU:
                            scores(k)
                        if 1 <= k <= NU:
                            turn_colmax(first + k - 1, (k - 1) % 2, HPG * IB)
                        if 2 <= k < NU + 2:
                            shift(k - 2)
                        if a == POS and r in (0, 1, 2, 6) and hg + 1 < HG:
                            spread(HPG * (hg + 1) + (0, 1, 2, 6).index(r))
                        if r == 3 and hg >= 1:
                            if a == POS and hg < HG:
                                pe.wait_ge(q_hot, H * b + min(H, HPG * hg + 7))
                            if hg >= 2 or a > 0:
                                pe.wait_ge(den_used, HG * MHAS * b + HG * a + hg - 1)
                            weigh(hg - 1)
                        if r == 4 and hg >= 1:
                            denominators(hg - 1)
                    pe.wait_ge(head_out, HG * MHAS * b + HG * (a + 1))
                    for t in range(NT):
                        for hg in range(HG):
                            ins = pe.matmul(bank(0)[:, E * t:E * t + E], AT[:, hg, P * t:P * t + P],
                                            w(f"wo{a}")[:, E * hg:E * hg + E], start=(hg == 0), stop=(hg == HG - 1))
                    ins.then_inc(y_ready, 1)

                def bit_ffn(f):
                    for t in range(FT):
                        pe.matmul(bank(t), Wfc[:, P * t:P * t + P], xnT[:, :], start=True, stop=True
                                  ).then_inc(hidden, 1)
                    pe.wait_ge(squared, FT * (2 * b + f + 1))
                    for t in range(NT):
                        for c in range(FT):
                            ins = pe.matmul(bank(4)[:, E * t:E * t + E], R2[:, c, P * t:P * t + P], Wpr[:, c, :],
                                            start=(c == 0), stop=(c == FT - 1))
                    ins.then_inc(y_ready, 1)

                def routed_ffn(f):
                    r = 2 * b + f
                    for c in range(2):
                        pe.matmul(bank(c), w("enc")[:, P * c:P * c + P], xnT[:, :], start=True, stop=True
                                  ).then_inc(encoded, 1)
                    for n in range(NA):
                        c = n // 4
                        if n % 4 == 0:
                            pe.wait_ge(enc_relued, 2 * r + c + 1)
                        if n >= 3:
                            pe.wait_ge(diff_ready, NA * r + n - 2)
                        pe.matmul(bank(2 + n % 3), w("dec")[:, E * n:E * n + E], EH[:, c, :], start=True, stop=True
                                  ).then_inc(decoded, 1)
                    pe.wait_ge(loss_part, NA * r + NA)
                    pe.matmul(TB[:, 0:NA], ones_f[:, :], LP[:, :], start=True, stop=True).then_inc(loss_ready, 1)
                    pe.wait_ge(adapter_ready, r + 1)
                    chosen = SEL[:, (NA - 1) % 2, :]
                    pe.matmul(bank(0)[0:AR, :], chosen[:, 0:AR], xnT[:, :], start=True, stop=True).then_inc(down_ready, 1)
                    pe.wait_ge(mid_ready, r + 1)
                    for t in range(NT):
                        pe.matmul(bank(1)[:, E * t:E * t + E], xnT[:, P * t:P * t + P], w("w_base"), start=True, stop=False)
                        ins = pe.matmul(bank(1)[:, E * t:E * t + E], MID[:, P * t:P * t + P], chosen[:, AR:AR + E],
                                        start=False, stop=True)
                    ins.then_inc(y_ready, 1)

                turn_normed(0)
                single_head()
                turn_normed(1)
                bit_ffn(0)
                turn_normed(2)
                multi_head(POS)
                turn_normed(3)
                bit_ffn(1)
                turn_normed(4)
                multi_head(FULL)
                turn_normed(5)
                routed_ffn(0)
                turn_normed(6)
                multi_head(WINDOW)
                turn_normed(7)
                routed_ffn(1)

        @block.scalar
        def _(act):
            act.wait_ge(w_loaded, 16 * (N_WLOADS + 1))
            with act.Fori(0, B) as b:
                def take_turned(n):
                    act.wait_ge(turned, LNS * b + n + 1)
                    act.activation(xnT[:, :], TB[:, :], ACT.Copy).then_inc(xnT_ready, 1)

                def single_head():
                    act.wait_ge(proj_a, 3 * b + 1)
                    act.activation(QF[:, :], bank(0), ACT.Identity, bias=w("bq_a")).then_inc(qk_a, 1)
                    act.wait_ge(proj_a, 3 * b + 2)
                    act.activation(KF[:, :], bank(1), ACT.Identity, bias=w("bk_a")).then_inc(qk_a, 1)
                    for u in range(NT):
                        act.wait_ge(scores_shifted, UNITS * b + u + 1)
                        if u >= 2:
                            act.wait_ge(out_a, NT * b + u - 1)
                        act.activation(PTA[:, u % 2, 0:u + 1, :],
                                       SB[:, u % 3, 0:P * (u + 1)].rearrange("p (t i) -> p t i", i=P), ACT.Exp,
                                       scale=float(E) ** -0.5).then_inc(probs_ready, 1)

                def multi_head(a):
                    d = DHEAD[a]
                    rows = d * H
                    first = NT + NU * a
                    bq = w(f"bq{a}") if a != FULL else zero_col[0:rows, :]
                    bk = w(f"bk{a}") if a != FULL else zero_col[0:rows, :]
                    act.wait_ge(proj, 3 * MHAS * b + 3 * a + 2)
                    act.activation(QF[0:rows, :], bank(0)[0:rows, :], ACT.Identity, bias=bq)
                    act.activation(Q3[0:rows, 0, :], bank(0)[0:rows, :], ACT.Identity, bias=bq).then_inc(q_high, 1)
                    act.wait_ge(proj, 3 * MHAS * b + 3 * a + 3)
                    act.activation(KF[0:rows, :], bank(1)[0:rows, :], ACT.Identity, bias=bk)
                    act.activation(K3[0:rows, 0, :], bank(1)[0:rows, :], ACT.Identity, bias=bk).then_inc(k_high, 1)
                    for k in range(2, NU + 5):
                        hg, r = divmod(k, NIB)
                        if k < NU + 2:
                            u = k - 2
                            ug, ib = divmod(u, NIB)
                            lo, hi = slots_of(a, ib)
                            act.wait_ge(scores_shifted, UNITS * b + first + u + 1)
                            sc = SB[:, u % 3, :].rearrange("p (t h i) -> p t h i", t=NT, h=HPG)
                            act.activation(pt(ug % 2)[:, lo:hi, :, IB * ib:IB * ib + IB], sc[:, lo:hi, :, :], ACT.Exp,
                                           scale=8.0 ** -0.5).then_inc(probs_ready, 1)
                        if r == 3 and hg >= 1:
                            g = HG * MHAS * b + HG * a + hg
                            act.wait_ge(pv_ready, g)
                            if hg >= 2:
                                act.wait_ge(head_out, g - 1)
                            act.activation(OS[:, :], OB[:, :], ACT.Copy).then_inc(pv_copied, 1)

                def bit_ffn(f):
                    for t in range(FT):
                        act.wait_ge(hidden, FT * (2 * b + f) + t + 1)
                        act.activation(RL[:, t, :], bank(t), ACT.Relu).then_inc(relued, 1)

                def routed_ffn(f):
                    r = 2 * b + f
                    for c in range(2):
                        act.wait_ge(encoded, 2 * r + c + 1)
                        act.activation(EH[:, c, :], bank(c), ACT.Relu, bias=w("b_enc")[:, c:c + 1]).then_inc(enc_relued, 1)
                    for n in range(NA):
                        act.wait_ge(diff_ready, NA * r + n + 1)
                        if n >= 2:
                            act.wait_ge(loss_part, NA * r + n - 1)
                        act.activation(sq[:, n % 2, :], DF[:, n % 2, :], ACT.Square, accum_out=LP[:, n:n + 1]
                                       ).then_inc(loss_part, 1)
                    act.wait_ge(down_ready, r + 1)
                    act.activation(MID[0:AR, :], bank(0)[0:AR, :], ACT.Relu,
                                   bias=SEL[0:AR, (NA - 1) % 2, PACK - 1:PACK]).then_inc(mid_ready, 1)

                take_turned(0)
                single_head()
                take_turned(1)
                bit_ffn(0)
                take_turned(2)
                multi_head(POS)
                take_turned(3)
                bit_ffn(1)
                take_turned(4)
                multi_head(FULL)
                take_turned(5)
                routed_ffn(0)
                take_turned(6)
                multi_head(WINDOW)
                take_turned(7)
                routed_ffn(1)

        @block.vector
        def _(dve):
            dve.wait_ge(w_loaded, 16 * (N_WLOADS + 1))
            own = Own(dve, dve_step, 0)
            dve.tensor_copy(ident_b[:, :], w("ident"))
            dve.tensor_copy(masks[:, 0, :], w("keep0"))
            dve.tensor_copy(masks[:, 1, :], w("keep1"))
            own.link(dve.tensor_copy(cidx_f[:, :], cidx_i[:, :]))
            own.link(dve.tensor_scalar(wrap[:, :], cidx_f[:, :], 0.0, float(NA), ALU.is_lt, ALU.mult))
            own.link(dve.tensor_tensor(cidx_f[:, :], cidx_f[:, :], wrap[:, :], ALU.add))
            own.link(dve.tensor_scalar(cidx_f[:, :], cidx_f[:, :], 0.0, float(NA - 1), ALU.max, ALU.min))

            def ternary(src, dst, blocks, width, at):
                mag = PT[:, 0, 4096:4096 + HID].rearrange("p (t i) -> p t i", t=blocks)
                low = PT[:, 0, 4608:4608 + HID].rearrange("p (t i) -> p t i", t=blocks)
                sc_ = ch[:, 0 + at, 0:blocks]
                half = ch[:, 1 + at, 0:blocks]
                nhalf = ch[:, 2 + at, 0:blocks]
                own.link(dve.scalar_tensor_tensor(out=mag, in0=src, scalar=-1.0, in1=src, op0=ALU.mult, op1=ALU.max))
                own.link(dve.tensor_reduce(sc_, mag, AX.X, ALU.add))
                own.link(dve.tensor_scalar(sc_, sc_, 1.0 / width, EPS, ALU.mult, ALU.max))
                own.done(dve.tensor_scalar(half, sc_, 0.5, None, ALU.mult))
                own.link(dve.tensor_scalar(nhalf, sc_, -0.5, None, ALU.mult))
                for t in range(blocks):
                    own.done(dve.tensor_scalar(mag[:, t, :], src[:, t, :], half[:, t:t + 1], None, ALU.is_gt))
                    own.link(dve.tensor_scalar(low[:, t, :], src[:, t, :], nhalf[:, t:t + 1], None, ALU.is_lt))
                own.link(dve.tensor_tensor(mag, mag, low, ALU.subtract))
                own.link(dve.tensor_tensor(mag, mag, src, ALU.subtract))
                own.link(dve.tensor_tensor(mag, mag, src, ALU.add))
                for t in range(blocks):
                    ins = dve.tensor_scalar(dst[:, t, :], mag[:, t, :], sc_[:, t:t + 1], None, ALU.mult)
                    if t < blocks - 1:
                        own.done(ins)
                return ins

            ternary(w("w_fc").rearrange("p (t i) -> p t i", t=FT), RL[:, 0, :].rearrange("p (t i) -> p t i", t=FT),
                    FT, E, 0).then_inc(prep_dve, 1)
            dve.wait_ge(prep_dve, 1)
            ternary(w("w_proj").rearrange("p (t i) -> p t i", t=1), RL[:, 1, :].rearrange("p (t i) -> p t i", t=1),
                    1, HID, 3).then_inc(prep_dve, 1)
            dve.wait_ge(prep_pe, 3)
            own.done(dve.tensor_copy(Wfc[:, :], bank(0)))
            own.done(dve.tensor_copy(Wpr[:, :, :], bank(1).rearrange("p (t i) -> p t i", t=FT)))
            dve.tensor_copy(R2[0:RANK, 0, :], bank(2)[0:RANK, :]).then_inc(prep_dve, 1)
            dve.wait_ge(prep_pe, 4)
            own.settle()
            dve.scalar_tensor_tensor(out=Wfc[:, :], in0=bank(3), scalar=w("gate"), in1=Wfc[:, :], op0=ALU.mult,
                                     op1=ALU.add).then_inc(prep_dve, 1)
            prepared = own.n
            dve.tensor_copy(fence[:, :], w("ident")[:, 0:1]).then_inc(xin_free, 1)

            with dve.Fori(0, B) as b:
                own = Own(dve, dve_step, b * DVE_STEPS + prepared)

                def layer_norm(n, src):
                    for t in range(NT):
                        own.done(dve.bn_stats(stats[:, t, :], src[:, t, :]))
                    own.settle()
                    dve.tensor_copy(fence[:, :], w("ident")[:, 0:1])
                    for t in range(NT):
                        own.done(dve.bn_aggr(mv[:, t, :], stats[:, t, :]))
                    own.settle()
                    own.done(dve.tensor_scalar(hvar[:, :], mv[:, :, 1], EPS, 0.5, ALU.add, ALU.mult))
                    own.link(dve.tensor_scalar(var[:, :], mv[:, :, 1], EPS, None, ALU.add))
                    own.link(dve.tensor_scalar(rs[0][:, :].bitcast(I32), var[:, :].bitcast(I32), 1, None,
                                               ALU.logical_shift_right))
                    own.link(dve.tensor_scalar(rs[1][:, :].bitcast(I32), rs[0][:, :].bitcast(I32), -1.0,
                                               float(0x5F3759DF), ALU.mult, ALU.add))
                    for i in range(3):
                        old, new = rs[(i + 1) % 2], rs[i % 2]
                        own.link(dve.tensor_tensor(nt_a[:, :], old[:, :], old[:, :], ALU.mult))
                        own.link(dve.scalar_tensor_tensor(out=nt_b[:, :], in0=nt_a[:, :], scalar=-1.0, in1=hvar[:, :],
                                                          op0=ALU.mult, op1=ALU.mult))
                        own.link(dve.scalar_tensor_tensor(out=new[:, :], in0=nt_b[:, :], scalar=1.5, in1=old[:, :],
                                                          op0=ALU.add, op1=ALU.mult))
                    for t in range(NT):
                        ins = dve.tensor_scalar(xn[:, t, :], src[:, t, :], mv[:, t, 0:1], rs[0][:, t:t + 1],
                                                ALU.subtract, ALU.mult)
                        if t < NT - 1:
                            own.done(ins)
                    ins.then_inc(normed, 1)

                def add_bank(y, n, dst):
                    dve.wait_ge(y_ready, YS * b + y + 1)
                    return dve.tensor_tensor(dst[:, :, :], X[:, :, :], bank(n).rearrange("p (t e) -> p t e", t=NT), ALU.add)

                def colmax(g, k, slot_view, n, cols, single):
                    dve.wait_ge(scores_ready, UNITS * b + g + 1)
                    if single:
                        dve.tensor_copy(MX[:, k % 2, 0:cols], slot_view).then_inc(colmax_ready, 1)
                    else:
                        dve.tensor_reduce(MX[:, k % 2, 0:cols], slot_view.rearrange("p (t c) -> p c t", t=n), AX.X, ALU.max
                                          ).then_inc(colmax_ready, 1)

                def shift_rows(g, k, q):
                    dve.wait_ge(colmax_turned, UNITS * b + g + 1)
                    own.link(dve.tensor_reduce(NM[:, k % 2, 0:q], TB[:, 0:P * q].rearrange("p (q j) -> p q j", q=q),
                                               AX.X, ALU.max))
                    if g >= 2:
                        dve.wait_ge(scores_shifted, UNITS * b + g - 1)
                    dve.tensor_tensor(DG[:, k % 2, 0:q, :], w("negident").unsqueeze(1).broadcast_to([P, q, P]),
                                      NM[:, k % 2, 0:q].unsqueeze(2).broadcast_to([P, q, P]), ALU.mult
                                      ).then_inc(shift_ready, 1)

                def single_head():
                    dve.wait_ge(proj_a, 3 * b + 3)
                    dve.tensor_tensor(VA[:, :, 0:E], bank(2).rearrange("p (t e) -> p t e", t=NT),
                                      w("bv_a").unsqueeze(1).broadcast_to([P, NT, E]), ALU.add).then_inc(v_a, 1)
                    for k in range(NT + 4):
                        if k < NT:
                            colmax(k, k, SB[:, k % 3, 0:P * (k + 1)], k + 1, P, k == 0)
                        if 1 <= k <= NT:
                            shift_rows(k - 1, k - 1, 1)
                        if k >= 4:
                            u = k - 4
                            dve.wait_ge(out_a, NT * b + u + 1)
                            o = OB if u % 2 == 0 else bank(5)
                            own.link(dve.reciprocal(arec[:, u:u + 1], o[:, E:E + 1]))
                            dve.scalar_tensor_tensor(out=X[:, u, :], in0=o[:, 0:E], scalar=arec[:, u:u + 1],
                                                     in1=xin[:, u, :], op0=ALU.mult, op1=ALU.add).then_inc(out_a_used, 1)
                    dve.wait_ge(out_a_used, NT * b + NT)
                    dve.tensor_copy(fence[:, :], w("ident")[:, 0:1]).then_inc(xin_free, 1)

                def multi_head(a):
                    d = DHEAD[a]
                    rows = d * H
                    first = NT + NU * a
                    dve.wait_ge(q_high, MHAS * b + a + 1)
                    own.done(dve.tensor_tensor(Qrest[0:rows, :], QF[0:rows, :], Q3[0:rows, 0, :], ALU.subtract))
                    dve.tensor_tensor(Q3[0:rows, 1, :], QF[0:rows, :], Q3[0:rows, 0, :], ALU.subtract
                                      ).then_inc(q_rest, 1)
                    own.settle()
                    dve.wait_ge(q_rest, 2 * MHAS * b + 2 * a + 1)
                    dve.tensor_tensor(Q3[0:rows, 2, :], Qrest[0:rows, :], Q3[0:rows, 1, :], ALU.subtract
                                      ).then_inc(q_rest, 1)
                    dve.wait_ge(proj, 3 * MHAS * b + 3 * a + 1)
                    vsrc = bank(2)[:, 0:NT * rows].rearrange("p (t h d) -> p t h d", t=NT, h=H)
                    if a == FULL:
                        dve.tensor_copy(VO[:, :, :, 0:d], vsrc).then_inc(v_ready, 1)
                    else:
                        bv = w(f"bv{a}").rearrange("p (h d) -> p h d", h=H).unsqueeze(1).broadcast_to([P, NT, H, d])
                        dve.tensor_tensor(VO[:, :, :, 0:d], vsrc, bv, ALU.add).then_inc(v_ready, 1)

                    def make_hot(h):
                        dve.wait_ge(q_spread, H * b + h + 1)
                        dve.scalar_tensor_tensor(out=QH[:, (h // HPG) % 2, h % HPG, :], in0=OB[:, :],
                                                 scalar=w("bqr0")[:, h:h + 1], in1=w("onehot"), op0=ALU.add, op1=ALU.mult
                                                 ).then_inc(q_hot, 1)

                    if a == POS:
                        for h in range(HPG):
                            make_hot(h)
                    for k in range(NU + 5):
                        hg, r = divmod(k, NIB)
                        if k < NU:
                            lo, hi = slots_of(a, r)
                            colmax(first + k, k, SB[:, k % 3, 256 * lo:256 * hi], hi - lo, HPG * IB, hi - lo == 1)
                        if 1 <= k <= NU:
                            shift_rows(first + k - 1, k - 1, 2)
                        if a == POS and r in (0, 1, 2, 6) and hg + 1 < HG:
                            make_hot(HPG * (hg + 1) + (0, 1, 2, 6).index(r))
                        if r == 4 and hg >= 1:
                            g = HG * MHAS * b + HG * a + hg
                            dve.wait_ge(den_ready, g)
                            dve.reciprocal(REC[:, :], OB[:, :]).then_inc(den_used, 1)
                            dve.wait_ge(den_used, g)
                            dve.tensor_tensor(AT[:, hg - 1, :], OS[:, :], REC[:, :], ALU.mult).then_inc(head_out, 1)

                def bit_ffn(f):
                    for t in range(FT):
                        n = FT * (2 * b + f) + t + 1
                        dve.wait_ge(relued, n)
                        dve.tensor_tensor(R2[:, t, :], RL[:, t, :], RL[:, t, :], ALU.mult).then_inc(squared, 1)

                def routed_ffn(f):
                    r = 2 * b + f
                    for n in range(NA):
                        dve.wait_ge(decoded, NA * r + n + 1)
                        if n >= 2:
                            dve.wait_ge(loss_part, NA * r + n - 1)
                        dve.scalar_tensor_tensor(out=DF[:, n % 2, :], in0=bank(2 + n % 3), scalar=w("b_dec")[:, n:n + 1],
                                                 in1=xnT[:, :], op0=ALU.add, op1=ALU.subtract).then_inc(diff_ready, 1)
                    loss, least, later, first_, hot, pick, cid, hot2 = (ch[:, i, :] for i in range(8))
                    dve.wait_ge(loss_ready, r + 1)
                    own.link(dve.tensor_copy(loss, TB[:, 0:NA]))
                    own.link(dve.tensor_reduce(least[:, 0:1], loss, AX.X, ALU.min))
                    own.link(dve.tensor_scalar(later, loss, least[:, 0:1], float(2 * NA), ALU.is_gt, ALU.mult))
                    own.link(dve.tensor_tensor(pick, later, w("iota"), ALU.add))
                    own.link(dve.tensor_reduce(first_[:, 0:1], pick, AX.X, ALU.min))
                    own.link(dve.tensor_scalar(hot, w("iota"), first_[:, 0:1], None, ALU.is_equal))
                    own.link(dve.tensor_tensor(pick, hot, cidx_f[:, :], ALU.mult))
                    own.link(dve.tensor_reduce(cid[:, 0:1], pick, AX.X, ALU.add))
                    own.link(dve.tensor_scalar(hot2, w("iota"), cid[:, 0:1], None, ALU.is_equal))
                    packs = w("pack").rearrange("p (n c) -> p n c", n=NA)
                    own.link(dve.tensor_scalar(SEL[:, 0, :], packs[:, 0, :], hot2[:, 0:1], None, ALU.mult))
                    for n in range(1, NA):
                        ins = dve.scalar_tensor_tensor(out=SEL[:, n % 2, :], in0=packs[:, n, :], scalar=hot2[:, n:n + 1],
                                                       in1=SEL[:, (n - 1) % 2, :], op0=ALU.mult, op1=ALU.add)
                        if n < NA - 1:
                            own.link(ins)
                    ins.then_inc(adapter_ready, 1)

                dve.wait_ge(x_loaded, 16 * b + 16)
                layer_norm(0, xin)
                single_head()
                layer_norm(1, X)
                bit_ffn(0)
                own.link(add_bank(0, 4, X))
                layer_norm(2, X)
                multi_head(POS)
                own.link(add_bank(1, 0, X))
                layer_norm(3, X)
                bit_ffn(1)
                own.link(add_bank(2, 4, X))
                layer_norm(4, X)
                multi_head(FULL)
                own.link(add_bank(3, 0, X))
                layer_norm(5, X)
                routed_ffn(0)
                own.link(add_bank(4, 1, X))
                layer_norm(6, X)
                multi_head(WINDOW)
                own.link(add_bank(5, 0, X))
                layer_norm(7, X)
                routed_ffn(1)
                dve.wait_ge(stored, 16 * b + 16)
                add_bank(6, 1, xout).then_inc(xout_ready, 1)
                assert own.n == DVE_STEPS, own.n


def layout(i):
    import numpy as np

    f = np.float32
    s = {}
    r = np.arange(P)
    s["ident"] = np.eye(P, dtype=f)
    s["negident"] = -np.eye(P, dtype=f)
    s["keep1"] = np.where(r[:, None] <= r[None, :], 0, NEG).astype(f)
    s["keep0"] = np.where(r[:, None] >= r[None, :], 0, NEG).astype(f)
    s["onehot"] = ((np.arange(T)[None, :] // TAPS) % 16 == r[:, None] // 8).astype(f)
    s["spread"] = ((r[:, None] % 32 == 8) & (r[:, None] // 32 == r[None, :] // 32)).astype(f)
    s["iota"] = np.broadcast_to(np.arange(NA, dtype=f), (P, NA))
    rep = lambda v: np.broadcast_to(v, (P,) + v.shape[-1:])
    s["gate"] = rep(i["L0_ffn_gate"].reshape(1, 1))
    s["w_fc"] = i["L0_ffn_w_fc"].reshape(FT, P, E).transpose(1, 0, 2).reshape(P, FT * E)
    s["w_proj"] = i["L0_ffn_w_proj"]
    s["fast_b"], s["uT"], s["v"] = i["L0_ffn_fast_b"], i["L0_ffn_u"].T, i["L0_ffn_v"]
    for n in "qk":
        s[f"w{n}_a"] = i[f"L0_attn_a_W{n}"].T
        s[f"b{n}_a"] = i[f"L0_attn_a_b{n}"][:, None]
    s["wv_a"], s["bv_a"] = i["L0_attn_a_Wv"].T, rep(i["L0_attn_a_bv"])
    s["relT"] = i["L0_attn_b_rel_table"][::-1].T
    w_in, b_in = i["L1_attn_b_w_in"], i["L1_attn_b_b_in"]
    heads = (
        [i[f"L0_attn_b_W{n}"] for n in "qkv"] + [i[f"L0_attn_b_b{n}"] for n in "qkv"] + [i["L0_attn_b_Wo"], i["L0_attn_b_bo"]],
        [i[f"L1_attn_a_W{n}"] for n in "qkv"] + [None] * 3 + [i["L1_attn_a_Wo"], i["L1_attn_a_bo"]],
        [w_in[E * n:E * n + E] for n in range(3)] + [b_in[E * n:E * n + E] for n in range(3)]
        + [i["L1_attn_b_w_out"], i["L1_attn_b_b_out"]],
    )
    for a, (wq, wk, wv, bq, bk, bv, wo, bo) in enumerate(heads):
        d = DHEAD[a]
        for n, m in (("q", wq), ("k", wk)):
            s[f"w{n}{a}"] = m.reshape(H, d, -1).transpose(2, 1, 0).reshape(-1, d * H)
        s[f"wv{a}"] = wv.T
        if bq is not None:
            for n, m in (("q", bq), ("k", bk)):
                s[f"b{n}{a}"] = m.reshape(H, d).T.reshape(-1, 1)
            s[f"bv{a}"] = rep(bv)
        padded = np.zeros((HPG, 32, HG, E), f)
        padded[:, 0:d] = wo.T.reshape(HG, HPG, d, E).transpose(1, 2, 0, 3)
        padded[0, 8, 0] = bo
        s[f"wo{a}"] = padded.reshape(P, HG * E)
    s["wqn0"] = heads[0][0].T
    s["bqr0"] = np.tile(heads[0][3].reshape(H, 8).T, (16, 1))
    s["enc"] = i["L1_ffn_W_enc"].transpose(1, 0, 2).reshape(E, NA * AH)
    s["b_enc"] = i["L1_ffn_b_enc"].reshape(2, P).T
    dec = np.zeros((P, NA, E), f)
    for n in range(NA):
        dec[AH * (n % 4):AH * (n % 4) + AH, n] = i["L1_ffn_W_dec"][n]
    s["dec"], s["b_dec"] = dec.reshape(P, NA * E), i["L1_ffn_b_dec"].T
    pack = np.zeros((P, NA, PACK), f)
    pack[:, :, 0:AR] = i["L1_ffn_W_down"].transpose(1, 0, 2)
    pack[0:AR, :, AR:AR + E] = i["L1_ffn_W_up"].transpose(1, 0, 2)
    pack[AR, :, AR:AR + E] = i["L1_ffn_b_up"]
    pack[AR + 1, :, AR:AR + E] = i["L1_ffn_b_base"]
    pack[0:AR, :, PACK - 1] = i["L1_ffn_b_down"].T
    s["pack"] = pack.reshape(P, NA * PACK)
    s["w_base"] = i["L1_ffn_W_base"]
    packed = np.zeros((P, WCOLS + PREP_COLS), f)
    for name, cols in SECTIONS + PREP_SECTIONS:
        v = s[name]
        assert v.shape[1] == cols, (name, v.shape)
        packed[0:v.shape[0], OFF[name][0]:OFF[name][0] + cols] = v
    return packed


def kernel(**inputs):
    import numpy as np
    import concourse.bacc as bacc
    from concourse.bass_utils import run_bass_kernel_spmd

    i = {k: np.asarray(v) for k, v in inputs.items()}
    arrays = {
        "x_dram": np.ascontiguousarray(i["L0_attn_a_x"]),
        "packed_dram": layout(i),
        "cidx_dram": np.ascontiguousarray(np.broadcast_to(i["L1_ffn_connected_idx"], (P, NA))),
    }
    nc = bacc.Bacc("TRN2", target_bir_lowering=False, num_devices=1)
    args = [nc.dram_tensor(n, a.shape, mybir.dt.from_np(a.dtype), kind="ExternalInput").ap() for n, a in arrays.items()]
    args.append(nc.dram_tensor("out_dram", (B, T, E), F32, kind="ExternalOutput").ap())
    build(nc, *args)
    r = run_bass_kernel_spmd(nc, [arrays], core_ids=[0])
    return r.results[0]["out_dram"]
```

```python
from contextlib import ExitStack

import concourse.bass as bass
from concourse import mybir

ALU = mybir.AluOpType
ACT = mybir.ActivationFunctionType
AX = mybir.AxisListType
F32 = mybir.dt.float32
BF16 = mybir.dt.bfloat16
I32 = mybir.dt.int32

P = 128
B, T, E = 8, 512, 128
NT = T // P
H = 16
HG, HPG = 4, 4
HT = T // 2
QU = 4
NU = HG * 2 * QU
COLS = HPG * HT // QU
POS, FULL, WINDOW = 0, 1, 2
DHEAD = (8, 4, 8)
A_UNITS = (((0, 0, 1), (1, 1, 2)), ((2, 0, 3),), ((3, 0, 4),))
RING = 3
HID = 512
FT = HID // P
RANK = 16
NA, AH, AR = 8, 32, 64
MAXLEN = 128
NREL = 2 * MAXLEN - 1
IB = 64
TAPS = 4
DELTAS = (192, 128, 64, 0, -64, -128)
RTL = 512
RWC = DELTAS[0] + TAPS - 1 + P + MAXLEN
ROWS = 64
SLOTS_Q = (0, 1, 2, 0, 1, 0)
SLOTS_K = (0, 0, 0, 1, 1, 2)
VC = 16
PREP_AT = 0
NEG = -1e30
EPS = 1e-5
PACK = AR + E + 1

PREP_SECTIONS = (
    ("gate", 1), ("w_fc", FT * P), ("w_proj", HID), ("fast_b", RANK), ("uT", HID), ("v", P), ("relT", NREL),
    ("keep1", P), ("keep0", P),
)
SECTIONS = (
    ("ident", P), ("negident", P), ("wq_a", E), ("wk_a", E), ("wv_a", E), ("bq_a", 1), ("bk_a", 1), ("bv_a", E),
    ("onehot", IB),
    ("wq0", E), ("wk0", E), ("wv0", E), ("wqn0", E), ("bq0", 1), ("bk0", 1), ("bv0", E), ("bqr0", H), ("wo0", E), ("bo0", E),
    ("wq1", E), ("wk1", E), ("wv1", 64), ("wo1", E), ("bo1", E),
    ("enc", NA * AH), ("b_enc", 2), ("dec", NA * E), ("b_dec", NA), ("pack", NA * PACK), ("w_base", E), ("iota", NA),
    ("wq2", E), ("wk2", E), ("wv2", E), ("bq2", 1), ("bk2", 1), ("bv2", E), ("wo2", E), ("bo2", E),
)
OFF = {}
WCOLS = 0
for _name, _cols in SECTIONS:
    OFF[_name] = (WCOLS, _cols)
    WCOLS += _cols
PREP_COLS = 0
for _name, _cols in PREP_SECTIONS:
    OFF[_name] = (WCOLS + PREP_COLS, _cols)
    PREP_COLS += _cols


MISC = frozenset(("turnx", "a_v", "a_q", "a_k", "a_out", "proj_v", "proj_q", "proj_k", "spread", "weigh", "renorm", "unturn",
                  "outproj", "hidden", "ffn_out", "enc", "dec", "total", "down", "up"))
DVE_LINKS = {"norm_a": NT, "norm_b": NT, "norm_c": 3, "a_out": 1, "renorm": 1, "bias": 1, "pick": 1, "select": 1}
POOL_LINKS = {"norm_d": 13, "split": 2}


class Event:
    def __init__(self, kind, args, counts):
        self.kind, self.args, self.c = kind, args, counts


class Section:

    def __init__(self, base, trips=1):
        self.base, self.trips, self.c, self.events, self.marks = dict(base), trips, {}, [], {}

    def add(self, kind, *args):
        c = self.c
        for k, n in ((kind, 1), ("misc", int(kind in MISC)), ("dve", DVE_LINKS.get(kind, 0)),
                     ("pool", POOL_LINKS.get(kind, 0))):
            if n:
                c[k] = c.get(k, 0) + n
        self.events.append(Event(kind, args, dict(c)))

    def after(self):
        return {k: self.base.get(k, 0) + self.trips * self.c.get(k, 0) for k in set(self.base) | set(self.c)}


def head_events(b):
    ffn = [("norm_a", "xa"), ("norm_b",), ("norm_c",), ("norm_d", "xa"), ("turnx", "xnT")]
    ffn += [("hidden", t) for t in range(FT)] + [("ffn_out", "xa")]
    norm = [("norm_a", "xa"), ("norm_b",), ("norm_c",), ("norm_d", "xa"), ("turnx", "xnT0")]
    first = [("load", b), ("norm_a", "xin"), ("norm_b",), ("norm_c",), ("norm_d", "xin"), ("turnx", "xnT"),
             ("a_v",), ("a_q",), ("a_k",)]
    return first, ffn + norm + proj_events(POS) + [("repeat", 0), ("spread", 0, 0), ("spread", 0, 1)]


def proj_events(a):
    return [("proj_q", a), ("proj_k", a), ("split", a), ("proj_v", a)]


def out_events(a, src, dst):
    return [("bias", a, src, dst), ("unturn", a), ("outproj", a, dst)]


def routed_events(x):
    ev = [("norm_a", x), ("norm_b",), ("norm_c",), ("norm_d", x), ("turnx", "xnT")]
    ev += [("enc", 0), ("enc", 1)] + [("dec", n) for n in range(NA)] + [("total",)]
    ev += [("pick", n) for n in range(1, 9)] + [("select", n) for n in range(NA - 1)] + [("selected",), ("down",), ("up", x)]
    return ev


def mid1_events():
    ev = out_events(POS, "xa", "xb") + [("norm_a", "xb"), ("norm_b",), ("norm_c",), ("norm_d", "xb"), ("turnx", "xnT")]
    ev += [("hidden", t) for t in range(FT)] + [("ffn_out", "xb")]
    return ev + [("norm_a", "xb"), ("norm_b",), ("norm_c",), ("norm_d", "xb"), ("turnx", "xnT")] + proj_events(FULL)


def mid2_events():
    ev = out_events(FULL, "xb", "xc") + routed_events("xc")
    return ev + [("norm_a", "xc"), ("norm_b",), ("norm_c",), ("norm_d", "xc"), ("turnx", "xnT")] + proj_events(WINDOW)


def tail_events(b):
    return out_events(WINDOW, "xc", "xout") + routed_events("xout") + [("store", b)]


def pipeline(sec, units, light, at=None):
    steps = len(units) + 4 if units else 0
    due = {}
    for lo, hi, events in light:
        n = len(events)
        for m, e in enumerate(events):
            due.setdefault(lo + (m * (hi - lo)) // max(n, 1), []).append(e)
    last = max([steps - 1] + list(due))
    marks = sec.marks
    for k in range(last + 1):
        if k < len(units):
            u = units[k]
            need = 0
            if u[0] == "a":
                need = marks["a_k"]
            elif u[1] == POS and u[2] % QU == 0:
                need = marks["spread", u[2] // QU]
            sec.add("scores", *u, need)
        if 1 <= k <= len(units):
            sec.add("turn", *units[k - 1])
        if 2 <= k < len(units) + 2:
            sec.add("shift", *units[k - 2])
            marks[units[k - 2]] = sec.c["shift"]
        heavy = []
        if 0 <= k - 3 < len(units) and units[k - 3][0] == "mha":
            _, a, u = units[k - 3]
            hg, r = divmod(u, 2 * QU)
            half = u // QU
            if u % QU == QU - 1:
                heavy.append(("weigh", a, half, marks[units[k - 3]]))
        if 0 <= k - 4 < len(units) and units[k - 4][0] == "mha":
            _, a, u = units[k - 4]
            if u % (2 * QU) == 2 * QU - 1:
                heavy.append(("renorm", a, u // (2 * QU)))
        if k < len(units) and units[k][0] == "mha" and units[k][1] == POS:
            u = units[k][2]
            nxt = u // QU + 1
            if nxt < 2 * HG and u % QU in (1, 2):
                heavy.append(("spread", nxt, u % QU - 1))
                if u % QU == 2 and nxt % 2 == 1 and nxt + 1 < 2 * HG:
                    heavy.append(("repeat", nxt // 2 + 1))
        for e in heavy:
            add_light(sec, e)
        for e in due.get(k, []):
            add_light(sec, e)


def add_light(sec, e):
    if e[0] == "norm_a":
        e = e + (sec.marks.get("x", 0),)
    if e[0] == "a_out":
        e = e + (sec.marks[("a", next(i for i, segs in enumerate(A_UNITS) for s in segs if s[0] == e[1]))],)
    if e[0] == "store":
        e = e + (sec.marks["x"],)
    if e[0] in ("split", "pick"):
        e = e + (sec.marks["proj_k" if e[0] == "split" else "total"],)
    sec.add(*e)
    if e[0] in ("a_out", "outproj", "ffn_out", "up"):
        sec.marks["x"] = sec.c["misc"]
    if e[0] in ("a_k", "proj_k", "total"):
        sec.marks[e[0]] = sec.c["misc"]
    if e[0] == "spread":
        sec.marks["spread", e[1]] = sec.c["misc"]


def plan():
    mha = [[("mha", a, u) for u in range(NU)] for a in range(3)]
    single = [("a", i) for i in range(len(A_UNITS))]
    outs = [("a_out", t) for t in range(NT)]

    def iteration(sec, tail, head, nxt):
        light = []
        units = list(mha[FULL])
        if head is not None:
            first, rest = head_events(head)
            units = units[:12] + single + units[12:]
            light = [(0, 10, first), (15, 17, outs), (17, 37, rest)]
        pipeline(sec, units, light)
        light = ([(0, 12, tail_events(tail))] if tail is not None else [])
        m2 = [(13 if tail is not None else 0, 31, mid2_events())]
        pipeline(sec, mha[POS] if nxt else [], light + m2)
        pipeline(sec, mha[WINDOW], [(0, 31, mid1_events())] if nxt else [])

    sections = []
    sec = Section({})
    first, rest = head_events(0)
    for e in first:
        add_light(sec, e)
    pipeline(sec, single, [(5, 6, outs), (7, 8, rest)])
    pipeline(sec, mha[POS], [])
    for e in mid1_events():
        add_light(sec, e)
    iteration(sec, None, 1, True)
    sections.append(sec)
    sec = Section(sec.after(), trips=B - 2)
    iteration(sec, 0, 2, True)
    sections.append(sec)
    sec = Section(sec.after())
    iteration(sec, B - 2, None, False)
    for e in tail_events(B - 1):
        add_light(sec, e)
    sections.append(sec)
    return sections


def build(nc: bass.Bass, x: bass.AP, packed: bass.AP, cidx: bass.AP, out: bass.AP):
    relpad = nc.dram_tensor("relpad_scratch", (8, RTL), F32, kind="Internal").ap()
    sections = plan()
    with ExitStack() as ctx:
        def sb(name, shape, dt=F32):
            return ctx.enter_context(nc.sbuf_tensor(name, shape, dt))

        def sem(name):
            return ctx.enter_context(nc.semaphore(name))

        W = sb("W", [P, WCOLS])
        PT = sb("PT", [P, 2, NT * HPG * HT])
        PREP = PT[:, :, :].rearrange("p u n -> p (u n)")[:, 0:PREP_COLS]
        TERN = PT[:, :, :].rearrange("p u n -> p (u n)")[:, PREP_COLS:PREP_COLS + 5 * HID].rearrange(
            "p (n i) -> p n i", n=5)
        relrow = PT[:, :, :].rearrange("p u n -> p (u n)")[0:8, PREP_COLS + 5 * HID:PREP_COLS + 5 * HID + RTL]

        def w(name, rows=P):
            o, n = OFF[name]
            return W[0:rows, o:o + n] if o < WCOLS else PREP[0:rows, o - WCOLS:o - WCOLS + n]

        ident_b = sb("ident_b", [P, P], BF16)
        ones_b = sb("ones_b", [P, P], BF16)
        ones_f = sb("ones_f", [P, P])
        masks = sb("masks", [P, 2, P], BF16)
        zero_col = sb("zero_col", [P, 1])
        three_halves = sb("three_halves", [P, NT])
        cidx_i = sb("cidx_i", [P, NA], I32)
        cidx_f = sb("cidx_f", [P, NA])
        wrap = sb("wrap", [P, NA])
        Wfc = sb("Wfc", [P, HID])
        Wpr = sb("Wpr", [P, FT, E])
        relwin = sb("relwin", [P, RWC])
        relparts = sb("relparts", [8, 3, 2], BF16)
        relrest = sb("relrest", [8, 2])
        relclip_c = sb("relclip_c", [ROWS, 2], BF16)
        relclip = sb("relclip", [ROWS, 2, P], BF16)

        X = {n: sb(n, [P, NT, E]) for n in ("xin", "xa", "xb", "xc", "xout")}
        stats = sb("stats", [P, NT, 6])
        mv = sb("mv", [P, NT, 2])
        fence = sb("fence", [P, 1])
        var = sb("var", [P, NT])
        nhvar = sb("nhvar", [P, NT])
        rs = [sb(f"rs{i}", [P, NT]) for i in range(2)]
        nt = [sb(f"nt{i}", [P, NT]) for i in range(3)]
        xn = sb("xn", [P, NT, E])
        xnT = {"xnT": sb("xnT", [E, T]), "xnT0": sb("xnT0", [E, T])}

        QF = sb("QF", [P, T])
        KF = sb("KF", [P, T])
        Q3 = sb("Q3", [P, 3, T], BF16)
        K3 = sb("K3", [P, 3, T], BF16)
        VA = sb("VA", [P, NT, E + 2])
        QOs = [sb(f"QO{i}", [P, H, T], BF16) for i in range(2)]
        KOs = [sb(f"KO{i}", [P, H, T], BF16) for i in range(2)]
        VO = [sb(f"VO{a}", [P, NT, H, VC]) for a in range(3)]
        WR = sb("WR", [P, HPG, 16, 8])
        QH = sb("QH", [P, 2, HPG, HT])
        MX = sb("MX", [P, RING, COLS])
        NM = sb("NM", [P, RING, 2])
        DG = sb("DG", [P, RING, 2, P], BF16)
        OS = sb("OS", [P, T])
        rec = sb("rec", [P, NT, HPG])
        AN = [sb(f"AN{a}", [P, NT, E]) for a in range(3)]
        ATT = sb("ATT", [E, T])
        Qrest, Krest = ATT, xn[:, :, :].rearrange("p t e -> p (t e)")
        arec = sb("arec", [P, 1])
        HB = sb("HB", [P, FT, T])
        EH, DF = HB[:, 0:2, :], HB[:, 2:4, :]
        PTA = HB[:, 0:len(A_UNITS), :]
        sq = sb("sq", [P, T], BF16)
        MID = sb("MID", [P, T])
        SEL = sb("SEL", [P, 2, PACK])
        LP = sb("LP", [P, NA])
        ch = sb("ch", [P, 8, NA])

        SB = ctx.enter_context(nc.psum_tensor("SB", [P, RING, 1024], F32))
        TB = ctx.enter_context(nc.psum_tensor("TB", [P, 512], F32))
        MB = ctx.enter_context(nc.psum_tensor("MB", [P, 512], F32))

        w_loaded = sem("w_loaded")
        prep_pe = sem("prep_pe")
        prep_dve = sem("prep_dve")
        prep_pool = sem("prep_pool")
        prep_step = sem("prep_step")
        prep_pool_step = sem("prep_pool_step")
        rel_loaded = sem("rel_loaded")
        clip_loaded = sem("clip_loaded")
        x_loaded = sem("x_loaded")
        stored = sem("stored")
        dve_step = sem("dve_step")
        pool_step = sem("pool_step")
        misc_filled = sem("misc_filled")
        misc_read = sem("misc_read")
        scores_ready = sem("scores_ready")
        colmax_ready = sem("colmax_ready")
        colmax_turned = sem("colmax_turned")
        rowmax_ready = sem("rowmax_ready")
        shift_ready = sem("shift_ready")
        scores_shifted = sem("scores_shifted")
        probs_ready = sem("probs_ready")
        seeded = sem("seeded")
        normed = sem("normed")
        parts_ready = sem("parts_ready")
        operands_in = sem("operands_in")
        wq_repeated = sem("wq_repeated")
        squared = sem("squared")
        loss_part = sem("loss_part")
        adapter_ready = sem("adapter_ready")

        class Walk:

            def __init__(self, sec, trip):
                self.sec, self.trip = sec, trip

            def n(self, ev, kind, back=0, times=1, before=0):
                return self.upto(ev.c.get(kind, 0) - back, kind, times, before)

            def upto(self, local, kind, times=1, before=0):
                v = (self.sec.base.get(kind, 0) + local) * times + before
                if self.trip is None:
                    return v
                assert v > 0, kind
                return self.trip * (self.sec.c[kind] * times) + v

            def ring(self, ev, kind, size):
                assert self.trip is None or self.sec.c[kind] % size == 0, (kind, self.sec.c[kind])
                return (self.sec.base.get(kind, 0) + ev.c[kind] - 1) % size

            def batch(self, b):
                return b if self.trip is None else self.trip + b

        def walk(eng, handlers):
            for sec in sections:
                if sec.trips == 1:
                    go = Walk(sec, None)
                    for ev in sec.events:
                        if ev.kind in handlers:
                            handlers[ev.kind](go, ev, *ev.args)
                else:
                    with eng.Fori(0, sec.trips) as trip:
                        go = Walk(sec, trip)
                        for ev in sec.events:
                            if ev.kind in handlers:
                                handlers[ev.kind](go, ev, *ev.args)

        def wait(eng, semaphore, value):
            if not isinstance(value, int) or value > 0:
                eng.wait_ge(semaphore, value)

        def unit(a, u):
            hg, hf, q = u // (2 * QU), u // QU % 2, u % QU
            if a == POS:
                h0, nh, i0, ni = HPG * hg, HPG, HT * hf + IB * q, IB
            elif a == FULL:
                h0, nh, i0, ni = HPG * hg + q, 1, HT * hf, HT
            else:
                h0, nh, i0, ni = HPG * hg + 2 * (q // 2), 2, HT * hf + P * (q % 2), P
            if a == WINDOW:
                t = i0 // P
                return h0, nh, i0, ni, {s: t - 1 + s for s in range(2) if t - 1 + s >= 0}
            return h0, nh, i0, ni, {s: s for s in range(NT)}

        def slot(r, nh=1):
            return SB[:, r, :].rearrange("p (t h i) -> p t h i", t=NT, h=nh)

        def pt(half):
            return PT[:, half % 2, :].rearrange("p (t h i) -> p t h i", t=NT, h=HPG)

        def operand(a, tensors):
            r0 = ROWS if a == FULL else 0
            return tensors[1 if a == WINDOW else 0], r0

        block = ctx.enter_context(nc.Block())

        @block.sync
        def _(sp):
            cuts = [0, OFF["onehot"][0], OFF["enc"][0], WCOLS]
            sp.dma_start(cidx_i[:, :], cidx).then_inc(w_loaded, 16)
            sp.dma_start(PREP, packed[:, WCOLS:]).then_inc(w_loaded, 16)
            for n in range(3):
                sp.dma_start(W[:, cuts[n]:cuts[n + 1]], packed[:, cuts[n]:cuts[n + 1]]).then_inc(w_loaded, 16)
            sp.wait_ge(prep_pool, 1)
            sp.dma_start(relpad, relrow).then_inc(stored, 16)
            sp.wait_ge(stored, 16)
            for a in range(16):
                y0 = 15 * TAPS - TAPS * a
                sp.dma_start(relwin[8 * a:8 * a + 8, :], relpad[:, y0:y0 + RWC]).then_inc(rel_loaded, 16)
            sp.wait_ge(prep_pool, 2)
            for s, part in enumerate(SLOTS_K):
                sp.dma_start(relclip_c[8 * s:8 * s + 8, :], relparts[:, part, :]).then_inc(clip_loaded, 16)

            def rows_of(ap):
                return ap.rearrange("o (t p) e -> p (o t) e", p=P)

            def load(go, ev, b):
                wait(sp, misc_read, go.n(ev, "misc"))
                src = x[b:b + 1] if go.trip is None else x[bass.ds(go.batch(b), 1), :, :]
                sp.dma_start(X["xin"][:, :, :], rows_of(src)).then_inc(x_loaded, 16)

            def place(a, part, slots, tensors, src):
                dst, r0 = operand(a, tensors)
                d = DHEAD[a]
                for s in range(6):
                    if slots[s] == part:
                        r = r0 + d * s
                        sp.dma_start(dst[r:r + d, :, :], src[0:d * H, part, :]).then_inc(operands_in, 16)

            def proj_q(go, ev, a):
                wait(sp, misc_read, go.n(ev, "misc"))
                place(a, 0, SLOTS_Q, QOs, Q3)

            def proj_k(go, ev, a):
                wait(sp, misc_read, go.n(ev, "misc"))
                place(a, 0, SLOTS_K, KOs, K3)

            def split(go, ev, a, mark):
                wait(sp, parts_ready, go.n(ev, "split", times=4) - 2)
                place(a, 1, SLOTS_Q, QOs, Q3)
                place(a, 1, SLOTS_K, KOs, K3)
                wait(sp, parts_ready, go.n(ev, "split", times=4))
                place(a, 2, SLOTS_Q, QOs, Q3)
                place(a, 2, SLOTS_K, KOs, K3)

            def store(go, ev, b, mark):
                wait(sp, misc_read, go.upto(mark, "misc"))
                dst = out[b:b + 1] if go.trip is None else out[bass.ds(go.batch(b), 1), :, :]
                sp.dma_start(rows_of(dst), X["xout"][:, :, :]).then_inc(stored, 16)

            walk(sp, {"load": load, "proj_q": proj_q, "proj_k": proj_k, "split": split, "store": store})
            sp.wait_ge(stored, 16 * B + 16)

        @block.gpsimd
        def _(pool):
            pool.memset(ones_b[:, :], 1.0)
            pool.memset(ones_f[:, :], 1.0)
            pool.memset(zero_col[:, :], 0.0)
            pool.memset(three_halves[:, :], 1.5)
            for t in QOs + KOs:
                pool.memset(t[:, :, :], 0.0)
            for v in VO:
                pool.memset(v[:, :, :, :], 0.0)
            pool.memset(VA[:, :, :], 1.0)
            pool.memset(MID[:, :], 1.0)
            pool.memset(AN[FULL][:, :, :], 0.0)
            pool.memset(relclip_c[:, :], 0.0).then_inc(prep_pool_step, 1)
            pool.wait_ge(prep_pool_step, 1)
            for v in VO:
                pool.memset(v[:, :, :, 8:9], 1.0)
            pool.wait_ge(w_loaded, 16 * 5)
            rel = w("relT", 8)
            pool.tensor_copy(relrow[:, 0:MAXLEN], rel[:, 0:1].broadcast_to([8, MAXLEN]))
            pool.tensor_copy(relrow[:, MAXLEN:MAXLEN + NREL], rel)
            pool.tensor_copy(relrow[:, MAXLEN + NREL:RTL], rel[:, NREL - 1:NREL].broadcast_to([8, RTL - MAXLEN - NREL])
                             ).then_inc(prep_pool, 1)
            ends = rel[:, 0:NREL:NREL - 1]
            pool.tensor_copy(relparts[:, 0, :], ends).then_inc(prep_pool_step, 1)
            pool.wait_ge(prep_pool_step, 2)
            pool.tensor_tensor(relrest[:, :], ends, relparts[:, 0, :], ALU.subtract).then_inc(prep_pool_step, 1)
            pool.wait_ge(prep_pool_step, 3)
            pool.tensor_copy(relparts[:, 1, :], relrest[:, :]).then_inc(prep_pool_step, 1)
            pool.wait_ge(prep_pool_step, 4)
            pool.tensor_tensor(relparts[:, 2, :], relrest[:, :], relparts[:, 1, :], ALU.subtract
                               ).then_inc(prep_pool, 1)
            pool.wait_ge(clip_loaded, 16 * 6)
            pool.tensor_copy(relclip[:, :, :], relclip_c[:, :].unsqueeze(2).broadcast_to([ROWS, 2, P])
                             ).then_inc(prep_pool, 1)

            def link(go, ev, k, ins):
                ins.then_inc(pool_step, 1)
                pool.wait_ge(pool_step, go.n(ev, "pool", back=POOL_LINKS[ev.kind] - k))

            def turn(go, ev, what, *unit_):
                r = go.ring(ev, "turn", RING)
                q = len(A_UNITS[unit_[0]]) if what == "a" else 2
                pool.wait_ge(rowmax_ready, go.n(ev, "turn"))
                pool.tensor_tensor(DG[:, r, 0:q, :], w("negident").unsqueeze(1).broadcast_to([P, q, P]),
                                   NM[:, r, 0:q].unsqueeze(2).broadcast_to([P, q, P]), ALU.mult).then_inc(shift_ready, 1)

            def norm_d(go, ev, src):
                pool.wait_ge(seeded, go.n(ev, "norm_c"))
                pool.tensor_tensor(xn[:, :, :], X[src][:, :, :], mv[:, :, 0:1].broadcast_to([P, NT, E]), ALU.subtract
                                   ).then_inc(pool_step, 1)
                k = 1
                for it in range(3):
                    old, new = rs[(it + 1) % 2], rs[it % 2]
                    for dst, in0, in1, op in ((nt[0], old, old, ALU.mult), (nt[1], nt[0], nhvar, ALU.mult),
                                              (nt[2], nt[1], three_halves, ALU.add), (new, nt[2], old, ALU.mult)):
                        k += 1
                        link(go, ev, k, pool.tensor_tensor(dst[:, :], in0[:, :], in1[:, :], op))
                pool.tensor_tensor(xn[:, :, :], xn[:, :, :], rs[0][:, :].unsqueeze(2).broadcast_to([P, NT, E]), ALU.mult
                                   ).then_inc(normed, 1)

            def split(go, ev, a, mark):
                rows = DHEAD[a] * H
                q, k = slice(0, rows), slice(0, rows)
                pool.wait_ge(misc_read, go.upto(mark, "misc"))
                pool.tensor_tensor(Qrest[q, :], QF[q, :], Q3[q, 0, :], ALU.subtract).then_inc(pool_step, 1)
                pool.tensor_tensor(Q3[q, 1, :], QF[q, :], Q3[q, 0, :], ALU.subtract).then_inc(parts_ready, 1)
                pool.tensor_tensor(Krest[k, :], KF[k, :], K3[k, 0, :], ALU.subtract).then_inc(pool_step, 1)
                pool.tensor_tensor(K3[k, 1, :], KF[k, :], K3[k, 0, :], ALU.subtract).then_inc(parts_ready, 1)
                pool.wait_ge(pool_step, go.n(ev, "pool"))
                pool.wait_ge(parts_ready, go.n(ev, "split", times=4) - 2)
                pool.tensor_tensor(Q3[q, 2, :], Qrest[q, :], Q3[q, 1, :], ALU.subtract).then_inc(parts_ready, 1)
                pool.tensor_tensor(K3[k, 2, :], Krest[k, :], K3[k, 1, :], ALU.subtract).then_inc(parts_ready, 1)

            def repeat(go, ev, hg):
                pool.wait_ge(misc_filled, go.n(ev, "misc"))
                pool.tensor_tensor(
                    WR[:, :, :, :],
                    w("wqn0")[:, 32 * hg:32 * hg + 32].rearrange("p (h d) -> p h d", h=HPG).unsqueeze(2)
                    .broadcast_to([P, HPG, 16, 8]),
                    ones_f[:, :].rearrange("p (a d) -> p a d", a=16).unsqueeze(1).broadcast_to([P, HPG, 16, 8]),
                    ALU.mult).then_inc(wq_repeated, 1)

            def hidden(go, ev, t):
                pool.wait_ge(misc_read, go.n(ev, "misc"))
                pool.tensor_tensor(HB[:, t, :], HB[:, t, :], HB[:, t, :], ALU.mult).then_inc(squared, 1)

            walk(pool, {"turn": turn, "norm_d": norm_d, "split": split, "repeat": repeat, "hidden": hidden})

        @block.tensor
        def _(pe):
            idf = w("ident")
            pe.wait_ge(prep_dve, 1)
            for t in range(FT):
                ins = pe.transpose(SB[:, 0, P * t:P * t + P], TERN[:, 0, P * t:P * t + P], idf)
            ins.then_inc(prep_pe, 1)
            pe.wait_ge(prep_dve, 2)
            for t in range(FT):
                ins = pe.transpose(SB[:, 1, P * t:P * t + P], TERN[:, 1, P * t:P * t + P], idf)
            ins.then_inc(prep_pe, 1)
            pe.matmul(SB[0:RANK, 2, 0:HID], w("fast_b", RANK), w("uT", RANK), start=True, stop=True).then_inc(prep_pe, 1)
            pe.wait_ge(prep_dve, 3)
            pe.matmul(SB[:, 2, 512:1024], w("v", RANK), TERN[0:RANK, 2, :], start=True, stop=True).then_inc(prep_pe, 1)
            pe.wait_ge(prep_dve, 4)
            pe.wait_ge(prep_pool, 3)
            pe.wait_ge(rel_loaded, 16 * 16)
            pe.matmul(MB[:, :], ident_b[:, :], QOs[0][:, 0, :], start=True, stop=True)

            def take(go, ev):
                wait(pe, misc_read, go.n(ev, "misc", back=1))

            def scores(go, ev, what, *args):
                r = go.ring(ev, "scores", RING)
                wait(pe, probs_ready, go.n(ev, "scores", back=RING))
                if args[-1]:
                    wait(pe, misc_read, go.upto(args[-1], "misc"))
                if what == "a":
                    first = True
                    for it, c0, n in A_UNITS[args[0]]:
                        for j in range(n):
                            pe.matmul(SB[:, r, P * (c0 + j):P * (c0 + j) + P], KF[:, P * j:P * j + P],
                                      QF[:, P * it:P * it + P], start=first, stop=False, skip_group_check=True)
                            first = False
                        c = P * (c0 + n - 1)
                        ins = pe.matmul(SB[:, r, c:c + P], ident_b[:, :], masks[:, 1, :], start=False, stop=False,
                                        skip_group_check=True)
                    ins.then_inc(scores_ready, 1)
                    return
                a, u = args[0:2]
                h0, nh, i0, ni, tiles = unit(a, u)
                if u == 0:
                    pe.wait_ge(operands_in, go.n(ev, "split", times=12 * 16))
                qo, r0 = operand(a, QOs)
                ko, _ = operand(a, KOs)
                sc = slot(r, nh)
                begun = set()
                for s, jt in tiles.items():
                    for h in range(nh):
                        pe_bank = s * COLS // 512
                        ins = pe.matmul(sc[:, s, h, :], ko[r0:r0 + ROWS, h0 + h, P * jt:P * jt + P],
                                        qo[r0:r0 + ROWS, h0 + h, i0:i0 + ni], start=pe_bank not in begun, stop=False,
                                        skip_group_check=True)
                        begun.add(pe_bank)
                    if a == POS:
                        dl = i0 - P * jt
                        if dl in DELTAS:
                            il = i0 % HT
                            for c in range(TAPS):
                                y = DELTAS[0] + TAPS - 1 - dl - c
                                ins = pe.matmul(sc[:, s, :, c:IB:TAPS], relwin[:, y:y + P],
                                                QH[:, u // QU % 2, :, il + c:il + IB:TAPS],
                                                start=False, stop=False, skip_group_check=True)
                        else:
                            ins = pe.matmul(sc[:, s, :, :], relclip[:, 0 if dl > 0 else 1, :],
                                            qo[0:ROWS, h0:h0 + nh, i0:i0 + ni],
                                            start=False, stop=False, skip_group_check=True)
                    if a == WINDOW:
                        ins = pe.matmul(sc[:, s, :, :], ident_b[:, :], masks[:, s:s + 1, :].broadcast_to([P, nh, P]),
                                        start=False, stop=False, skip_group_check=True)
                ins.then_inc(scores_ready, 1)

            def turn(go, ev, what, *args):
                r = go.ring(ev, "turn", RING)
                pe.wait_ge(colmax_ready, go.n(ev, "turn"))
                wait(pe, rowmax_ready, go.n(ev, "turn", back=1))
                for q in range(len(A_UNITS[args[0]]) if what == "a" else 2):
                    ins = pe.transpose(TB[:, P * q:P * q + P], MX[:, r, P * q:P * q + P], idf)
                ins.then_inc(colmax_turned, 1)

            def shift(go, ev, what, *args):
                r = go.ring(ev, "shift", RING)
                pe.wait_ge(shift_ready, go.n(ev, "shift"))
                if what == "a":
                    for n_, (it, c0, n) in enumerate(A_UNITS[args[0]]):
                        ins = pe.matmul(SB[:, r, P * c0:P * (c0 + n)], ones_b[:, :],
                                        DG[:, r, n_:n_ + 1, :].broadcast_to([P, n, P]), start=False, stop=True,
                                        skip_group_check=True)
                else:
                    tiles = sorted(unit(*args)[4])
                    row = DG[:, r, :, :].rearrange("p q i -> p (q i)").unsqueeze(1)
                    for s in range(tiles[0], tiles[-1] + 1, 2):
                        n = min(2, tiles[-1] + 1 - s)
                        ins = pe.matmul(SB[:, r, COLS * s:COLS * (s + n)], ones_b[:, :],
                                        row.broadcast_to([P, n, COLS]), start=False, stop=True, skip_group_check=True)
                ins.then_inc(scores_shifted, 1)

            def a_v(go, ev):
                take(go, ev)
                for t in range(NT):
                    ins = pe.matmul(MB[:, P * t:P * t + P], xnT["xnT"][:, P * t:P * t + P], w("wv_a"), start=True, stop=True)
                ins.then_inc(misc_filled, 1)

            def a_q(go, ev):
                take(go, ev)
                pe.matmul(MB[:, :], w("wq_a"), xnT["xnT"][:, :], start=True, stop=True).then_inc(misc_filled, 1)

            def a_k(go, ev):
                take(go, ev)
                pe.matmul(MB[:, :], w("wk_a"), xnT["xnT"][:, :], start=True, stop=True).then_inc(misc_filled, 1)

            def a_out(go, ev, it, mark):
                take(go, ev)
                pe.wait_ge(probs_ready, go.upto(mark, "shift"))
                ui, c0, n = next((i, s[1], s[2]) for i, segs in enumerate(A_UNITS) for s in segs if s[0] == it)
                for j in range(n):
                    ins = pe.matmul(MB[:, 0:E + 2], PTA[:, ui, P * (c0 + j):P * (c0 + j) + P], VA[:, j, :],
                                    start=(j == 0), stop=(j == n - 1))
                ins.then_inc(misc_filled, 1)

            def source(a):
                return (xnT["xnT0"] if a == POS else xnT["xnT"]), (E if a != FULL else E // 2)

            def proj_q(go, ev, a):
                take(go, ev)
                src, ein = source(a)
                pe.matmul(MB[:, :], w(f"wq{a}", ein), src[0:ein, :], start=True, stop=True).then_inc(misc_filled, 1)

            def proj_k(go, ev, a):
                take(go, ev)
                src, ein = source(a)
                pe.matmul(MB[:, :], w(f"wk{a}", ein), src[0:ein, :], start=True, stop=True).then_inc(misc_filled, 1)

            def proj_v(go, ev, a):
                take(go, ev)
                src, ein = source(a)
                rows = DHEAD[a] * H
                for t in range(NT):
                    ins = pe.matmul(MB[:, rows * t:rows * t + rows], src[0:ein, P * t:P * t + P], w(f"wv{a}", ein),
                                    start=True, stop=True)
                ins.then_inc(misc_filled, 1)

            def spread(go, ev, half, pair):
                take(go, ev)
                pe.wait_ge(wq_repeated, go.n(ev, "repeat"))
                for n in range(2):
                    ins = pe.matmul(MB[:, HT * n:HT * n + HT], WR[:, 2 * pair + n, :, :].rearrange("p a d -> p (a d)"),
                                    xnT["xnT0"][:, HT * (half % 2):HT * (half % 2) + HT], start=True, stop=True)
                ins.then_inc(misc_filled, 1)

            def weigh(go, ev, a, half, mark):
                take(go, ev)
                pe.wait_ge(probs_ready, go.upto(mark, "shift"))
                pr, h0 = pt(half), HPG * (half // 2)
                if a == WINDOW:
                    parts = [(P * n, P, s, t - 1 + s, s == max(0, 1 - t), s == 1)
                             for n, t in enumerate((2 * (half % 2), 2 * (half % 2) + 1)) for s in range(max(0, 1 - t), 2)]
                else:
                    parts = [(0, HT, j, j, j == 0, j == NT - 1) for j in range(NT)]
                for c0, n, s, jt, st, en in parts:
                    for h in range(HPG):
                        ins = pe.matmul(MB[32 * h:32 * h + VC, c0:c0 + n], VO[a][:, jt, h0 + h, :],
                                        pr[:, s, h, c0:c0 + n], start=st, stop=en)
                ins.then_inc(misc_filled, 1)

            def renorm(go, ev, a, hg):
                take(go, ev)
                for t in range(NT):
                    ins = pe.transpose(MB[:, P * t:P * t + P], OS[:, P * t:P * t + P], idf)
                ins.then_inc(misc_filled, 1)

            def unturn(go, ev, a):
                take(go, ev)
                for t in range(NT):
                    ins = pe.transpose(MB[:, P * t:P * t + P], AN[a][:, t, :], idf)
                ins.then_inc(misc_filled, 1)

            def outproj(go, ev, a, dst):
                take(go, ev)
                for t in range(NT):
                    ins = pe.matmul(MB[:, E * t:E * t + E], ATT[:, P * t:P * t + P], w(f"wo{a}"), start=True, stop=True)
                ins.then_inc(misc_filled, 1)

            def turnx(go, ev, dst):
                take(go, ev)
                pe.wait_ge(normed, go.n(ev, "norm_d"))
                for t in range(NT):
                    ins = pe.transpose(MB[:, P * t:P * t + P], xn[:, t, :], idf)
                ins.then_inc(misc_filled, 1)

            def hidden(go, ev, t):
                take(go, ev)
                pe.matmul(MB[:, :], Wfc[:, P * t:P * t + P], xnT["xnT"][:, :], start=True, stop=True
                          ).then_inc(misc_filled, 1)

            def ffn_out(go, ev, dst, *_):
                take(go, ev)
                pe.wait_ge(squared, go.n(ev, "hidden"))
                for t in range(NT):
                    for c in range(FT):
                        ins = pe.matmul(MB[:, E * t:E * t + E], HB[:, c, P * t:P * t + P], Wpr[:, c, :],
                                        start=(c == 0), stop=(c == FT - 1))
                ins.then_inc(misc_filled, 1)

            def enc(go, ev, c):
                take(go, ev)
                pe.matmul(MB[:, :], w("enc")[:, P * c:P * c + P], xnT["xnT"][:, :], start=True, stop=True
                          ).then_inc(misc_filled, 1)

            def dec(go, ev, n):
                take(go, ev)
                pe.matmul(MB[:, :], w("dec")[:, E * n:E * n + E], EH[:, n // 4, :], start=True, stop=True
                          ).then_inc(misc_filled, 1)

            def total(go, ev):
                take(go, ev)
                pe.wait_ge(loss_part, go.n(ev, "dec"))
                pe.matmul(MB[:, 0:NA], ones_f[:, :], LP[:, :], start=True, stop=True).then_inc(misc_filled, 1)

            def down(go, ev):
                take(go, ev)
                pe.wait_ge(adapter_ready, go.n(ev, "selected"))
                pe.matmul(MB[0:AR, :], SEL[:, (NA - 1) % 2, 0:AR], xnT["xnT"][:, :], start=True, stop=True
                          ).then_inc(misc_filled, 1)

            def up(go, ev, dst, *_):
                take(go, ev)
                for t in range(NT):
                    pe.matmul(MB[:, E * t:E * t + E], xnT["xnT"][:, P * t:P * t + P], w("w_base"), start=True, stop=False)
                    ins = pe.matmul(MB[:, E * t:E * t + E], MID[:, P * t:P * t + P], SEL[:, (NA - 1) % 2, AR:AR + E],
                                    start=False, stop=True)
                ins.then_inc(misc_filled, 1)

            walk(pe, {"scores": scores, "turn": turn, "shift": shift, "a_v": a_v, "a_q": a_q, "a_k": a_k, "a_out": a_out,
                      "proj_q": proj_q, "proj_k": proj_k, "proj_v": proj_v, "spread": spread, "weigh": weigh,
                      "renorm": renorm, "unturn": unturn, "outproj": outproj, "turnx": turnx, "hidden": hidden,
                      "ffn_out": ffn_out, "enc": enc, "dec": dec, "total": total, "down": down, "up": up})

        @block.scalar
        def _(act):
            act.wait_ge(w_loaded, 16 * 5)
            act.wait_ge(prep_pool, 3)

            def shift(go, ev, what, *args):
                r = go.ring(ev, "shift", RING)
                act.wait_ge(scores_shifted, go.n(ev, "shift"))
                if what == "a":
                    cols = P * sum(n for _, _, n in A_UNITS[args[0]])
                    act.activation(PTA[:, args[0], 0:cols], SB[:, r, 0:cols], ACT.Exp, scale=float(E) ** -0.5
                                   ).then_inc(probs_ready, 1)
                    return
                a, u = args
                h0, nh, i0, ni, tiles = unit(a, u)
                lo, hi = min(tiles), max(tiles) + 1
                il, hl = i0 % HT, h0 % HPG
                act.activation(pt(u // QU)[:, lo:hi, hl:hl + nh, il:il + ni], slot(r, nh)[:, lo:hi, :, :], ACT.Exp,
                               scale=8.0 ** -0.5).then_inc(probs_ready, 1)

            def copy_out(go, ev, dst, src, func=ACT.Copy, **kw):
                act.wait_ge(misc_filled, go.n(ev, "misc"))
                act.activation(dst, src, func, **kw).then_inc(misc_read, 1)

            def a_q(go, ev):
                copy_out(go, ev, QF[:, :], MB[:, :], ACT.Identity, bias=w("bq_a"))

            def a_k(go, ev):
                copy_out(go, ev, KF[:, :], MB[:, :], ACT.Identity, bias=w("bk_a"))

            def both(go, ev, full, high, a, bias):
                rows = DHEAD[a] * H
                bias = w(bias) if a != FULL else zero_col[0:rows, :]
                act.wait_ge(misc_filled, go.n(ev, "misc"))
                act.activation(full[0:rows, :], MB[0:rows, :], ACT.Identity, bias=bias)
                act.activation(high[0:rows, 0, :], MB[0:rows, :], ACT.Identity, bias=bias).then_inc(misc_read, 1)

            def proj_q(go, ev, a):
                both(go, ev, QF, Q3, a, f"bq{a}")

            def proj_k(go, ev, a):
                both(go, ev, KF, K3, a, f"bk{a}")

            def weigh(go, ev, a, half, mark):
                copy_out(go, ev, OS[:, HT * (half % 2):HT * (half % 2) + HT], MB[:, 0:HT])

            def unturn(go, ev, a):
                copy_out(go, ev, ATT[:, :], MB[:, :])

            def turnx(go, ev, dst):
                copy_out(go, ev, xnT[dst][:, :], MB[:, :])

            def hidden(go, ev, t):
                copy_out(go, ev, HB[:, t, :], MB[:, :], ACT.Relu)

            def enc(go, ev, c):
                copy_out(go, ev, EH[:, c, :], MB[:, :], ACT.Relu, bias=w("b_enc")[:, c:c + 1])

            def dec(go, ev, n):
                act.wait_ge(misc_read, go.n(ev, "misc"))
                wait(act, loss_part, go.n(ev, "dec", back=1))
                act.activation(sq[:, :], DF[:, n % 2, :], ACT.Square, accum_out=LP[:, n:n + 1]).then_inc(loss_part, 1)

            def down(go, ev):
                copy_out(go, ev, MID[0:AR, :], MB[0:AR, :], ACT.Relu, bias=SEL[0:AR, (NA - 1) % 2, PACK - 1:PACK])

            walk(act, {"shift": shift, "a_q": a_q, "a_k": a_k, "proj_q": proj_q, "proj_k": proj_k, "weigh": weigh,
                       "unturn": unturn, "turnx": turnx, "hidden": hidden, "enc": enc, "dec": dec, "down": down})

        @block.vector
        def _(dve):
            dve.wait_ge(w_loaded, 16 * 5)
            steps = [0]

            def done(ins):
                steps[0] += 1
                ins.then_inc(prep_step, 1)

            def plink(ins):
                done(ins)
                dve.wait_ge(prep_step, steps[0])

            dve.tensor_copy(ident_b[:, :], w("ident"))
            dve.tensor_copy(masks[:, 0, :], w("keep0"))
            dve.tensor_copy(masks[:, 1, :], w("keep1"))
            plink(dve.tensor_copy(cidx_f[:, :], cidx_i[:, :]))
            plink(dve.tensor_scalar(wrap[:, :], cidx_f[:, :], 0.0, float(NA), ALU.is_lt, ALU.mult))
            plink(dve.tensor_tensor(cidx_f[:, :], cidx_f[:, :], wrap[:, :], ALU.add))
            plink(dve.tensor_scalar(cidx_f[:, :], cidx_f[:, :], 0.0, float(NA - 1), ALU.max, ALU.min))

            def ternary(src, dst, blocks, width, at):
                mag = TERN[:, 3, :].rearrange("p (t i) -> p t i", t=blocks)
                low = TERN[:, 4, :].rearrange("p (t i) -> p t i", t=blocks)
                scale_, half, nhalf = ch[:, at, 0:blocks], ch[:, 1 + at, 0:blocks], ch[:, 2 + at, 0:blocks]
                plink(dve.scalar_tensor_tensor(out=mag, in0=src, scalar=-1.0, in1=src, op0=ALU.mult, op1=ALU.max))
                plink(dve.tensor_reduce(scale_, mag, AX.X, ALU.add))
                plink(dve.tensor_scalar(scale_, scale_, 1.0 / width, EPS, ALU.mult, ALU.max))
                done(dve.tensor_scalar(half, scale_, 0.5, None, ALU.mult))
                plink(dve.tensor_scalar(nhalf, scale_, -0.5, None, ALU.mult))
                for t in range(blocks):
                    done(dve.tensor_scalar(mag[:, t, :], src[:, t, :], half[:, t:t + 1], None, ALU.is_gt))
                    plink(dve.tensor_scalar(low[:, t, :], src[:, t, :], nhalf[:, t:t + 1], None, ALU.is_lt))
                plink(dve.tensor_tensor(mag, mag, low, ALU.subtract))
                plink(dve.tensor_tensor(mag, mag, src, ALU.subtract))
                plink(dve.tensor_tensor(mag, mag, src, ALU.add))
                for t in range(blocks):
                    ins = dve.tensor_scalar(dst[:, t, :], mag[:, t, :], scale_[:, t:t + 1], None, ALU.mult)
                    if t < blocks - 1:
                        done(ins)
                return ins

            ternary(w("w_fc").rearrange("p (t i) -> p t i", t=FT), TERN[:, 0, :].rearrange("p (t i) -> p t i", t=FT),
                    FT, E, 0).then_inc(prep_dve, 1)
            dve.wait_ge(prep_dve, 1)
            ternary(w("w_proj").rearrange("p (t i) -> p t i", t=1), TERN[:, 1, :].rearrange("p (t i) -> p t i", t=1),
                    1, HID, 3).then_inc(prep_dve, 1)
            dve.wait_ge(prep_pe, 3)
            done(dve.tensor_copy(Wfc[:, :], SB[:, 0, 0:HID]))
            done(dve.tensor_copy(Wpr[:, :, :], SB[:, 1, 0:HID].rearrange("p (t i) -> p t i", t=FT)))
            dve.tensor_copy(TERN[0:RANK, 2, :], SB[0:RANK, 2, 0:HID]).then_inc(prep_dve, 1)
            dve.wait_ge(prep_pe, 4)
            dve.wait_ge(prep_step, steps[0])
            dve.scalar_tensor_tensor(out=Wfc[:, :], in0=SB[:, 2, 512:1024], scalar=w("gate"), in1=Wfc[:, :],
                                     op0=ALU.mult, op1=ALU.add).then_inc(prep_dve, 1)

            def step(ins):
                ins.then_inc(dve_step, 1)

            def settle(go, ev, back=0):
                wait(dve, dve_step, go.n(ev, "dve", back=back))

            def filled(go, ev):
                dve.wait_ge(misc_filled, go.n(ev, "misc"))

            def scores(go, ev, what, *args):
                r = go.ring(ev, "scores", RING)
                dve.wait_ge(scores_ready, go.n(ev, "scores"))
                if what == "a":
                    segs = [(P * i, SB[:, r, P * c0:P * (c0 + n)], n, P) for i, (_, c0, n) in enumerate(A_UNITS[args[0]])]
                else:
                    tiles = unit(*args[0:2])[4]
                    lo, n = min(tiles), len(tiles)
                    segs = [(0, SB[:, r, COLS * lo:COLS * (lo + n)], n, COLS)]
                for o, src, n, cols in segs:
                    if n == 1:
                        ins = dve.tensor_copy(MX[:, r, o:o + cols], src)
                    else:
                        ins = dve.tensor_reduce(MX[:, r, o:o + cols], src.rearrange("p (t c) -> p c t", t=n), AX.X, ALU.max)
                ins.then_inc(colmax_ready, 1)

            def turn(go, ev, what, *args):
                r = go.ring(ev, "turn", RING)
                q = len(A_UNITS[args[0]]) if what == "a" else 2
                dve.wait_ge(colmax_turned, go.n(ev, "turn"))
                dve.tensor_reduce(NM[:, r, 0:q], TB[:, 0:P * q].rearrange("p (q j) -> p q j", q=q), AX.X, ALU.max
                                  ).then_inc(rowmax_ready, 1)

            def norm_a(go, ev, src, mark):
                if src == "xin":
                    dve.wait_ge(x_loaded, go.n(ev, "load", times=16))
                else:
                    dve.wait_ge(misc_read, go.upto(mark, "misc"))
                for t in range(NT):
                    step(dve.bn_stats(stats[:, t, :], X[src][:, t, :]))

            def norm_b(go, ev):
                settle(go, ev, NT)
                dve.tensor_copy(fence[:, :], w("ident")[:, 0:1])
                for t in range(NT):
                    step(dve.bn_aggr(mv[:, t, :], stats[:, t, :]))

            def norm_c(go, ev):
                settle(go, ev, 3)
                step(dve.tensor_scalar(nhvar[:, :], mv[:, :, 1], EPS, -0.5, ALU.add, ALU.mult))
                step(dve.tensor_scalar(var[:, :], mv[:, :, 1], EPS, None, ALU.add))
                settle(go, ev, 1)
                step(dve.tensor_scalar(rs[0][:, :].bitcast(I32), var[:, :].bitcast(I32), 1, None, ALU.logical_shift_right))
                settle(go, ev)
                dve.tensor_scalar(rs[1][:, :].bitcast(I32), rs[0][:, :].bitcast(I32), -1.0, float(0x5F3759DF),
                                  ALU.mult, ALU.add).then_inc(seeded, 1)

            def a_v(go, ev):
                filled(go, ev)
                dve.tensor_tensor(VA[:, :, 0:E], MB[:, :].rearrange("p (t e) -> p t e", t=NT),
                                  w("bv_a").unsqueeze(1).broadcast_to([P, NT, E]), ALU.add).then_inc(misc_read, 1)

            def a_out(go, ev, it, mark):
                filled(go, ev)
                step(dve.reciprocal(arec[:, :], MB[:, E:E + 1]))
                settle(go, ev)
                dve.scalar_tensor_tensor(out=X["xa"][:, it, :], in0=MB[:, 0:E], scalar=arec[:, :],
                                         in1=X["xin"][:, it, :], op0=ALU.mult, op1=ALU.add).then_inc(misc_read, 1)

            def proj_v(go, ev, a):
                filled(go, ev)
                d = DHEAD[a]
                src = MB[:, 0:NT * H * d].rearrange("p (t h d) -> p t h d", t=NT, h=H)
                if a == FULL:
                    ins = dve.tensor_copy(VO[a][:, :, :, 0:d], src)
                else:
                    bv = w(f"bv{a}").rearrange("p (h d) -> p h d", h=H).unsqueeze(1).broadcast_to([P, NT, H, d])
                    ins = dve.tensor_tensor(VO[a][:, :, :, 0:d], src, bv, ALU.add)
                ins.then_inc(misc_read, 1)

            def spread(go, ev, half, pair):
                filled(go, ev)
                for n in range(2):
                    h = HPG * (half // 2) + 2 * pair + n
                    ins = dve.scalar_tensor_tensor(out=QH[:, half % 2, 2 * pair + n, :].rearrange("p (k i) -> p k i", i=IB),
                                                   in0=MB[:, HT * n:HT * n + HT].rearrange("p (k i) -> p k i", i=IB),
                                                   scalar=w("bqr0")[:, h:h + 1],
                                                   in1=w("onehot").unsqueeze(1).broadcast_to([P, HT // IB, IB]),
                                                   op0=ALU.add, op1=ALU.mult)
                ins.then_inc(misc_read, 1)

            def renorm(go, ev, a, hg):
                filled(go, ev)
                d = DHEAD[a]
                src = MB[:, :].rearrange("p (t h c) -> p t h c", t=NT, h=HPG)
                step(dve.reciprocal(rec[:, :, :], src[:, :, :, 8]))
                settle(go, ev)
                dve.tensor_tensor(AN[a][:, :, HPG * d * hg:HPG * d * (hg + 1)].rearrange("p t (h d) -> p t h d", h=HPG),
                                  src[:, :, :, 0:d], rec[:, :, :].unsqueeze(3).broadcast_to([P, NT, HPG, d]), ALU.mult
                                  ).then_inc(misc_read, 1)

            def bias(go, ev, a, src, dst):
                if dst == "xout":
                    wait(dve, stored, go.n(ev, "store", times=16, before=16))
                step(dve.tensor_tensor(X[dst][:, :, :], X[src][:, :, :], w(f"bo{a}").unsqueeze(1).broadcast_to([P, NT, E]),
                                       ALU.add))

            def add(go, ev, dst):
                filled(go, ev)
                dve.tensor_tensor(X[dst][:, :, :], X[dst][:, :, :], MB[:, :].rearrange("p (t e) -> p t e", t=NT), ALU.add
                                  ).then_inc(misc_read, 1)

            def outproj(go, ev, a, dst):
                settle(go, ev)
                add(go, ev, dst)

            def ffn_out(go, ev, dst):
                add(go, ev, dst)

            def dec(go, ev, n):
                filled(go, ev)
                wait(dve, loss_part, go.n(ev, "dec", back=2))
                dve.scalar_tensor_tensor(out=DF[:, n % 2, :], in0=MB[:, :], scalar=w("b_dec")[:, n:n + 1],
                                         in1=xnT["xnT"][:, :], op0=ALU.add, op1=ALU.subtract).then_inc(misc_read, 1)

            loss, least, later, first_, hot, picked, cid, hot2 = (ch[:, i, :] for i in range(8))

            def total(go, ev):
                filled(go, ev)
                dve.tensor_copy(loss, MB[:, 0:NA]).then_inc(misc_read, 1)

            def pick(go, ev, n, mark):
                if n == 1:
                    dve.wait_ge(misc_read, go.upto(mark, "misc"))
                    step(dve.tensor_reduce(least[:, 0:1], loss, AX.X, ALU.min))
                    return
                settle(go, ev, 1)
                if n == 2:
                    step(dve.tensor_scalar(later, loss, least[:, 0:1], float(2 * NA), ALU.is_gt, ALU.mult))
                if n == 3:
                    step(dve.tensor_tensor(picked, later, w("iota"), ALU.add))
                if n == 4:
                    step(dve.tensor_reduce(first_[:, 0:1], picked, AX.X, ALU.min))
                if n == 5:
                    step(dve.tensor_scalar(hot, w("iota"), first_[:, 0:1], None, ALU.is_equal))
                if n == 6:
                    step(dve.tensor_tensor(picked, hot, cidx_f[:, :], ALU.mult))
                if n == 7:
                    step(dve.tensor_reduce(cid[:, 0:1], picked, AX.X, ALU.add))
                if n == 8:
                    step(dve.tensor_scalar(hot2, w("iota"), cid[:, 0:1], None, ALU.is_equal))

            packs = w("pack").rearrange("p (n c) -> p n c", n=NA)

            def select(go, ev, n):
                settle(go, ev, 1)
                if n == 0:
                    step(dve.tensor_scalar(SEL[:, 0, :], packs[:, 0, :], hot2[:, 0:1], None, ALU.mult))
                else:
                    step(dve.scalar_tensor_tensor(out=SEL[:, n % 2, :], in0=packs[:, n, :], scalar=hot2[:, n:n + 1],
                                                  in1=SEL[:, (n - 1) % 2, :], op0=ALU.mult, op1=ALU.add))

            def selected(go, ev):
                settle(go, ev)
                n = NA - 1
                dve.scalar_tensor_tensor(out=SEL[:, n % 2, :], in0=packs[:, n, :], scalar=hot2[:, n:n + 1],
                                         in1=SEL[:, (n - 1) % 2, :], op0=ALU.mult, op1=ALU.add).then_inc(adapter_ready, 1)

            def up(go, ev, dst):
                add(go, ev, dst)

            walk(dve, {"scores": scores, "turn": turn, "norm_a": norm_a, "norm_b": norm_b, "norm_c": norm_c, "a_v": a_v,
                       "a_out": a_out, "proj_v": proj_v, "spread": spread, "renorm": renorm, "bias": bias,
                       "outproj": outproj, "ffn_out": ffn_out, "dec": dec, "total": total, "pick": pick,
                       "select": select, "selected": selected, "up": up})


def layout(i):
    import numpy as np

    f = np.float32
    s = {}
    r = np.arange(P)
    s["ident"] = np.eye(P, dtype=f)
    s["negident"] = -np.eye(P, dtype=f)
    s["keep1"] = np.where(r[:, None] <= r[None, :], 0, NEG).astype(f)
    s["keep0"] = np.where(r[:, None] >= r[None, :], 0, NEG).astype(f)
    s["onehot"] = ((np.arange(IB)[None, :] // TAPS) % 16 == r[:, None] // 8).astype(f)
    s["iota"] = np.broadcast_to(np.arange(NA, dtype=f), (P, NA))
    rep = lambda v: np.broadcast_to(v, (P,) + v.shape[-1:])
    s["gate"] = rep(i["L0_ffn_gate"].reshape(1, 1))
    s["w_fc"] = i["L0_ffn_w_fc"].reshape(FT, P, E).transpose(1, 0, 2).reshape(P, FT * E)
    s["w_proj"] = i["L0_ffn_w_proj"]
    s["fast_b"], s["uT"], s["v"] = i["L0_ffn_fast_b"], i["L0_ffn_u"].T, i["L0_ffn_v"]
    for n in "qk":
        s[f"w{n}_a"] = i[f"L0_attn_a_W{n}"].T
        s[f"b{n}_a"] = i[f"L0_attn_a_b{n}"][:, None]
    s["wv_a"], s["bv_a"] = i["L0_attn_a_Wv"].T, rep(i["L0_attn_a_bv"])
    s["relT"] = i["L0_attn_b_rel_table"][::-1].T
    w_in, b_in = i["L1_attn_b_w_in"], i["L1_attn_b_b_in"]
    heads = (
        [i[f"L0_attn_b_W{n}"] for n in "qkv"] + [i[f"L0_attn_b_b{n}"] for n in "qkv"] + [i["L0_attn_b_Wo"], i["L0_attn_b_bo"]],
        [i[f"L1_attn_a_W{n}"] for n in "qkv"] + [None] * 3 + [i["L1_attn_a_Wo"], i["L1_attn_a_bo"]],
        [w_in[E * n:E * n + E] for n in range(3)] + [b_in[E * n:E * n + E] for n in range(3)]
        + [i["L1_attn_b_w_out"], i["L1_attn_b_b_out"]],
    )
    for a, (wq, wk, wv, bq, bk, bv, wo, bo) in enumerate(heads):
        d = DHEAD[a]
        for n, m in (("q", wq), ("k", wk)):
            s[f"w{n}{a}"] = np.zeros((P, E), f)
            s[f"w{n}{a}"][0:m.shape[1], 0:d * H] = m.reshape(H, d, -1).transpose(2, 1, 0).reshape(-1, d * H)
        s[f"wv{a}"] = wv.T
        if bq is not None:
            for n, m in (("q", bq), ("k", bk)):
                s[f"b{n}{a}"] = m.reshape(H, d).T.reshape(-1, 1)
            s[f"bv{a}"] = rep(bv)
        s[f"wo{a}"], s[f"bo{a}"] = wo.T, rep(bo)
    s["wqn0"] = heads[0][0].T
    s["bqr0"] = np.tile(heads[0][3].reshape(H, 8).T, (16, 1))
    s["enc"] = i["L1_ffn_W_enc"].transpose(1, 0, 2).reshape(E, NA * AH)
    s["b_enc"] = i["L1_ffn_b_enc"].reshape(2, P).T
    dec = np.zeros((P, NA, E), f)
    for n in range(NA):
        dec[AH * (n % 4):AH * (n % 4) + AH, n] = i["L1_ffn_W_dec"][n]
    s["dec"], s["b_dec"] = dec.reshape(P, NA * E), i["L1_ffn_b_dec"].T
    pack = np.zeros((P, NA, PACK), f)
    pack[:, :, 0:AR] = i["L1_ffn_W_down"].transpose(1, 0, 2)
    pack[0:AR, :, AR:AR + E] = i["L1_ffn_W_up"].transpose(1, 0, 2)
    pack[AR, :, AR:AR + E] = i["L1_ffn_b_up"]
    pack[AR + 1, :, AR:AR + E] = i["L1_ffn_b_base"]
    pack[0:AR, :, PACK - 1] = i["L1_ffn_b_down"].T
    s["pack"] = pack.reshape(P, NA * PACK)
    s["w_base"] = i["L1_ffn_W_base"]
    packed = np.zeros((P, WCOLS + PREP_COLS), f)
    for name, cols in SECTIONS + PREP_SECTIONS:
        v = s[name]
        assert v.shape[1] == cols, (name, v.shape)
        packed[0:v.shape[0], OFF[name][0]:OFF[name][0] + cols] = v
    return packed


def kernel(**inputs):
    import numpy as np
    import concourse.bacc as bacc
    from concourse.bass_utils import run_bass_kernel_spmd

    i = {k: np.asarray(v) for k, v in inputs.items()}
    arrays = {
        "x_dram": np.ascontiguousarray(i["L0_attn_a_x"]),
        "packed_dram": layout(i),
        "cidx_dram": np.ascontiguousarray(np.broadcast_to(i["L1_ffn_connected_idx"], (P, NA))),
    }
    nc = bacc.Bacc("TRN2", target_bir_lowering=False, num_devices=1)
    args = [nc.dram_tensor(n, a.shape, mybir.dt.from_np(a.dtype), kind="ExternalInput").ap() for n, a in arrays.items()]
    args.append(nc.dram_tensor("out_dram", (B, T, E), F32, kind="ExternalOutput").ap())
    build(nc, *args)
    r = run_bass_kernel_spmd(nc, [arrays], core_ids=[0])
    return r.results[0]["out_dram"]
```

```python
from contextlib import ExitStack

import concourse.bass as bass
from concourse import mybir

ALU = mybir.AluOpType
ACT = mybir.ActivationFunctionType
AX = mybir.AxisListType
F32 = mybir.dt.float32
BF16 = mybir.dt.bfloat16
I32 = mybir.dt.int32

P = 128
B, T, E = 8, 512, 128
NT = T // P
H = 16
HG, HPG = 4, 4
HT = T // 2
QU = 4
NU = HG * 2 * QU
COLS = HPG * HT // QU
POS, FULL, WINDOW = 0, 1, 2
DHEAD = (8, 4, 8)
A_UNITS = (((0, 0, 1), (1, 1, 2)), ((2, 0, 3),), ((3, 0, 4),))
RING = 3
HID = 512
FT = HID // P
RANK = 16
NA, AH, AR = 8, 32, 64
MAXLEN = 128
NREL = 2 * MAXLEN - 1
IB = 64
TAPS = 4
DELTAS = (192, 128, 64, 0, -64, -128)
RTL = 512
RWC = DELTAS[0] + TAPS - 1 + P + MAXLEN
ROWS = 64
SLOTS_Q = (0, 1, 2, 0, 1, 0)
SLOTS_K = (0, 0, 0, 1, 1, 2)
VC = 16
NEG = -1e30
EPS = 1e-5
PACK = AR + E + 1

PREP_SECTIONS = (
    ("gate", 1), ("w_fc", FT * P), ("w_proj", HID), ("fast_b", RANK), ("uT", HID), ("v", P), ("relT", NREL),
    ("keep1", P), ("keep0", P),
)
SECTIONS = (
    ("ident", P), ("wq_a", E), ("wk_a", E), ("wv_a", E), ("bq_a", 1), ("bk_a", 1), ("bv_a", E),
    ("onehot", IB),
    ("wq0", E), ("wk0", E), ("wv0", E), ("wqn0", E), ("bq0", 1), ("bk0", 1), ("bv0", E), ("bqr0", H), ("wo0", E), ("bo0", E),
    ("wq1", E), ("wk1", E), ("wv1", 64), ("wo1", E), ("bo1", E),
    ("enc", NA * AH), ("b_enc", 2), ("dec", NA * E), ("b_dec", NA), ("pack", NA * PACK), ("w_base", E), ("iota", NA),
    ("wq2", E), ("wk2", E), ("wv2", E), ("bq2", 1), ("bk2", 1), ("bv2", E), ("wo2", E), ("bo2", E),
)
OFF = {}
WCOLS = 0
for _name, _cols in SECTIONS:
    OFF[_name] = (WCOLS, _cols)
    WCOLS += _cols
PREP_COLS = 0
for _name, _cols in PREP_SECTIONS:
    OFF[_name] = (WCOLS + PREP_COLS, _cols)
    PREP_COLS += _cols


MISC = frozenset(("turnx", "a_v", "a_q", "a_k", "a_out", "proj_v", "proj_q", "proj_k", "spread", "weigh", "renorm", "unturn",
                  "outproj", "hidden", "ffn_out", "enc", "dec", "total", "down", "up"))
TAIL_STEPS = 10
LAGS = {"norm_a": 1, "norm_b": 1, "norm_c": 1, "newton": 0.5, "normalise": 0.5, "turnx": 3, "rest": 0, "ffn_out": 4, "down": 3}
DVE_LINKS = {"norm_a": NT, "norm_b": NT, "norm_c": 4, "newton": 3, "rest": 1, "a_out": 1, "renorm": 1, "bias": 1, "pick": 1, "select": 1}
POOL_LINKS = {"rest": 1}


class Event:
    def __init__(self, kind, args, counts):
        self.kind, self.args, self.c = kind, args, counts


def banks_of(u):
    return 2 if u[0] == "mha" and u[1] != WINDOW else 1


class Section:

    def __init__(self, base, trips=1):
        self.base, self.trips, self.c, self.events, self.marks = dict(base), trips, {}, [], {}
        self.filled = []

    def add(self, kind, *args):
        c = self.c
        if kind == "shift":
            c["banks"] = c.get("banks", 0) + banks_of(args)
        for k, n in ((kind, 1), ("misc", int(kind in MISC)), ("dve", DVE_LINKS.get(kind, 0)),
                     ("pool", POOL_LINKS.get(kind, 0))):
            if n:
                c[k] = c.get(k, 0) + n
        self.events.append(Event(kind, args, dict(c)))

    def after(self):
        return {k: self.base.get(k, 0) + self.trips * self.c.get(k, 0) for k in set(self.base) | set(self.c)}


def norm_events(x):
    return [("norm_a", x), ("norm_b",), ("norm_c",)] + [("newton", i) for i in range(3)] + [("normalise", x)]


def head_events(b):
    ffn = [*norm_events("xa"), ("turnx", "xnT")]
    ffn += [("hidden", t) for t in range(FT)] + [("ffn_out", "xa")]
    norm = [*norm_events("xa"), ("turnx", "xnT0")]
    first = [("load", b), *norm_events("xin"), ("turnx", "xnT"),
             ("a_v",), ("a_q",), ("a_k",)]
    return first, ffn + norm + proj_events(POS) + [("repeat", 0), ("spread", 0, 0), ("spread", 0, 1)]


def proj_events(a):
    return [("proj_q", a), ("proj_k", a), ("rest", a), ("proj_v", a), ("middle", a), ("low", a)]


def out_events(a, src, dst):
    return [("bias", a, src, dst), ("unturn", a), ("outproj", a, dst)]


def routed_events(x):
    ev = [*norm_events(x), ("turnx", "xnT")]
    ev += [("enc", 0), ("enc", 1)] + [("dec", n) for n in range(NA)] + [("total",)]
    ev += [("pick", n) for n in range(1, 9)] + [("select", n) for n in range(NA - 1)] + [("selected",), ("down",), ("up", x)]
    return ev


def mid1_events():
    ev = out_events(POS, "xa", "xb") + [*norm_events("xb"), ("turnx", "xnT")]
    ev += [("hidden", t) for t in range(FT)] + [("ffn_out", "xb")]
    return ev + [*norm_events("xb"), ("turnx", "xnT")] + proj_events(FULL)


def mid2_events():
    ev = out_events(FULL, "xb", "xc") + routed_events("xc")
    return ev + [*norm_events("xc"), ("turnx", "xnT")] + proj_events(WINDOW)


def tail_events(b):
    return out_events(WINDOW, "xc", "xout"), routed_events("xout") + [("store", b)]


def lag(e):
    if e == ("norm_a", "xin"):
        return 6
    return LAGS.get(e[0], 3 if e[0] in MISC else 0.3)


def pipeline(sec, units, light):
    steps = len(units) + 4 if units else 0
    due = {}
    for lo, hi, events in light:
        total, at, slot, ready = sum(lag(e) for e in events[1:]), 0, 0, 0
        for m, e in enumerate(events):
            at += lag(e) if m else 0
            slot = max(slot, int(3 * lo + 3 * (hi - lo) * at / max(total, 1)))
            if e[0] in ("turnx", "down"):
                slot = max(slot, ready + 4)
            if e[0] not in MISC:
                slot += (2 - slot) % 3
                ready = slot
            due.setdefault(slot, []).append(e)
    last = max([steps - 1] + [k // 3 for k in due])
    marks = sec.marks
    for k in range(last + 1):
        if k < len(units):
            u = units[k]
            need = 0
            if u[0] == "a":
                need = marks["a_k"]
            elif u[1] == POS and u[2] % QU == 0:
                need = marks["spread", u[2] // QU]
            m = len(sec.filled)
            sec.filled.append(((sec.filled[-1][0] if m else 0) + banks_of(u), banks_of(u)))
            if m >= RING:
                before = sec.filled[m - RING]
            else:
                before = (m + 1 - RING, 1) if sec.base else None
            sec.add("scores", *u, before, need)
        for e in due.get(3 * k, []):
            add_light(sec, e)
        if 0 <= k - 2 < len(units):
            sec.add("shift", *units[k - 2])
            marks[units[k - 2]] = sec.c["banks"]
        heavy = []
        if 0 <= k - 3 < len(units) and units[k - 3][0] == "mha":
            _, a, u = units[k - 3]
            if u % QU == QU - 1:
                heavy.append(("weigh", a, u // QU, marks[units[k - 3]]))
        if 0 <= k - 4 < len(units) and units[k - 4][0] == "mha":
            _, a, u = units[k - 4]
            if u % (2 * QU) == 2 * QU - 1:
                heavy.append(("renorm", a, u // (2 * QU)))
        if k < len(units) and units[k][0] == "mha" and units[k][1] == POS:
            u = units[k][2]
            nxt = u // QU + 1
            if nxt < 2 * HG and u % QU in (0, 1):
                heavy.append(("spread", nxt, u % QU))
                if u % QU == 1 and nxt % 2 == 1 and nxt + 1 < 2 * HG:
                    heavy.append(("repeat", nxt // 2 + 1))
        for e in due.get(3 * k + 1, []):
            add_light(sec, e)
        if 0 <= k - 1 < len(units):
            sec.add("turn", *units[k - 1])
        for e in heavy + due.get(3 * k + 2, []):
            add_light(sec, e)


def add_light(sec, e):
    if e[0] == "norm_a":
        e = e + (sec.marks.get("x", 0),)
    if e[0] == "a_out":
        e = e + (sec.marks[("a", next(i for i, segs in enumerate(A_UNITS) for s in segs if s[0] == e[1]))],)
    if e[0] == "store":
        e = e + (sec.marks["x"],)
    if e[0] in ("rest", "pick"):
        e = e + (sec.marks["proj_k" if e[0] == "rest" else "total"],)
    sec.add(*e)
    if e[0] in ("a_out", "outproj", "ffn_out", "up"):
        sec.marks["x"] = sec.c["misc"]
    if e[0] in ("a_k", "proj_k", "total"):
        sec.marks[e[0]] = sec.c["misc"]
    if e[0] == "spread":
        sec.marks["spread", e[1]] = sec.c["misc"]


def plan():
    mha = [[("mha", a, u) for u in range(NU)] for a in range(3)]
    single = [("a", i) for i in range(len(A_UNITS))]
    outs = [("a_out", t) for t in range(NT)]

    def iteration(sec, tail, head, nxt):
        light = []
        units = list(mha[FULL])
        if head is not None:
            first, rest = head_events(head)
            units = units[:8] + single + units[8:]
            light += [(0, 7, first), (11, 13, outs), (14, len(units) - 2, rest)]
        full_done = len(units) + 4
        if nxt:
            units += mha[POS] + mha[WINDOW]
            pos_done = len(units) - NU + 4
            mid2_from, mid2_to = full_done, pos_done - 7
            if tail is not None:
                outs_, rest = tail_events(tail)
                mid2_from += TAIL_STEPS
                light.append((full_done - 3, mid2_from - 1, outs_ + rest))
            light.append((mid2_from, mid2_to, mid2_events()))
            light.append((pos_done, len(units) + 2, mid1_events()))
        else:
            outs_, rest = tail_events(tail)
            light.append((full_done - 2, full_done, outs_))
            light.append((full_done + 1, full_done + 30, mid2_events()))
        pipeline(sec, units, light)
        if not nxt:
            pipeline(sec, mha[WINDOW], [(0, 20, rest)])

    sections = []
    sec = Section({})
    first, rest = head_events(0)
    for e in first:
        add_light(sec, e)
    pipeline(sec, single, [(5, 6, outs), (7, 8, rest)])
    pipeline(sec, mha[POS], [])
    for e in mid1_events():
        add_light(sec, e)
    iteration(sec, None, 1, True)
    sections.append(sec)
    sec = Section(sec.after(), trips=B - 2)
    iteration(sec, 0, 2, True)
    sections.append(sec)
    sec = Section(sec.after())
    iteration(sec, B - 2, None, False)
    for part in tail_events(B - 1):
        for e in part:
            add_light(sec, e)
    sections.append(sec)
    return sections


def build(nc: bass.Bass, x: bass.AP, packed: bass.AP, cidx: bass.AP, out: bass.AP):
    relpad = nc.dram_tensor("relpad_scratch", (8, RTL), F32, kind="Internal").ap()
    sections = plan()
    with ExitStack() as ctx:
        def sb(name, shape, dt=F32):
            return ctx.enter_context(nc.sbuf_tensor(name, shape, dt))

        def sem(name):
            return ctx.enter_context(nc.semaphore(name))

        W = sb("W", [P, WCOLS])
        PT = sb("PT", [P, 2, NT * HPG * HT])
        PREP = PT[:, :, :].rearrange("p u n -> p (u n)")[:, 0:PREP_COLS]
        TERN = PT[:, :, :].rearrange("p u n -> p (u n)")[:, PREP_COLS:PREP_COLS + 5 * HID].rearrange(
            "p (n i) -> p n i", n=5)
        relrow = PT[:, :, :].rearrange("p u n -> p (u n)")[0:8, PREP_COLS + 5 * HID:PREP_COLS + 5 * HID + RTL]

        def w(name, rows=P):
            o, n = OFF[name]
            return W[0:rows, o:o + n] if o < WCOLS else PREP[0:rows, o - WCOLS:o - WCOLS + n]

        ident_b = sb("ident_b", [P, P], BF16)
        negident_b = sb("negident_b", [P, P], BF16)
        ones_b = sb("ones_b", [P, P], BF16)
        ones_f = sb("ones_f", [P, P])
        masks = sb("masks", [P, 2, P], BF16)
        zero_col = sb("zero_col", [P, 1])
        cidx_i = sb("cidx_i", [P, NA], I32)
        cidx_f = sb("cidx_f", [P, NA])
        wrap = sb("wrap", [P, NA])
        Wfc = sb("Wfc", [P, HID])
        Wpr = sb("Wpr", [P, FT, E])
        relwin = sb("relwin", [P, RWC])
        relparts = sb("relparts", [8, 3, 2], BF16)
        relrest = sb("relrest", [8, 2])
        relclip_c = sb("relclip_c", [ROWS, 2], BF16)
        relclip = sb("relclip", [ROWS, 2, P], BF16)

        X = {n: sb(n, [P, NT, E]) for n in ("xin", "xa", "xb", "xc", "xout")}
        stats = sb("stats", [P, NT, 6])
        mv = sb("mv", [P, NT, 2])
        fence = sb("fence", [P, 1])
        var = sb("var", [P, NT])
        nhvar = sb("nhvar", [P, NT])
        rs = [sb(f"rs{i}", [P, NT]) for i in range(2)]
        nt = [sb(f"nt{i}", [P, NT]) for i in range(2)]
        xn = sb("xn", [P, NT, E])
        xnT = {"xnT": sb("xnT", [E, T]), "xnT0": sb("xnT0", [E, T])}

        QF = sb("QF", [P, T])
        KF = sb("KF", [P, T])
        Q3 = sb("Q3", [P, 3, T], BF16)
        K3 = sb("K3", [P, 3, T], BF16)
        VA = sb("VA", [P, NT, E + 2])
        QOs = [sb(f"QO{i}", [P, H, T], BF16) for i in range(2)]
        KOs = [sb(f"KO{i}", [P, H, T], BF16) for i in range(2)]
        VO = [sb(f"VO{a}", [P, NT, H, VC]) for a in range(3)]
        WR = sb("WR", [P, HPG, 16, 8])
        QH = sb("QH", [P, 2, HPG, HT])
        MX = sb("MX", [P, RING, COLS], BF16)
        NM = sb("NM", [P, RING, 2])
        DG = sb("DG", [P, RING, 2, P], BF16)
        OS = sb("OS", [P, T])
        rec = sb("rec", [P, NT, HPG])
        AN = [sb(f"AN{a}", [P, NT, E]) for a in range(3)]
        ATT = sb("ATT", [E, T])
        Qrest, Krest = ATT, xn[:, :, :].rearrange("p t e -> p (t e)")
        arec = sb("arec", [P, 1])
        HB = sb("HB", [P, FT, T])
        EH, DF = HB[:, 0:2, :], HB[:, 2:4, :]
        PTA = HB[:, 0:len(A_UNITS), :]
        sq = sb("sq", [P, T], BF16)
        MID = sb("MID", [P, T])
        SEL = sb("SEL", [P, 2, PACK])
        LP = sb("LP", [P, NA])
        ch = sb("ch", [P, 8, NA])

        SB = ctx.enter_context(nc.psum_tensor("SB", [P, RING, 1024], F32))
        TB = ctx.enter_context(nc.psum_tensor("TB", [P, 1024], BF16))
        MB = ctx.enter_context(nc.psum_tensor("MB", [P, 512], F32))

        w_loaded = sem("w_loaded")
        prep_pe = sem("prep_pe")
        prep_dve = sem("prep_dve")
        prep_pool = sem("prep_pool")
        prep_step = sem("prep_step")
        prep_pool_step = sem("prep_pool_step")
        rel_loaded = sem("rel_loaded")
        clip_loaded = sem("clip_loaded")
        x_loaded = sem("x_loaded")
        stored = sem("stored")
        dve_step = sem("dve_step")
        pool_step = sem("pool_step")
        misc_filled = sem("misc_filled")
        misc_read = sem("misc_read")
        scores_ready = sem("scores_ready")
        colmax_ready = sem("colmax_ready")
        colmax_turned = sem("colmax_turned")
        rowmax_ready = sem("rowmax_ready")
        shift_ready = sem("shift_ready")
        scores_shifted = sem("scores_shifted")
        probs_ready = sem("probs_ready")
        normed = sem("normed")
        q_parts = sem("q_parts")
        k_parts = sem("k_parts")
        operands_in = sem("operands_in")
        wq_repeated = sem("wq_repeated")
        squared = sem("squared")
        loss_part = sem("loss_part")
        adapter_ready = sem("adapter_ready")

        class Walk:

            def __init__(self, sec, trip):
                self.sec, self.trip = sec, trip

            def n(self, ev, kind, back=0, times=1, before=0):
                return self.upto(ev.c.get(kind, 0) - back, kind, times, before)

            def upto(self, local, kind, times=1, before=0):
                v = (self.sec.base.get(kind, 0) + local) * times + before
                if self.trip is None:
                    return v
                assert v > 0, kind
                return self.trip * (self.sec.c[kind] * times) + v

            def ring(self, ev, kind, size):
                assert self.trip is None or self.sec.c[kind] % size == 0, (kind, self.sec.c[kind])
                return (self.sec.base.get(kind, 0) + ev.c[kind] - 1) % size

            def batch(self, b):
                return b if self.trip is None else self.trip + b

        def walk(eng, handlers):
            for sec in sections:
                if sec.trips == 1:
                    go = Walk(sec, None)
                    for ev in sec.events:
                        if ev.kind in handlers:
                            handlers[ev.kind](go, ev, *ev.args)
                else:
                    with eng.Fori(0, sec.trips) as trip:
                        go = Walk(sec, trip)
                        for ev in sec.events:
                            if ev.kind in handlers:
                                handlers[ev.kind](go, ev, *ev.args)

        def wait(eng, semaphore, value):
            if not isinstance(value, int) or value > 0:
                eng.wait_ge(semaphore, value)

        def unit(a, u):
            hg, hf, q = u // (2 * QU), u // QU % 2, u % QU
            if a == POS:
                h0, nh, i0, ni = HPG * hg, HPG, HT * hf + IB * q, IB
            elif a == FULL:
                h0, nh, i0, ni = HPG * hg + q, 1, HT * hf, HT
            else:
                h0, nh, i0, ni = HPG * hg + 2 * (q // 2), 2, HT * hf + P * (q % 2), P
            if a == WINDOW:
                t = i0 // P
                return h0, nh, i0, ni, {s: t - 1 + s for s in range(2) if t - 1 + s >= 0}
            return h0, nh, i0, ni, {s: s for s in range(NT)}

        def slot(r, nh=1):
            return SB[:, r, :].rearrange("p (t h i) -> p t h i", t=NT, h=nh)

        def pt(half):
            return PT[:, half % 2, :].rearrange("p (t h i) -> p t h i", t=NT, h=HPG)

        def operand(a, tensors):
            r0 = ROWS if a == FULL else 0
            return tensors[1 if a == WINDOW else 0], r0

        block = ctx.enter_context(nc.Block())

        @block.sync
        def _(sp):
            cuts = [0, OFF["onehot"][0], OFF["enc"][0], WCOLS]
            sp.dma_start(cidx_i[:, :], cidx).then_inc(w_loaded, 16)
            sp.dma_start(PREP, packed[:, WCOLS:]).then_inc(w_loaded, 16)
            for n in range(3):
                sp.dma_start(W[:, cuts[n]:cuts[n + 1]], packed[:, cuts[n]:cuts[n + 1]]).then_inc(w_loaded, 16)
            sp.wait_ge(prep_pool, 1)
            sp.dma_start(relpad, relrow).then_inc(stored, 16)
            sp.wait_ge(stored, 16)
            for a in range(16):
                y0 = 15 * TAPS - TAPS * a
                sp.dma_start(relwin[8 * a:8 * a + 8, :], relpad[:, y0:y0 + RWC]).then_inc(rel_loaded, 16)
            sp.wait_ge(prep_pool, 2)
            for s, part in enumerate(SLOTS_K):
                sp.dma_start(relclip_c[8 * s:8 * s + 8, :], relparts[:, part, :]).then_inc(clip_loaded, 16)

            def rows_of(ap):
                return ap.rearrange("o (t p) e -> p (o t) e", p=P)

            def load(go, ev, b):
                wait(sp, misc_read, go.n(ev, "misc"))
                src = x[b:b + 1] if go.trip is None else x[bass.ds(go.batch(b), 1), :, :]
                sp.dma_start(X["xin"][:, :, :], rows_of(src)).then_inc(x_loaded, 16)

            def place(a, part, slots, tensors, src):
                dst, r0 = operand(a, tensors)
                d = DHEAD[a]
                for s in range(6):
                    if slots[s] == part:
                        r = r0 + d * s
                        sp.dma_start(dst[r:r + d, :, :], src[0:d * H, part, :]).then_inc(operands_in, 16)

            def proj_q(go, ev, a):
                wait(sp, misc_read, go.n(ev, "misc"))
                place(a, 0, SLOTS_Q, QOs, Q3)

            def proj_k(go, ev, a):
                wait(sp, misc_read, go.n(ev, "misc"))
                place(a, 0, SLOTS_K, KOs, K3)

            def middle(go, ev, a):
                wait(sp, q_parts, go.n(ev, "middle", times=2, before=-1))
                place(a, 1, SLOTS_Q, QOs, Q3)
                wait(sp, k_parts, go.n(ev, "middle", times=2, before=-1))
                place(a, 1, SLOTS_K, KOs, K3)

            def low(go, ev, a):
                wait(sp, q_parts, go.n(ev, "low", times=2))
                place(a, 2, SLOTS_Q, QOs, Q3)
                wait(sp, k_parts, go.n(ev, "low", times=2))
                place(a, 2, SLOTS_K, KOs, K3)

            def store(go, ev, b, mark):
                wait(sp, misc_read, go.upto(mark, "misc"))
                dst = out[b:b + 1] if go.trip is None else out[bass.ds(go.batch(b), 1), :, :]
                sp.dma_start(rows_of(dst), X["xout"][:, :, :]).then_inc(stored, 16)

            walk(sp, {"load": load, "proj_q": proj_q, "proj_k": proj_k, "middle": middle, "low": low, "store": store})
            sp.wait_ge(stored, 16 * B + 16)

        @block.gpsimd
        def _(pool):
            pool.memset(ones_b[:, :], 1.0)
            pool.memset(ones_f[:, :], 1.0)
            pool.memset(zero_col[:, :], 0.0)
            for t in QOs + KOs:
                pool.memset(t[:, :, :], 0.0)
            for v in VO:
                pool.memset(v[:, :, :, :], 0.0)
            pool.memset(VA[:, :, :], 1.0)
            pool.memset(MID[:, :], 1.0)
            pool.memset(AN[FULL][:, :, :], 0.0)
            pool.memset(relclip_c[:, :], 0.0).then_inc(prep_pool_step, 1)
            pool.wait_ge(prep_pool_step, 1)
            for v in VO:
                pool.memset(v[:, :, :, 8:9], 1.0)
            pool.wait_ge(w_loaded, 16 * 5)
            rel = w("relT", 8)
            pool.tensor_copy(relrow[:, 0:MAXLEN], rel[:, 0:1].broadcast_to([8, MAXLEN]))
            pool.tensor_copy(relrow[:, MAXLEN:MAXLEN + NREL], rel)
            pool.tensor_copy(relrow[:, MAXLEN + NREL:RTL], rel[:, NREL - 1:NREL].broadcast_to([8, RTL - MAXLEN - NREL])
                             ).then_inc(prep_pool, 1)
            ends = rel[:, 0:NREL:NREL - 1]
            pool.tensor_copy(relparts[:, 0, :], ends).then_inc(prep_pool_step, 1)
            pool.wait_ge(prep_pool_step, 2)
            pool.tensor_tensor(relrest[:, :], ends, relparts[:, 0, :], ALU.subtract).then_inc(prep_pool_step, 1)
            pool.wait_ge(prep_pool_step, 3)
            pool.tensor_copy(relparts[:, 1, :], relrest[:, :]).then_inc(prep_pool_step, 1)
            pool.wait_ge(prep_pool_step, 4)
            pool.tensor_tensor(relparts[:, 2, :], relrest[:, :], relparts[:, 1, :], ALU.subtract
                               ).then_inc(prep_pool, 1)
            pool.wait_ge(clip_loaded, 16 * 6)
            pool.tensor_copy(relclip[:, :, :], relclip_c[:, :].unsqueeze(2).broadcast_to([ROWS, 2, P])
                             ).then_inc(prep_pool, 1)

            def rest(go, ev, a, mark):
                k = slice(0, DHEAD[a] * H)
                pool.wait_ge(misc_read, go.upto(mark, "misc"))
                pool.tensor_tensor(Krest[k, :], KF[k, :], K3[k, 0, :], ALU.subtract).then_inc(pool_step, 1)

            def middle(go, ev, a):
                k = slice(0, DHEAD[a] * H)
                pool.tensor_tensor(K3[k, 1, :], KF[k, :], K3[k, 0, :], ALU.subtract).then_inc(k_parts, 1)

            def low(go, ev, a):
                k = slice(0, DHEAD[a] * H)
                pool.wait_ge(pool_step, go.n(ev, "pool"))
                pool.wait_ge(k_parts, go.n(ev, "low", times=2, before=-1))
                pool.tensor_tensor(K3[k, 2, :], Krest[k, :], K3[k, 1, :], ALU.subtract).then_inc(k_parts, 1)

            def repeat(go, ev, hg):
                pool.wait_ge(misc_filled, go.n(ev, "misc"))
                pool.tensor_tensor(
                    WR[:, :, :, :],
                    w("wqn0")[:, 32 * hg:32 * hg + 32].rearrange("p (h d) -> p h d", h=HPG).unsqueeze(2)
                    .broadcast_to([P, HPG, 16, 8]),
                    ones_f[:, :].rearrange("p (a d) -> p a d", a=16).unsqueeze(1).broadcast_to([P, HPG, 16, 8]),
                    ALU.mult).then_inc(wq_repeated, 1)

            def hidden(go, ev, t):
                pool.wait_ge(misc_read, go.n(ev, "misc"))
                pool.tensor_tensor(HB[:, t, :], HB[:, t, :], HB[:, t, :], ALU.mult).then_inc(squared, 1)

            walk(pool, {"rest": rest, "middle": middle, "low": low, "repeat": repeat, "hidden": hidden})

        @block.tensor
        def _(pe):
            idf = w("ident")
            pe.wait_ge(prep_dve, 1)
            for t in range(FT):
                ins = pe.transpose(SB[:, 0, P * t:P * t + P], TERN[:, 0, P * t:P * t + P], idf)
            ins.then_inc(prep_pe, 1)
            pe.wait_ge(prep_dve, 2)
            for t in range(FT):
                ins = pe.transpose(SB[:, 1, P * t:P * t + P], TERN[:, 1, P * t:P * t + P], idf)
            ins.then_inc(prep_pe, 1)
            pe.matmul(SB[0:RANK, 2, 0:HID], w("fast_b", RANK), w("uT", RANK), start=True, stop=True).then_inc(prep_pe, 1)
            pe.wait_ge(prep_dve, 3)
            pe.matmul(SB[:, 2, 512:1024], w("v", RANK), TERN[0:RANK, 2, :], start=True, stop=True).then_inc(prep_pe, 1)
            pe.wait_ge(prep_dve, 4)
            pe.wait_ge(prep_pool, 3)
            pe.wait_ge(rel_loaded, 16 * 16)
            pe.matmul(MB[:, :], ident_b[:, :], QOs[0][:, 0, :], start=True, stop=True)

            def take(go, ev):
                wait(pe, misc_read, go.n(ev, "misc", back=1))

            def scores(go, ev, what, *args):
                r = go.ring(ev, "scores", RING)
                before = args[-2]
                if before:
                    pe.wait_ge(probs_ready, go.upto(before[0] + 1 - before[1], "banks"))
                if args[-1]:
                    wait(pe, misc_read, go.upto(args[-1], "misc"))
                if what == "a":
                    first = True
                    for it, c0, n in A_UNITS[args[0]]:
                        for j in range(n):
                            pe.matmul(SB[:, r, P * (c0 + j):P * (c0 + j) + P], KF[:, P * j:P * j + P],
                                      QF[:, P * it:P * it + P], start=first, stop=False, skip_group_check=True)
                            first = False
                        c = P * (c0 + n - 1)
                        ins = pe.matmul(SB[:, r, c:c + P], ident_b[:, :], masks[:, 1, :], start=False, stop=False,
                                        skip_group_check=True)
                    ins.then_inc(scores_ready, 1)
                    return
                a, u = args[0:2]
                h0, nh, i0, ni, tiles = unit(a, u)
                if u == 0:
                    pe.wait_ge(operands_in, go.n(ev, "low", times=12 * 16))
                qo, r0 = operand(a, QOs)
                ko, _ = operand(a, KOs)
                sc = slot(r, nh)
                begun = set()
                for s, jt in tiles.items():
                    pe_bank = s * COLS // 512
                    if pe_bank == 1 and pe_bank not in begun and before and before[1] == 2:
                        pe.wait_ge(probs_ready, go.upto(before[0], "banks"))
                    for h in range(nh):
                        ins = pe.matmul(sc[:, s, h, :], ko[r0:r0 + ROWS, h0 + h, P * jt:P * jt + P],
                                        qo[r0:r0 + ROWS, h0 + h, i0:i0 + ni], start=pe_bank not in begun, stop=False,
                                        skip_group_check=True)
                        begun.add(pe_bank)
                    if a == POS:
                        dl = i0 - P * jt
                        if dl in DELTAS:
                            il = i0 % HT
                            for c in range(TAPS):
                                y = DELTAS[0] + TAPS - 1 - dl - c
                                ins = pe.matmul(sc[:, s, :, c:IB:TAPS], relwin[:, y:y + P],
                                                QH[:, u // QU % 2, :, il + c:il + IB:TAPS],
                                                start=False, stop=False, skip_group_check=True)
                        else:
                            ins = pe.matmul(sc[:, s, :, :], relclip[:, 0 if dl > 0 else 1, :],
                                            qo[0:ROWS, h0:h0 + nh, i0:i0 + ni],
                                            start=False, stop=False, skip_group_check=True)
                    if a == WINDOW:
                        ins = pe.matmul(sc[:, s, :, :], ident_b[:, :], masks[:, s:s + 1, :].broadcast_to([P, nh, P]),
                                        start=False, stop=False, skip_group_check=True)
                ins.then_inc(scores_ready, 1)

            def turn(go, ev, what, *args):
                r = go.ring(ev, "turn", RING)
                pe.wait_ge(colmax_ready, go.n(ev, "turn"))
                wait(pe, rowmax_ready, go.n(ev, "turn", back=1))
                for q in range(len(A_UNITS[args[0]]) if what == "a" else 2):
                    ins = pe.transpose(TB[:, P * q:P * q + P], MX[:, r, P * q:P * q + P], ident_b[:, :])
                ins.then_inc(colmax_turned, 1)

            def shift(go, ev, what, *args):
                r = go.ring(ev, "shift", RING)
                pe.wait_ge(shift_ready, go.n(ev, "shift"))
                if what == "a":
                    for n_, (it, c0, n) in enumerate(A_UNITS[args[0]]):
                        ins = pe.matmul(SB[:, r, P * c0:P * (c0 + n)], ones_b[:, :],
                                        DG[:, r, n_:n_ + 1, :].broadcast_to([P, n, P]), start=False, stop=True,
                                        skip_group_check=True)
                    ins.then_inc(scores_shifted, 1)
                    return
                tiles = sorted(unit(*args)[4])
                row = DG[:, r, :, :].rearrange("p q i -> p (q i)").unsqueeze(1)
                for s in range(tiles[0], tiles[-1] + 1, 2):
                    n = min(2, tiles[-1] + 1 - s)
                    pe.matmul(SB[:, r, COLS * s:COLS * (s + n)], ones_b[:, :], row.broadcast_to([P, n, COLS]),
                              start=False, stop=True, skip_group_check=True).then_inc(scores_shifted, 1)

            def a_v(go, ev):
                take(go, ev)
                for t in range(NT):
                    ins = pe.matmul(MB[:, P * t:P * t + P], xnT["xnT"][:, P * t:P * t + P], w("wv_a"), start=True, stop=True)
                ins.then_inc(misc_filled, 1)

            def a_q(go, ev):
                take(go, ev)
                pe.matmul(MB[:, :], w("wq_a"), xnT["xnT"][:, :], start=True, stop=True).then_inc(misc_filled, 1)

            def a_k(go, ev):
                take(go, ev)
                pe.matmul(MB[:, :], w("wk_a"), xnT["xnT"][:, :], start=True, stop=True).then_inc(misc_filled, 1)

            def a_out(go, ev, it, mark):
                take(go, ev)
                pe.wait_ge(probs_ready, go.upto(mark, "banks"))
                ui, c0, n = next((i, s[1], s[2]) for i, segs in enumerate(A_UNITS) for s in segs if s[0] == it)
                for j in range(n):
                    ins = pe.matmul(MB[:, 0:E + 2], PTA[:, ui, P * (c0 + j):P * (c0 + j) + P], VA[:, j, :],
                                    start=(j == 0), stop=(j == n - 1))
                ins.then_inc(misc_filled, 1)

            def source(a):
                return (xnT["xnT0"] if a == POS else xnT["xnT"]), (E if a != FULL else E // 2)

            def proj_q(go, ev, a):
                take(go, ev)
                src, ein = source(a)
                pe.matmul(MB[:, :], w(f"wq{a}", ein), src[0:ein, :], start=True, stop=True).then_inc(misc_filled, 1)

            def proj_k(go, ev, a):
                take(go, ev)
                src, ein = source(a)
                pe.matmul(MB[:, :], w(f"wk{a}", ein), src[0:ein, :], start=True, stop=True).then_inc(misc_filled, 1)

            def proj_v(go, ev, a):
                take(go, ev)
                src, ein = source(a)
                rows = DHEAD[a] * H
                for t in range(NT):
                    ins = pe.matmul(MB[:, rows * t:rows * t + rows], src[0:ein, P * t:P * t + P], w(f"wv{a}", ein),
                                    start=True, stop=True)
                ins.then_inc(misc_filled, 1)

            def spread(go, ev, half, pair):
                take(go, ev)
                pe.wait_ge(wq_repeated, go.n(ev, "repeat"))
                for n in range(2):
                    ins = pe.matmul(MB[:, HT * n:HT * n + HT], WR[:, 2 * pair + n, :, :].rearrange("p a d -> p (a d)"),
                                    xnT["xnT0"][:, HT * (half % 2):HT * (half % 2) + HT], start=True, stop=True)
                ins.then_inc(misc_filled, 1)

            def weigh(go, ev, a, half, mark):
                take(go, ev)
                pe.wait_ge(probs_ready, go.upto(mark, "banks"))
                pr, h0 = pt(half), HPG * (half // 2)
                if a == WINDOW:
                    parts = [(P * n, P, s, t - 1 + s, s == max(0, 1 - t), s == 1)
                             for n, t in enumerate((2 * (half % 2), 2 * (half % 2) + 1)) for s in range(max(0, 1 - t), 2)]
                else:
                    parts = [(0, HT, j, j, j == 0, j == NT - 1) for j in range(NT)]
                for c0, n, s, jt, st, en in parts:
                    for h in range(HPG):
                        ins = pe.matmul(MB[32 * h:32 * h + VC, c0:c0 + n], VO[a][:, jt, h0 + h, :],
                                        pr[:, s, h, c0:c0 + n], start=st, stop=en)
                ins.then_inc(misc_filled, 1)

            def renorm(go, ev, a, hg):
                take(go, ev)
                for t in range(NT):
                    ins = pe.transpose(MB[:, P * t:P * t + P], OS[:, P * t:P * t + P], idf)
                ins.then_inc(misc_filled, 1)

            def unturn(go, ev, a):
                take(go, ev)
                for t in range(NT):
                    ins = pe.transpose(MB[:, P * t:P * t + P], AN[a][:, t, :], idf)
                ins.then_inc(misc_filled, 1)

            def outproj(go, ev, a, dst):
                take(go, ev)
                for t in range(NT):
                    ins = pe.matmul(MB[:, E * t:E * t + E], ATT[:, P * t:P * t + P], w(f"wo{a}"), start=True, stop=True)
                ins.then_inc(misc_filled, 1)

            def turnx(go, ev, dst):
                take(go, ev)
                pe.wait_ge(normed, go.n(ev, "normalise"))
                for t in range(NT):
                    ins = pe.transpose(MB[:, P * t:P * t + P], xn[:, t, :], idf)
                ins.then_inc(misc_filled, 1)

            def hidden(go, ev, t):
                take(go, ev)
                pe.matmul(MB[:, :], Wfc[:, P * t:P * t + P], xnT["xnT"][:, :], start=True, stop=True
                          ).then_inc(misc_filled, 1)

            def ffn_out(go, ev, dst, *_):
                take(go, ev)
                pe.wait_ge(squared, go.n(ev, "hidden"))
                for t in range(NT):
                    for c in range(FT):
                        ins = pe.matmul(MB[:, E * t:E * t + E], HB[:, c, P * t:P * t + P], Wpr[:, c, :],
                                        start=(c == 0), stop=(c == FT - 1))
                ins.then_inc(misc_filled, 1)

            def enc(go, ev, c):
                take(go, ev)
                pe.matmul(MB[:, :], w("enc")[:, P * c:P * c + P], xnT["xnT"][:, :], start=True, stop=True
                          ).then_inc(misc_filled, 1)

            def dec(go, ev, n):
                take(go, ev)
                pe.matmul(MB[:, :], w("dec")[:, E * n:E * n + E], EH[:, n // 4, :], start=True, stop=True
                          ).then_inc(misc_filled, 1)

            def total(go, ev):
                take(go, ev)
                pe.wait_ge(loss_part, go.n(ev, "dec"))
                pe.matmul(MB[:, 0:NA], ones_f[:, :], LP[:, :], start=True, stop=True).then_inc(misc_filled, 1)

            def down(go, ev):
                take(go, ev)
                pe.wait_ge(adapter_ready, go.n(ev, "selected"))
                pe.matmul(MB[0:AR, :], SEL[:, (NA - 1) % 2, 0:AR], xnT["xnT"][:, :], start=True, stop=True
                          ).then_inc(misc_filled, 1)

            def up(go, ev, dst, *_):
                take(go, ev)
                for t in range(NT):
                    pe.matmul(MB[:, E * t:E * t + E], xnT["xnT"][:, P * t:P * t + P], w("w_base"), start=True, stop=False)
                    ins = pe.matmul(MB[:, E * t:E * t + E], MID[:, P * t:P * t + P], SEL[:, (NA - 1) % 2, AR:AR + E],
                                    start=False, stop=True)
                ins.then_inc(misc_filled, 1)

            walk(pe, {"scores": scores, "turn": turn, "shift": shift, "a_v": a_v, "a_q": a_q, "a_k": a_k, "a_out": a_out,
                      "proj_q": proj_q, "proj_k": proj_k, "proj_v": proj_v, "spread": spread, "weigh": weigh,
                      "renorm": renorm, "unturn": unturn, "outproj": outproj, "turnx": turnx, "hidden": hidden,
                      "ffn_out": ffn_out, "enc": enc, "dec": dec, "total": total, "down": down, "up": up})

        @block.scalar
        def _(act):
            act.wait_ge(w_loaded, 16 * 5)
            act.wait_ge(prep_pool, 3)

            def shift(go, ev, what, *args):
                r = go.ring(ev, "shift", RING)
                if what == "a":
                    act.wait_ge(scores_shifted, go.n(ev, "banks"))
                    cols = P * sum(n for _, _, n in A_UNITS[args[0]])
                    act.activation(PTA[:, args[0], 0:cols], SB[:, r, 0:cols], ACT.Exp, scale=float(E) ** -0.5
                                   ).then_inc(probs_ready, 1)
                    return
                a, u = args
                h0, nh, i0, ni, tiles = unit(a, u)
                lo, hi = min(tiles), max(tiles) + 1
                il, hl = i0 % HT, h0 % HPG
                banks = banks_of((what, a, u))
                parts = [(lo, hi)] if a != FULL else [(0, 2), (2, 4)]
                for n, (lo, hi) in enumerate(parts):
                    act.wait_ge(scores_shifted, go.n(ev, "banks", back=len(parts) - 1 - n))
                    act.activation(pt(u // QU)[:, lo:hi, hl:hl + nh, il:il + ni], slot(r, nh)[:, lo:hi, :, :], ACT.Exp,
                                   scale=8.0 ** -0.5).then_inc(probs_ready, banks // len(parts))

            def copy_out(go, ev, dst, src, func=ACT.Copy, **kw):
                act.wait_ge(misc_filled, go.n(ev, "misc"))
                act.activation(dst, src, func, **kw).then_inc(misc_read, 1)

            def a_q(go, ev):
                copy_out(go, ev, QF[:, :], MB[:, :], ACT.Identity, bias=w("bq_a"))

            def a_k(go, ev):
                copy_out(go, ev, KF[:, :], MB[:, :], ACT.Identity, bias=w("bk_a"))

            def both(go, ev, full, high, a, bias):
                rows = DHEAD[a] * H
                bias = w(bias) if a != FULL else zero_col[0:rows, :]
                act.wait_ge(misc_filled, go.n(ev, "misc"))
                act.activation(full[0:rows, :], MB[0:rows, :], ACT.Identity, bias=bias)
                act.activation(high[0:rows, 0, :], MB[0:rows, :], ACT.Identity, bias=bias).then_inc(misc_read, 1)

            def proj_q(go, ev, a):
                both(go, ev, QF, Q3, a, f"bq{a}")

            def proj_k(go, ev, a):
                both(go, ev, KF, K3, a, f"bk{a}")

            def weigh(go, ev, a, half, mark):
                copy_out(go, ev, OS[:, HT * (half % 2):HT * (half % 2) + HT], MB[:, 0:HT])

            def unturn(go, ev, a):
                copy_out(go, ev, ATT[:, :], MB[:, :])

            def turnx(go, ev, dst):
                copy_out(go, ev, xnT[dst][:, :], MB[:, :])

            def hidden(go, ev, t):
                copy_out(go, ev, HB[:, t, :], MB[:, :], ACT.Relu)

            def enc(go, ev, c):
                copy_out(go, ev, EH[:, c, :], MB[:, :], ACT.Relu, bias=w("b_enc")[:, c:c + 1])

            def dec(go, ev, n):
                act.wait_ge(misc_read, go.n(ev, "misc"))
                wait(act, loss_part, go.n(ev, "dec", back=1))
                act.activation(sq[:, :], DF[:, n % 2, :], ACT.Square, accum_out=LP[:, n:n + 1]).then_inc(loss_part, 1)

            def down(go, ev):
                copy_out(go, ev, MID[0:AR, :], MB[0:AR, :], ACT.Relu, bias=SEL[0:AR, (NA - 1) % 2, PACK - 1:PACK])

            walk(act, {"shift": shift, "a_q": a_q, "a_k": a_k, "proj_q": proj_q, "proj_k": proj_k, "weigh": weigh,
                       "unturn": unturn, "turnx": turnx, "hidden": hidden, "enc": enc, "dec": dec, "down": down})

        @block.vector
        def _(dve):
            dve.wait_ge(w_loaded, 16 * 5)
            steps = [0]

            def done(ins):
                steps[0] += 1
                ins.then_inc(prep_step, 1)

            def plink(ins):
                done(ins)
                dve.wait_ge(prep_step, steps[0])

            dve.tensor_copy(ident_b[:, :], w("ident"))
            done(dve.tensor_scalar(negident_b[:, :], w("ident"), -1.0, None, ALU.mult))
            dve.tensor_copy(masks[:, 0, :], w("keep0"))
            dve.tensor_copy(masks[:, 1, :], w("keep1"))
            plink(dve.tensor_copy(cidx_f[:, :], cidx_i[:, :]))
            plink(dve.tensor_scalar(wrap[:, :], cidx_f[:, :], 0.0, float(NA), ALU.is_lt, ALU.mult))
            plink(dve.tensor_tensor(cidx_f[:, :], cidx_f[:, :], wrap[:, :], ALU.add))
            plink(dve.tensor_scalar(cidx_f[:, :], cidx_f[:, :], 0.0, float(NA - 1), ALU.max, ALU.min))

            def ternary(src, dst, blocks, width, at):
                mag = TERN[:, 3, :].rearrange("p (t i) -> p t i", t=blocks)
                low = TERN[:, 4, :].rearrange("p (t i) -> p t i", t=blocks)
                scale_, half, nhalf = ch[:, at, 0:blocks], ch[:, 1 + at, 0:blocks], ch[:, 2 + at, 0:blocks]
                plink(dve.scalar_tensor_tensor(out=mag, in0=src, scalar=-1.0, in1=src, op0=ALU.mult, op1=ALU.max))
                plink(dve.tensor_reduce(scale_, mag, AX.X, ALU.add))
                plink(dve.tensor_scalar(scale_, scale_, 1.0 / width, EPS, ALU.mult, ALU.max))
                done(dve.tensor_scalar(half, scale_, 0.5, None, ALU.mult))
                plink(dve.tensor_scalar(nhalf, scale_, -0.5, None, ALU.mult))
                for t in range(blocks):
                    done(dve.tensor_scalar(mag[:, t, :], src[:, t, :], half[:, t:t + 1], None, ALU.is_gt))
                    plink(dve.tensor_scalar(low[:, t, :], src[:, t, :], nhalf[:, t:t + 1], None, ALU.is_lt))
                plink(dve.tensor_tensor(mag, mag, low, ALU.subtract))
                plink(dve.tensor_tensor(mag, mag, src, ALU.subtract))
                plink(dve.tensor_tensor(mag, mag, src, ALU.add))
                for t in range(blocks):
                    ins = dve.tensor_scalar(dst[:, t, :], mag[:, t, :], scale_[:, t:t + 1], None, ALU.mult)
                    if t < blocks - 1:
                        done(ins)
                return ins

            ternary(w("w_fc").rearrange("p (t i) -> p t i", t=FT), TERN[:, 0, :].rearrange("p (t i) -> p t i", t=FT),
                    FT, E, 0).then_inc(prep_dve, 1)
            dve.wait_ge(prep_dve, 1)
            ternary(w("w_proj").rearrange("p (t i) -> p t i", t=1), TERN[:, 1, :].rearrange("p (t i) -> p t i", t=1),
                    1, HID, 3).then_inc(prep_dve, 1)
            dve.wait_ge(prep_pe, 3)
            done(dve.tensor_copy(Wfc[:, :], SB[:, 0, 0:HID]))
            done(dve.tensor_copy(Wpr[:, :, :], SB[:, 1, 0:HID].rearrange("p (t i) -> p t i", t=FT)))
            dve.tensor_copy(TERN[0:RANK, 2, :], SB[0:RANK, 2, 0:HID]).then_inc(prep_dve, 1)
            dve.wait_ge(prep_pe, 4)
            dve.wait_ge(prep_step, steps[0])
            dve.scalar_tensor_tensor(out=Wfc[:, :], in0=SB[:, 2, 512:1024], scalar=w("gate"), in1=Wfc[:, :],
                                     op0=ALU.mult, op1=ALU.add).then_inc(prep_dve, 1)

            def step(ins):
                ins.then_inc(dve_step, 1)

            def settle(go, ev, back=0):
                wait(dve, dve_step, go.n(ev, "dve", back=back))

            def filled(go, ev):
                dve.wait_ge(misc_filled, go.n(ev, "misc"))

            def scores(go, ev, what, *args):
                r = go.ring(ev, "scores", RING)
                dve.wait_ge(scores_ready, go.n(ev, "scores"))
                if what == "a":
                    segs = [(P * i, SB[:, r, P * c0:P * (c0 + n)], n, P) for i, (_, c0, n) in enumerate(A_UNITS[args[0]])]
                else:
                    tiles = unit(*args[0:2])[4]
                    lo, n = min(tiles), len(tiles)
                    segs = [(0, SB[:, r, COLS * lo:COLS * (lo + n)], n, COLS)]
                for o, src, n, cols in segs:
                    if n == 1:
                        ins = dve.tensor_copy(MX[:, r, o:o + cols], src)
                    else:
                        ins = dve.tensor_reduce(MX[:, r, o:o + cols], src.rearrange("p (t c) -> p c t", t=n), AX.X, ALU.max)
                ins.then_inc(colmax_ready, 1)

            def turn(go, ev, what, *args):
                r = go.ring(ev, "turn", RING)
                q = len(A_UNITS[args[0]]) if what == "a" else 2
                dve.wait_ge(colmax_turned, go.n(ev, "turn"))
                dve.tensor_reduce(NM[:, r, 0:q], TB[:, 0:P * q].rearrange("p (q j) -> p q j", q=q), AX.X, ALU.max
                                  ).then_inc(rowmax_ready, 1)
                dve.wait_ge(rowmax_ready, go.n(ev, "turn"))
                for i in range(q):
                    ins = dve.tensor_scalar(DG[:, r, i, :], negident_b[:, :], NM[:, r, i:i + 1], None, ALU.mult)
                ins.then_inc(shift_ready, 1)

            def norm_a(go, ev, src, mark):
                if src == "xin":
                    dve.wait_ge(x_loaded, go.n(ev, "load", times=16))
                else:
                    dve.wait_ge(misc_read, go.upto(mark, "misc"))
                for t in range(NT):
                    step(dve.bn_stats(stats[:, t, :], X[src][:, t, :]))

            def norm_b(go, ev):
                settle(go, ev, NT)
                dve.tensor_copy(fence[:, :], w("ident")[:, 0:1])
                for t in range(NT):
                    step(dve.bn_aggr(mv[:, t, :], stats[:, t, :]))

            def norm_c(go, ev):
                settle(go, ev, 4)
                step(dve.tensor_scalar(nhvar[:, :], mv[:, :, 1], EPS, -0.5, ALU.add, ALU.mult))
                step(dve.tensor_scalar(var[:, :], mv[:, :, 1], EPS, None, ALU.add))
                settle(go, ev, 2)
                step(dve.tensor_scalar(rs[0][:, :].bitcast(I32), var[:, :].bitcast(I32), 1, None, ALU.logical_shift_right))
                settle(go, ev, 1)
                step(dve.tensor_scalar(rs[1][:, :].bitcast(I32), rs[0][:, :].bitcast(I32), -1.0, float(0x5F3759DF),
                                       ALU.mult, ALU.add))

            def newton(go, ev, it):
                old, new = rs[(it + 1) % 2], rs[it % 2]
                settle(go, ev, 3)
                step(dve.tensor_tensor(nt[0][:, :], old[:, :], old[:, :], ALU.mult))
                settle(go, ev, 2)
                step(dve.tensor_tensor(nt[1][:, :], nt[0][:, :], nhvar[:, :], ALU.mult))
                settle(go, ev, 1)
                step(dve.scalar_tensor_tensor(out=new[:, :], in0=nt[1][:, :], scalar=1.5, in1=old[:, :],
                                              op0=ALU.add, op1=ALU.mult))

            def normalise(go, ev, src):
                settle(go, ev)
                wait(dve, k_parts, go.n(ev, "low", times=2))
                for t in range(NT):
                    ins = dve.tensor_scalar(xn[:, t, :], X[src][:, t, :], mv[:, t, 0:1], rs[0][:, t:t + 1],
                                            ALU.subtract, ALU.mult)
                ins.then_inc(normed, 1)

            def rest(go, ev, a, mark):
                q = slice(0, DHEAD[a] * H)
                dve.wait_ge(misc_read, go.upto(mark, "misc"))
                step(dve.tensor_tensor(Qrest[q, :], QF[q, :], Q3[q, 0, :], ALU.subtract))

            def middle(go, ev, a):
                q = slice(0, DHEAD[a] * H)
                dve.tensor_tensor(Q3[q, 1, :], QF[q, :], Q3[q, 0, :], ALU.subtract).then_inc(q_parts, 1)

            def low(go, ev, a):
                q = slice(0, DHEAD[a] * H)
                settle(go, ev)
                dve.wait_ge(q_parts, go.n(ev, "low", times=2, before=-1))
                dve.tensor_tensor(Q3[q, 2, :], Qrest[q, :], Q3[q, 1, :], ALU.subtract).then_inc(q_parts, 1)

            def a_v(go, ev):
                filled(go, ev)
                dve.tensor_tensor(VA[:, :, 0:E], MB[:, :].rearrange("p (t e) -> p t e", t=NT),
                                  w("bv_a").unsqueeze(1).broadcast_to([P, NT, E]), ALU.add).then_inc(misc_read, 1)

            def a_out(go, ev, it, mark):
                filled(go, ev)
                step(dve.reciprocal(arec[:, :], MB[:, E:E + 1]))
                settle(go, ev)
                dve.scalar_tensor_tensor(out=X["xa"][:, it, :], in0=MB[:, 0:E], scalar=arec[:, :],
                                         in1=X["xin"][:, it, :], op0=ALU.mult, op1=ALU.add).then_inc(misc_read, 1)

            def proj_v(go, ev, a):
                filled(go, ev)
                d = DHEAD[a]
                src = MB[:, 0:NT * H * d].rearrange("p (t h d) -> p t h d", t=NT, h=H)
                if a == FULL:
                    ins = dve.tensor_copy(VO[a][:, :, :, 0:d], src)
                else:
                    bv = w(f"bv{a}").rearrange("p (h d) -> p h d", h=H).unsqueeze(1).broadcast_to([P, NT, H, d])
                    ins = dve.tensor_tensor(VO[a][:, :, :, 0:d], src, bv, ALU.add)
                ins.then_inc(misc_read, 1)

            def spread(go, ev, half, pair):
                filled(go, ev)
                for n in range(2):
                    h = HPG * (half // 2) + 2 * pair + n
                    ins = dve.scalar_tensor_tensor(out=QH[:, half % 2, 2 * pair + n, :].rearrange("p (k i) -> p k i", i=IB),
                                                   in0=MB[:, HT * n:HT * n + HT].rearrange("p (k i) -> p k i", i=IB),
                                                   scalar=w("bqr0")[:, h:h + 1],
                                                   in1=w("onehot").unsqueeze(1).broadcast_to([P, HT // IB, IB]),
                                                   op0=ALU.add, op1=ALU.mult)
                ins.then_inc(misc_read, 1)

            def renorm(go, ev, a, hg):
                filled(go, ev)
                d = DHEAD[a]
                src = MB[:, :].rearrange("p (t h c) -> p t h c", t=NT, h=HPG)
                step(dve.reciprocal(rec[:, :, :], src[:, :, :, 8]))
                settle(go, ev)
                dve.tensor_tensor(AN[a][:, :, HPG * d * hg:HPG * d * (hg + 1)].rearrange("p t (h d) -> p t h d", h=HPG),
                                  src[:, :, :, 0:d], rec[:, :, :].unsqueeze(3).broadcast_to([P, NT, HPG, d]), ALU.mult
                                  ).then_inc(misc_read, 1)

            def bias(go, ev, a, src, dst):
                if dst == "xout":
                    wait(dve, stored, go.n(ev, "store", times=16, before=16))
                step(dve.tensor_tensor(X[dst][:, :, :], X[src][:, :, :], w(f"bo{a}").unsqueeze(1).broadcast_to([P, NT, E]),
                                       ALU.add))

            def add(go, ev, dst):
                filled(go, ev)
                dve.tensor_tensor(X[dst][:, :, :], X[dst][:, :, :], MB[:, :].rearrange("p (t e) -> p t e", t=NT), ALU.add
                                  ).then_inc(misc_read, 1)

            def outproj(go, ev, a, dst):
                settle(go, ev)
                add(go, ev, dst)

            def ffn_out(go, ev, dst):
                add(go, ev, dst)

            def dec(go, ev, n):
                filled(go, ev)
                wait(dve, loss_part, go.n(ev, "dec", back=2))
                dve.scalar_tensor_tensor(out=DF[:, n % 2, :], in0=MB[:, :], scalar=w("b_dec")[:, n:n + 1],
                                         in1=xnT["xnT"][:, :], op0=ALU.add, op1=ALU.subtract).then_inc(misc_read, 1)

            loss, least, later, first_, hot, picked, cid, hot2 = (ch[:, i, :] for i in range(8))

            def total(go, ev):
                filled(go, ev)
                dve.tensor_copy(loss, MB[:, 0:NA]).then_inc(misc_read, 1)

            def pick(go, ev, n, mark):
                if n == 1:
                    dve.wait_ge(misc_read, go.upto(mark, "misc"))
                    step(dve.tensor_reduce(least[:, 0:1], loss, AX.X, ALU.min))
                    return
                settle(go, ev, 1)
                if n == 2:
                    step(dve.tensor_scalar(later, loss, least[:, 0:1], float(2 * NA), ALU.is_gt, ALU.mult))
                if n == 3:
                    step(dve.tensor_tensor(picked, later, w("iota"), ALU.add))
                if n == 4:
                    step(dve.tensor_reduce(first_[:, 0:1], picked, AX.X, ALU.min))
                if n == 5:
                    step(dve.tensor_scalar(hot, w("iota"), first_[:, 0:1], None, ALU.is_equal))
                if n == 6:
                    step(dve.tensor_tensor(picked, hot, cidx_f[:, :], ALU.mult))
                if n == 7:
                    step(dve.tensor_reduce(cid[:, 0:1], picked, AX.X, ALU.add))
                if n == 8:
                    step(dve.tensor_scalar(hot2, w("iota"), cid[:, 0:1], None, ALU.is_equal))

            packs = w("pack").rearrange("p (n c) -> p n c", n=NA)

            def select(go, ev, n):
                settle(go, ev, 1)
                if n == 0:
                    step(dve.tensor_scalar(SEL[:, 0, :], packs[:, 0, :], hot2[:, 0:1], None, ALU.mult))
                else:
                    step(dve.scalar_tensor_tensor(out=SEL[:, n % 2, :], in0=packs[:, n, :], scalar=hot2[:, n:n + 1],
                                                  in1=SEL[:, (n - 1) % 2, :], op0=ALU.mult, op1=ALU.add))

            def selected(go, ev):
                settle(go, ev)
                n = NA - 1
                dve.scalar_tensor_tensor(out=SEL[:, n % 2, :], in0=packs[:, n, :], scalar=hot2[:, n:n + 1],
                                         in1=SEL[:, (n - 1) % 2, :], op0=ALU.mult, op1=ALU.add).then_inc(adapter_ready, 1)

            def up(go, ev, dst):
                add(go, ev, dst)

            walk(dve, {"scores": scores, "turn": turn, "norm_a": norm_a, "norm_b": norm_b, "norm_c": norm_c,
                       "newton": newton, "normalise": normalise, "rest": rest, "middle": middle, "low": low, "a_v": a_v,
                       "a_out": a_out, "proj_v": proj_v, "spread": spread, "renorm": renorm, "bias": bias,
                       "outproj": outproj, "ffn_out": ffn_out, "dec": dec, "total": total, "pick": pick,
                       "select": select, "selected": selected, "up": up})


def layout(i):
    import numpy as np

    f = np.float32
    s = {}
    r = np.arange(P)
    s["ident"] = np.eye(P, dtype=f)
    s["keep1"] = np.where(r[:, None] <= r[None, :], 0, NEG).astype(f)
    s["keep0"] = np.where(r[:, None] >= r[None, :], 0, NEG).astype(f)
    s["onehot"] = ((np.arange(IB)[None, :] // TAPS) % 16 == r[:, None] // 8).astype(f)
    s["iota"] = np.broadcast_to(np.arange(NA, dtype=f), (P, NA))
    rep = lambda v: np.broadcast_to(v, (P,) + v.shape[-1:])
    s["gate"] = rep(i["L0_ffn_gate"].reshape(1, 1))
    s["w_fc"] = i["L0_ffn_w_fc"].reshape(FT, P, E).transpose(1, 0, 2).reshape(P, FT * E)
    s["w_proj"] = i["L0_ffn_w_proj"]
    s["fast_b"], s["uT"], s["v"] = i["L0_ffn_fast_b"], i["L0_ffn_u"].T, i["L0_ffn_v"]
    for n in "qk":
        s[f"w{n}_a"] = i[f"L0_attn_a_W{n}"].T
        s[f"b{n}_a"] = i[f"L0_attn_a_b{n}"][:, None]
    s["wv_a"], s["bv_a"] = i["L0_attn_a_Wv"].T, rep(i["L0_attn_a_bv"])
    s["relT"] = i["L0_attn_b_rel_table"][::-1].T
    w_in, b_in = i["L1_attn_b_w_in"], i["L1_attn_b_b_in"]
    heads = (
        [i[f"L0_attn_b_W{n}"] for n in "qkv"] + [i[f"L0_attn_b_b{n}"] for n in "qkv"] + [i["L0_attn_b_Wo"], i["L0_attn_b_bo"]],
        [i[f"L1_attn_a_W{n}"] for n in "qkv"] + [None] * 3 + [i["L1_attn_a_Wo"], i["L1_attn_a_bo"]],
        [w_in[E * n:E * n + E] for n in range(3)] + [b_in[E * n:E * n + E] for n in range(3)]
        + [i["L1_attn_b_w_out"], i["L1_attn_b_b_out"]],
    )
    for a, (wq, wk, wv, bq, bk, bv, wo, bo) in enumerate(heads):
        d = DHEAD[a]
        for n, m in (("q", wq), ("k", wk)):
            s[f"w{n}{a}"] = np.zeros((P, E), f)
            s[f"w{n}{a}"][0:m.shape[1], 0:d * H] = m.reshape(H, d, -1).transpose(2, 1, 0).reshape(-1, d * H)
        s[f"wv{a}"] = wv.T
        if bq is not None:
            for n, m in (("q", bq), ("k", bk)):
                s[f"b{n}{a}"] = m.reshape(H, d).T.reshape(-1, 1)
            s[f"bv{a}"] = rep(bv)
        s[f"wo{a}"], s[f"bo{a}"] = wo.T, rep(bo)
    s["wqn0"] = heads[0][0].T
    s["bqr0"] = np.tile(heads[0][3].reshape(H, 8).T, (16, 1))
    s["enc"] = i["L1_ffn_W_enc"].transpose(1, 0, 2).reshape(E, NA * AH)
    s["b_enc"] = i["L1_ffn_b_enc"].reshape(2, P).T
    dec = np.zeros((P, NA, E), f)
    for n in range(NA):
        dec[AH * (n % 4):AH * (n % 4) + AH, n] = i["L1_ffn_W_dec"][n]
    s["dec"], s["b_dec"] = dec.reshape(P, NA * E), i["L1_ffn_b_dec"].T
    pack = np.zeros((P, NA, PACK), f)
    pack[:, :, 0:AR] = i["L1_ffn_W_down"].transpose(1, 0, 2)
    pack[0:AR, :, AR:AR + E] = i["L1_ffn_W_up"].transpose(1, 0, 2)
    pack[AR, :, AR:AR + E] = i["L1_ffn_b_up"]
    pack[AR + 1, :, AR:AR + E] = i["L1_ffn_b_base"]
    pack[0:AR, :, PACK - 1] = i["L1_ffn_b_down"].T
    s["pack"] = pack.reshape(P, NA * PACK)
    s["w_base"] = i["L1_ffn_W_base"]
    packed = np.zeros((P, WCOLS + PREP_COLS), f)
    for name, cols in SECTIONS + PREP_SECTIONS:
        v = s[name]
        assert v.shape[1] == cols, (name, v.shape)
        packed[0:v.shape[0], OFF[name][0]:OFF[name][0] + cols] = v
    return packed


def kernel(**inputs):
    import numpy as np
    import concourse.bacc as bacc
    from concourse.bass_utils import run_bass_kernel_spmd

    i = {k: np.asarray(v) for k, v in inputs.items()}
    arrays = {
        "x_dram": np.ascontiguousarray(i["L0_attn_a_x"]),
        "packed_dram": layout(i),
        "cidx_dram": np.ascontiguousarray(np.broadcast_to(i["L1_ffn_connected_idx"], (P, NA))),
    }
    nc = bacc.Bacc("TRN2", target_bir_lowering=False, num_devices=1)
    args = [nc.dram_tensor(n, a.shape, mybir.dt.from_np(a.dtype), kind="ExternalInput").ap() for n, a in arrays.items()]
    args.append(nc.dram_tensor("out_dram", (B, T, E), F32, kind="ExternalOutput").ap())
    build(nc, *args)
    r = run_bass_kernel_spmd(nc, [arrays], core_ids=[0])
    return r.results[0]["out_dram"]
```
